# Optimizing a Trainium2 kernel written in Bass

```python
import numpy as np
import jax
import jax.numpy as jnp

def _softmax(x, axis=-1):
    return jax.nn.softmax(x, axis=axis)
def _gelu(x):
    return jax.nn.gelu(x, approximate=True)
def _silu(x):
    return jax.nn.silu(x)
def _sigmoid(x):
    return jax.nn.sigmoid(x)
def _layernorm(x, axis=-1, eps=1e-5):
    m = jnp.mean(x, axis=axis, keepdims=True)
    v = jnp.var(x, axis=axis, keepdims=True)
    return (x - m) / jnp.sqrt(v + eps)
def _scatter_add(tgt, idx, src, axis=0):
    return tgt.at[idx].add(src)
def _segment_sum(src, seg, n):
    return jax.ops.segment_sum(src, seg, n)

kernel_name = 'mk_conv_attn_hybrid_d2_conv_nhwc128_28afdb'

def setup_inputs(seed: int = 0):
    np.random.seed(seed)
    _w = jnp.asarray
    def _rec_inputs():
        import jax
        import jax.numpy as jnp
        _gk = jax.random.key(seed)
        x = -0.0005207 + 1.001 * jax.random.normal(jax.random.fold_in(_gk, 1), (4, 64, 64, 128), jnp.float32)
        return x
    x = _rec_inputs()
    def _L0_conv_setup():
        import jax, jax.numpy as jnp
        import numpy as np
        B, H, W = (4, 64, 64)
        D_MODEL, D_STATE, D_CONV, EXPAND = (128, 16, 3, 2)
        D_INNER = EXPAND * D_MODEL
        DT_RANK = D_MODEL // 16
        LN_EPS = 1e-05

        def _selective_scan(u, delta, A, Bm, Cm, Dp, delta_bias):
            delta = jax.nn.softplus(delta + delta_bias[None, :, None])
            u_t = jnp.moveaxis(u, 2, 0)
            d_t = jnp.moveaxis(delta, 2, 0)
            B_t = jnp.moveaxis(Bm, 2, 0)
            C_t = jnp.moveaxis(Cm, 2, 0)

            def step(h, inp):
                u_i, d_i, b_i, c_i = inp
                dA = jnp.exp(d_i[..., None] * A)
                h = h * dA + (d_i * u_i)[..., None] * b_i[:, None, :]
                y = jnp.einsum('gdn,gn->gd', h, c_i)
                return (h, y)
            h0 = jnp.zeros((u.shape[0], u.shape[1], A.shape[1]), u.dtype)
            _, ys = jax.lax.scan(step, h0, (u_t, d_t, B_t, C_t))
            return jnp.moveaxis(ys, 0, 2) + u * Dp[None, :, None]

        def _forward(x, w_in, conv_w, conv_b, w_xproj, w_dt, b_dt, A_log, D_param, ln_w, ln_b, w_out):
            b, h, w, _ = x.shape
            L = h * w
            xz = x @ w_in
            xc, z = jnp.split(xz, 2, axis=-1)
            pad = (D_CONV - 1) // 2
            xc = jax.lax.conv_general_dilated(xc, conv_w, window_strides=(1, 1), padding=[(pad, pad), (pad, pad)], feature_group_count=D_INNER, dimension_numbers=('NHWC', 'HWIO', 'NHWC')) + conv_b
            xa = jax.nn.silu(xc)
            x_flat = xa.reshape(b, L, D_INNER)
            x_dbl = x_flat @ w_xproj
            dts, Bp, Cp = jnp.split(x_dbl, [DT_RANK, DT_RANK + D_STATE], axis=-1)
            dts = dts @ w_dt
            x_t = jnp.transpose(xa, (0, 2, 1, 3)).reshape(b, L, D_INNER)
            xs = jnp.stack([x_flat, x_t, jnp.flip(x_flat, 1), jnp.flip(x_t, 1)], axis=1)
            xs = xs.reshape(b * 4, L, D_INNER).transpose(0, 2, 1)

            def rep4(t):
                return jnp.broadcast_to(t[:, None], (b, 4) + t.shape[1:]).reshape((b * 4,) + t.shape[1:]).transpose(0, 2, 1)
            dts4, Bp4, Cp4 = (rep4(dts), rep4(Bp), rep4(Cp))
            A = -jnp.exp(A_log.astype(jnp.float32))
            ys = _selective_scan(xs, dts4, A, Bp4, Cp4, D_param.astype(jnp.float32), b_dt.astype(jnp.float32))
            ys = ys.transpose(0, 2, 1).reshape(b, 4, L, D_INNER)
            y = ys[:, 0].reshape(b, h, w, D_INNER) + jnp.transpose(ys[:, 1].reshape(b, w, h, D_INNER), (0, 2, 1, 3)) + jnp.flip(ys[:, 2], 1).reshape(b, h, w, D_INNER) + jnp.transpose(jnp.flip(ys[:, 3], 1).reshape(b, w, h, D_INNER), (0, 2, 1, 3))
            mu = jnp.mean(y, axis=-1, keepdims=True)
            var = jnp.mean(jnp.square(y - mu), axis=-1, keepdims=True)
            y = (y - mu) * jax.lax.rsqrt(var + LN_EPS) * ln_w + ln_b
            y = y * jax.nn.silu(z)
            return y @ w_out
        key = jax.random.key(seed)
        ks = jax.random.split(key, 9)
        s = 0.02
        x = jax.random.normal(ks[0], (B, H, W, D_MODEL), dtype=jnp.float32)
        w_in = jax.random.normal(ks[1], (D_MODEL, 2 * D_INNER), dtype=jnp.float32) * s
        conv_w = jax.random.normal(ks[2], (D_CONV, D_CONV, 1, D_INNER), dtype=jnp.float32) * s
        conv_b = jax.random.normal(ks[3], (D_INNER,), dtype=jnp.float32) * s
        w_xproj = jax.random.normal(ks[4], (D_INNER, DT_RANK + 2 * D_STATE), dtype=jnp.float32) * s
        w_dt = jax.random.normal(ks[5], (DT_RANK, D_INNER), dtype=jnp.float32) * s
        b_dt = jax.random.normal(ks[6], (D_INNER,), dtype=jnp.float32) * s
        A_log = jnp.log(jnp.broadcast_to(jnp.arange(1, D_STATE + 1, dtype=jnp.float32), (D_INNER, D_STATE)))
        D_param = jnp.ones((D_INNER,), dtype=jnp.float32)
        ln_w = jnp.ones((D_INNER,), dtype=jnp.float32)
        ln_b = jnp.zeros((D_INNER,), dtype=jnp.float32)
        w_out = jax.random.normal(ks[7], (D_INNER, D_MODEL), dtype=jnp.float32) * s
        return {'x': x, 'w_in': w_in, 'conv_w': conv_w, 'conv_b': conv_b, 'w_xproj': w_xproj, 'w_dt': w_dt, 'b_dt': b_dt, 'A_log': A_log, 'D_param': D_param, 'ln_w': ln_w, 'ln_b': ln_b, 'w_out': w_out}
    _L0_conv_all = _L0_conv_setup()
    _L0_conv_in = {k: v for k, v in _L0_conv_all.items() if k in ('w_in', 'conv_w', 'conv_b', 'w_xproj', 'w_dt', 'b_dt', 'A_log', 'D_param', 'ln_w', 'ln_b', 'w_out', )}
    del _L0_conv_all

    def _L1_attn_setup():
        import jax, jax.numpy as jnp
        import numpy as np
        HEADS = 8
        DIM = 128
        key = jax.random.key(seed)
        k1, k2, k3 = jax.random.split(key, 3)
        b, t, d, h = (4, 4096, DIM, HEADS)
        x = jax.random.normal(k1, (b, t, d), dtype=jnp.float32)
        W_kv = jax.random.normal(k2, (h * d * 2, d), dtype=jnp.float32) * (1.0 / np.sqrt(d))
        q_proj = jax.random.normal(k3, (h, d), dtype=jnp.float32) * (1.0 / np.sqrt(d))
        return {'x': x, 'W_kv': W_kv, 'q_proj': q_proj}
    _L1_attn_all = _L1_attn_setup()
    _L1_attn_in = {k: v for k, v in _L1_attn_all.items() if k in ('W_kv', 'q_proj', )}
    del _L1_attn_all

    def _L1_ffn_setup():
        import jax, jax.numpy as jnp
        import numpy as np
        B, N, D, C, E, K = (8, 8192, 128, 128, 8, 2)
        key = jax.random.key(seed)
        k0, k1, k2 = jax.random.split(key, 3)
        x = jax.random.normal(k0, (B, N, D), dtype=jnp.float32)
        router_w = jax.random.normal(k1, (D, E), dtype=jnp.float32) * 0.05
        router_b = jnp.zeros((E,), dtype=jnp.float32)
        expert_w = jax.random.normal(k2, (E, D, C), dtype=jnp.float32) * (1.0 / np.sqrt(D))
        expert_b = jnp.zeros((E, C), dtype=jnp.float32)
        return {'x': x, 'router_w': router_w, 'router_b': router_b, 'expert_w': expert_w, 'expert_b': expert_b}
    _L1_ffn_all = _L1_ffn_setup()
    _L1_ffn_in = {k: v for k, v in _L1_ffn_all.items() if k in ('router_w', 'router_b', 'expert_w', 'expert_b', )}
    del _L1_ffn_all

    return {
        "x": x,
        "L0_conv_w_in": _L0_conv_in["w_in"],
        "L0_conv_conv_w": _L0_conv_in["conv_w"],
        "L0_conv_conv_b": _L0_conv_in["conv_b"],
        "L0_conv_w_xproj": _L0_conv_in["w_xproj"],
        "L0_conv_w_dt": _L0_conv_in["w_dt"],
        "L0_conv_b_dt": _L0_conv_in["b_dt"],
        "L0_conv_A_log": _L0_conv_in["A_log"],
        "L0_conv_D_param": _L0_conv_in["D_param"],
        "L0_conv_ln_w": _L0_conv_in["ln_w"],
        "L0_conv_ln_b": _L0_conv_in["ln_b"],
        "L0_conv_w_out": _L0_conv_in["w_out"],
        "L1_attn_W_kv": _L1_attn_in["W_kv"],
        "L1_attn_q_proj": _L1_attn_in["q_proj"],
        "L1_ffn_router_w": _L1_ffn_in["router_w"],
        "L1_ffn_router_b": _L1_ffn_in["router_b"],
        "L1_ffn_expert_w": _L1_ffn_in["expert_w"],
        "L1_ffn_expert_b": _L1_ffn_in["expert_b"],
    }

def reference(x, L0_conv_w_in, L0_conv_conv_w, L0_conv_conv_b, L0_conv_w_xproj, L0_conv_w_dt, L0_conv_b_dt, L0_conv_A_log, L0_conv_D_param, L0_conv_ln_w, L0_conv_ln_b, L0_conv_w_out, L1_attn_W_kv, L1_attn_q_proj, L1_ffn_router_w, L1_ffn_router_b, L1_ffn_expert_w, L1_ffn_expert_b):
    import jax
    import jax.numpy as jnp
    def _L0_conv_ref(x, w_in, conv_w, conv_b, w_xproj, w_dt, b_dt, A_log, D_param, ln_w, ln_b, w_out):
        import jax, jax.numpy as jnp
        import numpy as np
        B, H, W = (4, 64, 64)
        D_MODEL, D_STATE, D_CONV, EXPAND = (128, 16, 3, 2)
        D_INNER = EXPAND * D_MODEL
        DT_RANK = D_MODEL // 16
        LN_EPS = 1e-05

        def _selective_scan(u, delta, A, Bm, Cm, Dp, delta_bias):
            delta = jax.nn.softplus(delta + delta_bias[None, :, None])
            u_t = jnp.moveaxis(u, 2, 0)
            d_t = jnp.moveaxis(delta, 2, 0)
            B_t = jnp.moveaxis(Bm, 2, 0)
            C_t = jnp.moveaxis(Cm, 2, 0)

            def step(h, inp):
                u_i, d_i, b_i, c_i = inp
                dA = jnp.exp(d_i[..., None] * A)
                h = h * dA + (d_i * u_i)[..., None] * b_i[:, None, :]
                y = jnp.einsum('gdn,gn->gd', h, c_i)
                return (h, y)
            h0 = jnp.zeros((u.shape[0], u.shape[1], A.shape[1]), u.dtype)
            _, ys = jax.lax.scan(step, h0, (u_t, d_t, B_t, C_t))
            return jnp.moveaxis(ys, 0, 2) + u * Dp[None, :, None]

        def _forward(x, w_in, conv_w, conv_b, w_xproj, w_dt, b_dt, A_log, D_param, ln_w, ln_b, w_out):
            b, h, w, _ = x.shape
            L = h * w
            xz = x @ w_in
            xc, z = jnp.split(xz, 2, axis=-1)
            pad = (D_CONV - 1) // 2
            xc = jax.lax.conv_general_dilated(xc, conv_w, window_strides=(1, 1), padding=[(pad, pad), (pad, pad)], feature_group_count=D_INNER, dimension_numbers=('NHWC', 'HWIO', 'NHWC')) + conv_b
            xa = jax.nn.silu(xc)
            x_flat = xa.reshape(b, L, D_INNER)
            x_dbl = x_flat @ w_xproj
            dts, Bp, Cp = jnp.split(x_dbl, [DT_RANK, DT_RANK + D_STATE], axis=-1)
            dts = dts @ w_dt
            x_t = jnp.transpose(xa, (0, 2, 1, 3)).reshape(b, L, D_INNER)
            xs = jnp.stack([x_flat, x_t, jnp.flip(x_flat, 1), jnp.flip(x_t, 1)], axis=1)
            xs = xs.reshape(b * 4, L, D_INNER).transpose(0, 2, 1)

            def rep4(t):
                return jnp.broadcast_to(t[:, None], (b, 4) + t.shape[1:]).reshape((b * 4,) + t.shape[1:]).transpose(0, 2, 1)
            dts4, Bp4, Cp4 = (rep4(dts), rep4(Bp), rep4(Cp))
            A = -jnp.exp(A_log.astype(jnp.float32))
            ys = _selective_scan(xs, dts4, A, Bp4, Cp4, D_param.astype(jnp.float32), b_dt.astype(jnp.float32))
            ys = ys.transpose(0, 2, 1).reshape(b, 4, L, D_INNER)
            y = ys[:, 0].reshape(b, h, w, D_INNER) + jnp.transpose(ys[:, 1].reshape(b, w, h, D_INNER), (0, 2, 1, 3)) + jnp.flip(ys[:, 2], 1).reshape(b, h, w, D_INNER) + jnp.transpose(jnp.flip(ys[:, 3], 1).reshape(b, w, h, D_INNER), (0, 2, 1, 3))
            mu = jnp.mean(y, axis=-1, keepdims=True)
            var = jnp.mean(jnp.square(y - mu), axis=-1, keepdims=True)
            y = (y - mu) * jax.lax.rsqrt(var + LN_EPS) * ln_w + ln_b
            y = y * jax.nn.silu(z)
            return y @ w_out
        return _forward(x, w_in, conv_w, conv_b, w_xproj, w_dt, b_dt, A_log, D_param, ln_w, ln_b, w_out)

    def _L1_attn_ref(x, W_kv, q_proj):
        import jax, jax.numpy as jnp
        import numpy as np
        HEADS = 8
        DIM = 128
        b, t, d = x.shape
        h = q_proj.shape[0]
        kv = jnp.einsum('btd,ed->bte', x, W_kv).reshape(b, t, h, d, 2)
        kv = jax.nn.silu(kv)
        k, v = (kv[..., 0], kv[..., 1])
        s = jnp.einsum('hd,bthd->bth', q_proj, k)
        m_A = jax.lax.cummax(s, axis=1)
        exp_scores = jnp.exp(s - m_A)
        u_A = jnp.cumsum(exp_scores, axis=1)
        w_A = jnp.cumsum(exp_scores[..., None] * v, axis=1)
        output = w_A / u_A[..., None]
        return output.mean(axis=2)

    def _L1_ffn_ref(x, router_w, router_b, expert_w, expert_b):
        import jax, jax.numpy as jnp
        import numpy as np
        B, N, D, C, E, K = (8, 8192, 128, 128, 8, 2)
        router_probs = jax.nn.softmax(x @ router_w + router_b, axis=-1)
        top_p, top_i = jax.lax.top_k(router_probs, K)
        top_p = top_p / jnp.sum(top_p, axis=-1, keepdims=True)
        expert_out = jnp.einsum('bnd,edc->bnec', x, expert_w) + expert_b
        gathered = jnp.take_along_axis(expert_out, top_i[..., None], axis=2)
        return jnp.einsum('bnk,bnkc->bnc', top_p, gathered)

    def _gn(v, G=32, eps=1e-5):
        B_, H_, W_, C_ = v.shape
        g = v.reshape(B_, H_, W_, G, C_ // G)
        m = jnp.mean(g, axis=(1, 2, 4), keepdims=True)
        s = jnp.var(g, axis=(1, 2, 4), keepdims=True)
        return ((g - m) / jnp.sqrt(s + eps)).reshape(v.shape)

    def _ln_c(v, eps=1e-6):
        m = jnp.mean(v, axis=-1, keepdims=True)
        s = jnp.var(v, axis=-1, keepdims=True)
        return (v - m) / jnp.sqrt(s + eps)

    def _ln_t(v, eps=1e-5):
        m = jnp.mean(v, axis=-1, keepdims=True)
        s = jnp.var(v, axis=-1, keepdims=True)
        return (v - m) / jnp.sqrt(s + eps)

    def _to_tokens(v):
        B_, H_, W_, C_ = v.shape
        return v.reshape(B_, H_ * W_, C_)
    def _from_tokens(t, like):
        return t.reshape(like.shape)

    x = x + _L0_conv_ref(_gn(x), L0_conv_w_in, L0_conv_conv_w, L0_conv_conv_b, L0_conv_w_xproj, L0_conv_w_dt, L0_conv_b_dt, L0_conv_A_log, L0_conv_D_param, L0_conv_ln_w, L0_conv_ln_b, L0_conv_w_out)
    t = _to_tokens(x)
    t = t + _L1_attn_ref(_ln_t(t), L1_attn_W_kv, L1_attn_q_proj)
    t = t + _L1_ffn_ref(_ln_t(t), L1_ffn_router_w, L1_ffn_router_b, L1_ffn_expert_w, L1_ffn_expert_b)
    x = _from_tokens(t, x)
    return x


_drawn_inputs = setup_inputs


def setup_inputs(seed=0):
    import zlib

    import numpy as np

    out = dict(_drawn_inputs(seed))
    spreads = {'L0_conv_D_param': (1.0, 0.2),
     'L0_conv_ln_w': (1.0, 0.2),
     'L0_conv_ln_b': (0.0, 0.1),
     'L1_ffn_router_b': (0.0, 0.1),
     'L1_ffn_expert_b': (0.0, 0.1)}
    factors = {'L0_conv_w_xproj': 64.0, 'L0_conv_w_dt': 64.0, 'L0_conv_b_dt': 64.0, 'L0_conv_A_log': 64.0}
    for name, (base, spread) in spreads.items():
        noise = np.random.default_rng([zlib.crc32(name.encode()), seed]).standard_normal(out[name].shape)
        drawn = base * np.exp(spread * noise) if base else spread * noise
        out[name] = jnp.asarray(drawn.astype(out[name].dtype))
    for name, factor in factors.items():
        out[name] = (out[name] * factor).astype(out[name].dtype)
    return out
```

```python
from contextlib import ExitStack

import concourse.bass as bass
from concourse import mybir

F32=mybir.dt.float32; BF16=mybir.dt.bfloat16
ACT=mybir.ActivationFunctionType; ALU=mybir.AluOpType

N_STATE=16; BATCH=4; HALVES=2; DIRS=4; DH=128
GROUPS=BATCH*HALVES
TERMS=((0,0),(0,1),(0,2),(1,0),(1,1),(2,0))
TROWS=len(TERMS)*GROUPS
BLK=16; RING=4; STEPS=BLK*RING
DECAY_SCALE=2.0**30; DECAY_FLOOR=-200.0
FLOOR_STEPS=(1,3,5,7)

def selective_scan(nc, L, delta_d, input_d, bterm_d, cmat_d, alog, y_d):
    BODIES=L//STEPS
    HC=DIRS*DH//2
    with ExitStack() as ctx:
        def sb(name,shape,dt=F32): return ctx.enter_context(nc.sbuf_tensor("ss_"+name,shape,dt))
        def ps(name): return ctx.enter_context(nc.psum_tensor("ss_"+name,[128,512],F32))
        def sem(name): return ctx.enter_context(nc.semaphore("ss_"+name))
        decay=sb("decay",[128,RING,BLK*DH])
        drive=sb("drive",[TROWS,RING,BLK*DIRS*DH],BF16)
        bstream=sb("bstream",[TROWS,N_STATE,STEPS],BF16)
        bdiag=sb("bdiag",[TROWS,RING,BLK,N_STATE,GROUPS],BF16)
        call=sb("call",[128,L])
        DIAG=BLK*GROUPS+GROUPS
        cdiag=sb("cdiag",[128,2,BLK*DIAG])
        hcopy=sb("hcopy",[128,2,4,HC])
        neg_a=sb("neg_a",[128,DH])
        alog_s=sb("alog_s",[128,DH])
        ysb=sb("ysb",[128,2,512])
        bmask=sb("bmask",[TROWS,GROUPS],BF16)
        bm_i=sb("bm_i",[128,GROUPS]); cmask=sb("cmask",[128,GROUPS])
        zero_w=sb("zero_w",[128,128],BF16); zero_x=sb("zero_x",[128,HC],BF16)
        state=[[ps(f"state{c}{i}") for i in range(2)] for c in range(2)]
        ybank=[ps(f"y{i}") for i in range(2)]
        delta_in=[sem(f"delta_in{q}") for q in range(RING)]
        drive_in=[sem(f"drive_in{q}") for q in range(RING)]
        b_in=sem("b_in"); c_in=sem("c_in"); a_in=sem("a_in")
        scaled=sem("scaled"); floored=sem("floored"); decay_ready=sem("decay_ready")
        bd_ready=sem("bd_ready"); cd_ready=sem("cd_ready");
        masks=sem("masks"); a_exp=sem("a_exp"); a_clip=sem("a_clip")
        zeroed=sem("zeroed")
        added=[sem(f"added{c}") for c in range(2)]
        decayed=[sem(f"decayed{c}") for c in range(2)]
        copied=[sem(f"copied{c}") for c in range(2)]
        summed=[sem(f"summed{c}") for c in range(2)]
        y_ready=sem("y_ready"); y_out=[sem(f"y_out{i}") for i in range(2)]
        block=ctx.enter_context(nc.Block())

        def at(i, first, per, c):
            if first:
                return c if c>0 else None
            return i*per + c
        def wait(eng, s, v):
            if v is not None: eng.wait_ge(s, v)

        @block.sync
        def _(sp):
            sp.dma_start(alog_s[:,:],alog).then_inc(a_in,16)
            sp.dma_start(call[:,:],cmat_d).then_inc(c_in,16)
            def body(i, first):
                wait(sp, bd_ready, at(i,first,RING,0))
                sp.dma_start(bstream[:,:,:], bterm_d[:,:,bass.ds(i*STEPS,STEPS)]).then_inc(b_in,16)
                for q in range(RING):
                    wait(sp, decayed[1], at(i,first,STEPS,(q-RING+1)*BLK))
                    sp.dma_start(decay[:,q,:], delta_d[:, :, bass.ds((i*STEPS+q*BLK)*DH,BLK*DH)]).then_inc(delta_in[q],16)
                    if not first: sp.wait_ge(added[1], i*STEPS+(q-RING+1)*BLK+2)
                    row=0
                    for parts in (3,2,1):
                        n=parts*GROUPS
                        sp.dma_start(drive[row:row+n,q,:], input_d[0:n, bass.ds((i*STEPS+q*BLK)*DIRS*DH,BLK*DIRS*DH)]).then_inc(drive_in[q],16)
                        row+=n
                    if not first: store_y(i,q-4)
            def store_y(i,q):
                n=q%2
                sp.wait_ge(y_ready, i*RING+q+1)
                sp.dma_start(y_d(i*STEPS+q*BLK), ysb[:,n,:]).then_inc(y_out[n],16)
            body(0,True)
            with sp.Fori(1,BODIES) as i: body(i,False)
            for q in range(RING-4,RING): store_y(BODIES-1,q)
            for n in range(2): sp.wait_ge(y_out[n], BODIES*RING//2*16)

        @block.gpsimd
        def _(pool):
            pool.memset(bm_i[:,:],0.0).then_inc(masks,1)
            pool.memset(zero_w[:,:],0.0).then_inc(zeroed,1)
            pool.memset(zero_x[:,:],0.0).then_inc(zeroed,1)
            pool.memset(cdiag[:,:,:],0.0).then_inc(zeroed,1)
            pool.wait_ge(masks,1)
            for m in range(128//GROUPS):
                pool.affine_select(out=bm_i[:,:],in_=bm_i[:,:],compare_op=ALU.not_equal,fill=1.0,base=-GROUPS*m,pattern=[[-1,GROUPS]],channel_multiplier=1).then_inc(masks,1)
                pool.wait_ge(masks,2+m)
            pool.tensor_copy(cmask[:,:],bm_i[:,:]).then_inc(masks,1)
            pool.tensor_copy(bmask[:,:],bm_i[0:TROWS,:]).then_inc(masks,1)
            pool.wait_ge(masks,3+128//GROUPS)
            pool.wait_ge(a_exp,1)
            pool.tensor_scalar(neg_a[:,:],neg_a[:,:],-1.0/DECAY_SCALE,None,ALU.mult).then_inc(a_clip,1)
            pool.wait_ge(a_clip,2)
            pool.wait_ge(zeroed,3)
            pool.wait_ge(c_in,16)
            def body(i, first):
                for q in range(RING):
                    pool.wait_ge(delta_in[q], i*16+16)
                    d=decay[:,q,:].rearrange("p (t d) -> p t d",d=DH)
                    pool.tensor_tensor(d,d,neg_a[:,:].unsqueeze(1).broadcast_to((128,BLK,DH)),ALU.mult).then_inc(scaled,1)
                    if q==0: pool.wait_ge(b_in, i*16+16)
                    if not first: pool.wait_ge(added[1], i*STEPS+(q-RING+1)*BLK+2)
                    src=bstream[:,:,q*BLK:(q+1)*BLK].rearrange("p n t -> p t n").unsqueeze(3).broadcast_to((TROWS,BLK,N_STATE,GROUPS))
                    m=bmask[:,:].unsqueeze(1).unsqueeze(1).broadcast_to((TROWS,BLK,N_STATE,GROUPS))
                    pool.tensor_tensor(bdiag[:,q],src,m,ALU.mult).then_inc(bd_ready,1)
                    wait(pool, summed[1], at(i,first,STEPS,(q-1)*BLK))
                    cd=cdiag[:,q%2,:].rearrange("p (t x) -> p t x",t=BLK)[:,:,0:GROUPS]
                    pool.tensor_tensor(cd, call[:,bass.ds(i*STEPS+q*BLK,BLK)].unsqueeze(2).broadcast_to((128,BLK,GROUPS)), cmask[:,:].unsqueeze(1).broadcast_to((128,BLK,GROUPS)),ALU.mult).then_inc(cd_ready,1)
            body(0,True)
            with pool.Fori(1,BODIES) as i: body(i,False)

        @block.scalar
        def _(act):
            act.wait_ge(a_clip,1)
            act.activation(neg_a[:,:],alog_s[:,:],ACT.Exp).then_inc(a_exp,1)
            def exp_block(i,q):
                act.wait_ge(floored,(i*RING+q+1)*len(FLOOR_STEPS))
                act.activation(decay[:,q,:],decay[:,q,:],ACT.Exp).then_inc(decay_ready,1)
            def copy(i,first,s,c):
                act.wait_ge(decayed[c], i*STEPS+s+1)
                wait(act, summed[c], at(i,first,STEPS,s-4))
                act.activation(hcopy[:,c,(s-1)%4,:],state[c][(s-1)%2][:,0:HC],ACT.Copy).then_inc(copied[c],1)
            def evac_y(i,first,q):
                wait(act, summed[1], at(i,first,STEPS,q*BLK))
                n=(q+1)%2
                k=(i*RING+q-1)
                if not (first and q<=2):
                    act.wait_ge(y_out[n], (i*2+(q-1)//2)*16)
                act.activation(ysb[:,n,:],ybank[n][:,:],ACT.Copy).then_inc(y_ready,1)
            def body(i,first):
                for s in range(STEPS):
                    q=s//BLK
                    if s%BLK==5 and not (first and q==0):
                        evac_y(i,first,q)
                    if s%BLK==9 and (q<RING-1):
                        exp_block(i,q+1)
                    if s%BLK==9 and q==RING-1 and first is not None:
                        exp_next(i)
                    for c in range(2):
                        if first and s==0: continue
                        copy(i,first,s,c)
            def exp_next(i):
                act.wait_ge(floored,((i+1)*RING+1)*len(FLOOR_STEPS))
                act.activation(decay[:,0,:],decay[:,0,:],ACT.Exp).then_inc(decay_ready,1)
            exp_block(0,0)
            body(0,True)
            with act.Fori(1,BODIES-1) as i: body(i,False)
            body(BODIES-1,None)
            for c in range(2):
                act.wait_ge(added[c],L+2)
                act.wait_ge(summed[c],L-4)
                act.activation(hcopy[:,c,(L-1)%4,:],state[c][(L-1)%2][:,0:HC],ACT.Copy).then_inc(copied[c],1)
            evac_y(BODIES-1,None,RING)

        @block.vector
        def _(dve):
            dve.wait_ge(a_in,16)
            dve.tensor_scalar(alog_s[:,:],alog_s[:,:],88.7,None,ALU.min).then_inc(a_clip,1)
            def floor(i,q,part):
                n=BLK*DH//len(FLOOR_STEPS)
                d=decay[:,q%RING,part*n:(part+1)*n]
                dve.wait_ge(scaled, i*RING+q+1)
                dve.tensor_scalar(d,d,DECAY_FLOOR/DECAY_SCALE,DECAY_SCALE,ALU.max,ALU.mult).then_inc(floored,1)
            def body(i,first):
                for s in range(STEPS):
                    q=s//BLK
                    for c in range(2):
                        if s%BLK==0 and c==0: dve.wait_ge(decay_ready, i*RING+q+1)
                        dve.wait_ge(added[c], i*STEPS+s+2)
                        wait(dve, copied[c], at(i,first,STEPS,s-1))
                        a=decay[:,q,(s%BLK)*DH:(s%BLK+1)*DH].unsqueeze(1).broadcast_to((128,2,DH))
                        op=dve.tensor_tensor(state[c][s%2][:,0:HC].rearrange("p (k d) -> p k d",k=2),a,state[c][(s-1)%2][:,0:HC].rearrange("p (k d) -> p k d",k=2),ALU.mult)
                        op.then_inc(decayed[c],1)
                    if s%BLK in FLOOR_STEPS and not (first is None and q==RING-1):
                        floor(i,q+1,FLOOR_STEPS.index(s%BLK))
            for part in range(len(FLOOR_STEPS)): floor(0,0,part)
            body(0,True)
            with dve.Fori(1,BODIES-1) as i: body(i,False)
            body(BODIES-1,None)

        @block.tensor
        def _(pe):
            pe.wait_ge(zeroed,3)
            for c in range(2):
                for j in range(2):
                    pe.matmul(state[c][j][:,0:HC],zero_w[:,:],zero_x[:,:],start=True,stop=True,skip_group_check=True).then_inc(added[c],1)
            def sum_states(i,first,s,c):
                b=s//BLK; t=s%BLK
                wait(pe, copied[c], at(i,first,STEPS,s+1))
                if t==0 and c==0:
                    wait(pe, cd_ready, at(i,first,RING,b+1))
                    wait(pe, y_ready, at(i,first,RING,b-1))
                pe.matmul(ybank[b%2][:,c*HC:(c+1)*HC],cdiag[:,b%2,t*128:(t+1)*128],hcopy[:,c,s%4,:],start=(t==0 and c==0),stop=(t==BLK-1),skip_group_check=True).then_inc(summed[c],1)
            def body(i,first):
                for s in range(STEPS):
                    q=s//BLK; t=s%BLK
                    if t==0:
                        pe.wait_ge(drive_in[q], i*48+48)
                        pe.wait_ge(bd_ready, i*RING+q+1)
                    for c in range(2):
                        pe.wait_ge(decayed[c], i*STEPS+s+1)
                        mm=pe.matmul(state[c][s%2][:,0:HC],bdiag[:,q,t].rearrange("p n g -> p (n g)"),drive[:,q,t*DIRS*DH+c*HC:t*DIRS*DH+(c+1)*HC],start=False,stop=True,skip_group_check=True)
                        mm.then_inc(added[c],1)
                        if not(first and s<2):
                            sum_states(i,first,s-2,c)
            body(0,True)
            with pe.Fori(1,BODIES) as i: body(i,False)
            for s in (STEPS-2,STEPS-1):
                for c in range(2):
                    sum_states(BODIES-1,None,s,c)
        return None

IMG=64; TOK=IMG*IMG; CH=128; INNER=256; RANK=8; TAPS=9
TILE=128; TILES=TOK//TILE; PART_TILES=4; PARTS=TILES//PART_TILES
CHUNK=512; CHUNKS=TOK//CHUNK
PADW=IMG+2
DT_ROW,B_ROW,C_ROW,XD_ROWS=0,32,64,80
EPS=1e-5
AX=mybir.AxisListType

class Count:
    def __init__(self, sem, per, step=1):
        self.sem, self.per, self.step, self.n = sem, per, step, 0
    def credit(self, eng):
        eng.sem_inc(self.sem, self.per*self.step)
    def at(self, image, n):
        return (image+1)*(self.per*self.step) + n*self.step
    def inc(self, ins):
        ins.then_inc(self.sem, self.step)
        self.n += 1
        return self.n
    def link(self, eng, image, ins):
        eng.wait_ge(self.sem, self.at(image, self.inc(ins)))
    def done(self):
        assert self.n % self.per == 0, (self.n, self.per)

def project_and_convolve(nc, d):
    with ExitStack() as ctx:
        def sb(name,shape,dt=F32): return ctx.enter_context(nc.sbuf_tensor("pc_"+name,shape,dt))
        def ps(name,n=512): return ctx.enter_context(nc.psum_tensor("pc_"+name,[128,n],F32))
        def sem(name): return ctx.enter_context(nc.semaphore("pc_"+name))
        def count(name,per,step=1): return Count(sem(name),per,step)
        w_in=sb("w_in",[CH,2*INNER]); w_x=sb("w_x",[128,2,XD_ROWS]); w_dt=sb("w_dt",[RANK,INNER]); b_dt=sb("b_dt",[128,INNER])
        conv_w=sb("conv_w",[128,2,TAPS]); conv_b=sb("conv_b",[128,2]); tapdiag=sb("tapdiag",[128,TAPS,128])
        d4=sb("d4",[128,INNER]); ident=sb("ident",[128,128]); group=sb("group",[128,128])
        xn=sb("xn",[CH,TOK]); padded=sb("padded",[128,2,PADW*PADW])
        xa=sb("xa",[128,2,TOK]); xr=sb("xr",[128,2,TOK]); xd=sb("xd",[XD_ROWS,TOK])
        SPLIT=512; SPLITS=TOK//SPLIT
        bres=sb("bres",[48,SPLIT]); ones=sb("ones",[48,1]); bpart=sb("bpart",[48,3,SPLIT],BF16)
        stats=sb("stats",[128,CHUNKS,6]); mv=sb("mv",[128,2]); gmv=sb("gmv",[128,2]); dev=sb("dev",[128,1]); var=sb("var",[128,1]); std=sb("std",[128,1]); rstd=sb("rstd",[128,1])
        delta=sb("delta",[128,2,PART_TILES,INNER]); ex=sb("ex",[128,PART_TILES*INNER]); ln=sb("ln",[128,PART_TILES*INNER])
        R=3
        du=sb("du",[128,R,1024]); dp=sb("dp",[128,R,3,1024],BF16)
        gate=sb("gate",[128,2,2,INNER]); skip=sb("skip",[128,2,2,INNER])
        mm=[ps(f"mm{i}") for i in range(2)]; dl=[ps(f"dl{i}") for i in range(2)]; up=[ps(f"up{i}",1024) for i in range(2)]
        IN=(0,CHUNKS); GT=2*CHUNKS; CV=GT+TILES//2; XD=CV+CHUNKS; MM=XD+CHUNKS
        DL=2+TILES//2
        w_ld=sem("w_ld"); setup=sem("setup"); borders=sem("borders"); apart=sem("apart")
        x_in=count("x_in",1,16)
        mm_full=count("mm_full",MM); mm_taken=count("mm_taken",MM)
        dl_full=count("dl_full",DL); dl_taken=count("dl_taken",DL)
        u_full=count("u_full",TILES); u_taken=count("u_taken",TILES)
        norm=count("norm",CHUNKS+5+CHUNKS); std_ready=count("std_ready",1)
        conv=count("conv",2*TAPS); xa0=count("xa0",2); turned=count("turned",2)
        b_split=count("b_split",5*SPLITS); b_out=count("b_out",SPLITS*12,16); c_out=count("c_out",2,16)
        v_steps=count("v_steps",PARTS*5); e_ready=count("e_ready",PARTS); l_ready=count("l_ready",PARTS)
        delta_out=[count(f"delta_out{n}",PARTS,16) for n in range(2)]
        hi=count("hi",TILES); res=count("res",TILES); mid=count("mid",TILES); dp_ready=count("dp_ready",TILES)
        slot_n=[len(range(n,TILES,R)) for n in range(R)]
        dp_out=[count(f"dp_out{n}",slot_n[n],16) for n in range(R)]
        gate_ready=count("gate_ready",TILES//2); gate_out=[count(f"gate_out{n}",TILES//4,16) for n in range(2)]
        skip_ready=count("skip_ready",TILES); skip_out=[count(f"skip_out{n}",TILES//4,16) for n in range(2)]
        block=ctx.enter_context(nc.Block())

        def wait(eng,c,image,n): eng.wait_ge(c.sem,c.at(image,n))
        loads=((w_in[:,:],"w_in"),(w_x[:,:,:],"w_x"),(w_dt[:,:],"w_dt"),(b_dt[:,:],"b_dt"),(conv_w[:,:,:],"conv_w"),(conv_b[:,:],"conv_b"),(d4[:,:],"d_param"),(ident[:,:],"ident"),(group[:,:],"group"))

        def interior(h,k): return padded[:,h,:].rearrange("p (r c) -> p r c",c=PADW)[:,1+8*k:9+8*k,1:1+IMG]
        def shifted(h,row,rows,tap):
            return padded[:,h,:].rearrange("p (r c) -> p r c",c=PADW)[:,row+tap//3:row+tap//3+rows,tap%3:tap%3+IMG]

        @block.sync
        def _(sp):
            for dst,name in loads: sp.dma_start(dst,d[name]).then_inc(w_ld,16)
            for c in (x_in,b_out,c_out,*delta_out,*dp_out,*skip_out): c.credit(sp)
            bterm=d["bterm"].rearrange("(t h b) n l -> t h b n l",h=2,b=BATCH)
            cmat=d["cmat"].rearrange("(n h b) l -> h b n l",h=2,b=BATCH)
            delta_d=d["delta"].rearrange("(h b) x -> h b x",h=2)
            drive_d=d["drive"].rearrange("(g b) x -> g b x",b=BATCH)
            with sp.Fori(0,BATCH) as b:
                wait(sp,mm_full,b-1,CV)
                x_in.inc(sp.dma_start(xn[:,:], d["x_t"][b]))
                for c in range(SPLITS):
                    wait(sp,b_split,b,5*c+5)
                    for t,(i,_) in enumerate(TERMS):
                        for h in range(2):
                            b_out.inc(sp.dma_start(bterm[t,h,b,:,c*SPLIT:(c+1)*SPLIT], bpart[B_ROW:B_ROW+16,i,:]))
                wait(sp,mm_taken,b,MM)
                for h in range(2):
                    c_out.inc(sp.dma_start(cmat[h,b], xd[C_ROW:C_ROW+16,:]))
                def store_tiles(q):
                    for j in range(q*PART_TILES,(q+1)*PART_TILES):
                        wait(sp,dp_ready,b,j+1)
                        dp_out[j%R].inc(sp.dma_start(drive_d[:,b,j*TILE*512:(j+1)*TILE*512].rearrange("g (t f) -> t g f",t=TILE), dp[:,j%R,:,:].rearrange("p a (h f) -> p (a h) f",h=2)))
                        if j%2==1:
                            n=(j//2)%2
                            wait(sp,skip_ready,b,j+1)
                            skip_out[n].inc(sp.dma_start(d["skip"][b,(j-1)*TILE:(j+1)*TILE].rearrange("(j t) f -> t j f",t=TILE), skip[:,n,:,:]))
                for q in range(PARTS+1):
                    if q<PARTS:
                        wait(sp,v_steps,b,5*q+5)
                        for h in range(2):
                            delta_out[q%2].inc(sp.dma_start(delta_d[h,b,q*PART_TILES*TILE*DH:(q+1)*PART_TILES*TILE*DH].rearrange("(j t e) -> t j e",t=TILE,e=DH), delta[:,q%2,:,h*DH:(h+1)*DH]))
                    if q: store_tiles(q-1)
            for c in (b_out,c_out,*delta_out,*dp_out,*skip_out,*gate_out): wait(sp,c,BATCH-1,c.per)

        @block.gpsimd
        def _(pool):
            pool.memset(padded[:,:,:],0.0).then_inc(borders,1)
            pool.memset(ones[:,:],1.0).then_inc(borders,1)
            one=ones[B_ROW:B_ROW+16,:].broadcast_to((16,SPLIT))
            pool.wait_ge(borders,2)
            for c in (b_split,res): c.credit(pool)
            with pool.Fori(0,BATCH) as b:
                for c in range(SPLITS):
                    wait(pool,mm_taken,b,XD+c+1)
                    wait(pool,b_out,b,12*c)
                    src=xd[B_ROW:B_ROW+16,c*SPLIT:(c+1)*SPLIT]; r=bres[B_ROW:B_ROW+16,:]
                    p=[bpart[B_ROW:B_ROW+16,i,:] for i in range(3)]
                    b_split.link(pool,b,pool.tensor_tensor(p[0],src,one,ALU.mult))
                    b_split.link(pool,b,pool.tensor_tensor(r,src,p[0],ALU.subtract))
                    b_split.link(pool,b,pool.tensor_tensor(p[1],r,one,ALU.mult))
                    b_split.link(pool,b,pool.tensor_tensor(r,r,p[1],ALU.subtract))
                    b_split.link(pool,b,pool.tensor_tensor(p[2],r,one,ALU.mult))
                for j in range(TILES):
                    wait(pool,hi,b,j+1)
                    res.inc(pool.tensor_tensor(du[:,j%R,:],du[:,j%R,:],dp[:,j%R,0,:],ALU.subtract))

        @block.scalar
        def _(act):
            for c in (mm_taken,std_ready,xa0,turned,e_ready,l_ready,hi,mid,gate_ready,*gate_out): c.credit(act)
            act.wait_ge(w_ld,16*len(loads)); act.wait_ge(borders,2)
            with act.Fori(0,BATCH) as b:
                wait(act,norm,b,CHUNKS+4)
                std_ready.inc(act.activation(std[:,:],var[:,:],ACT.Sqrt))
                for h in range(2):
                    if h==0: wait(act,conv,b-1,2*TAPS)
                    for k in range(CHUNKS):
                        wait(act,mm_full,b,IN[h]+k+1)
                        mm_taken.inc(act.activation(interior(h,k),mm[(IN[h]+k)%2][:,:].rearrange("p (r c) -> p r c",c=IMG),ACT.Copy))
                for k in range(TILES//2):
                    wait(act,mm_full,b,GT+k+1)
                    wait(act,gate_out[k%2],b,k//2)
                    mm_taken.inc(act.activation(gate[:,k%2,:,:],mm[(GT+k)%2][:,:].rearrange("p (j f) -> p j f",j=2),ACT.Silu))
                    wait(act,mm_taken,b,GT+k+1)
                    gate_out[k%2].inc(act.dma_start(d["gate"][b,2*k*TILE:(2*k+2)*TILE].rearrange("(j t) f -> t j f",t=TILE), gate[:,k%2,:,:]))
                wait(act,u_full,b-1,TILES)
                for k in range(CHUNKS):
                    wait(act,mm_full,b,CV+k+1)
                    mm_taken.inc(act.activation(xa[:,1,k*CHUNK:(k+1)*CHUNK],mm[(CV+k)%2][:,:],ACT.Silu,bias=conv_b[:,1:2]))
                for k in range(2):
                    wait(act,conv,b,2*TAPS-1+k)
                    s=slice(k*(TOK//2),(k+1)*(TOK//2))
                    xa0.inc(act.activation(xa[:,0,s],xa[:,0,s],ACT.Silu))
                for h in range(2):
                    if h==0: wait(act,xa0,b,2)
                    else: wait(act,mm_taken,b,CV+CHUNKS)
                    turned.inc(act.activation(xr[:,h,:],xa[:,h,::-1],ACT.Copy))
                wait(act,b_split,b-1,5*SPLITS); wait(act,c_out,b-1,2); wait(act,dl_full,b-1,DL)
                for k in range(CHUNKS):
                    wait(act,mm_full,b,XD+k+1)
                    mm_taken.inc(act.activation(xd[:,k*CHUNK:(k+1)*CHUNK],mm[(XD+k)%2][0:XD_ROWS,:],ACT.Copy))
                def parts(j):
                    n=j%R
                    wait(act,u_taken,b,j+1)
                    wait(act,dp_out[n],b,j//R)
                    hi.inc(act.activation(dp[:,n,0,:],du[:,n,:],ACT.Copy))
                    wait(act,res,b,j+1)
                    mid.inc(act.activation(dp[:,n,1,:],du[:,n,:],ACT.Copy))
                for q in range(PARTS+1):
                    if q<PARTS:
                        wait(act,v_steps,b,5*q+1)
                        e_ready.inc(act.activation(ex[:,:],ex[:,:],ACT.Exp))
                    if q:
                        for j in range((q-1)*PART_TILES,(q-1)*PART_TILES+2): parts(j)
                    if q<PARTS:
                        wait(act,v_steps,b,5*q+3)
                        l_ready.inc(act.activation(ln[:,:],ln[:,:],ACT.Ln))
                    if q:
                        for j in range((q-1)*PART_TILES+2,q*PART_TILES): parts(j)

        @block.vector
        def _(dve):
            for c in (norm,dl_taken,conv,v_steps,u_taken,dp_ready,skip_ready): c.credit(dve)
            dve.wait_ge(w_ld,16*len(loads))
            for t in range(TAPS):
                dve.tensor_scalar(tapdiag[:,t,:],ident[:,:],conv_w[:,1,t:t+1],None,ALU.mult).then_inc(setup,1)
            dve.tensor_scalar(d4[:,:],d4[:,:],float(DIRS),None,ALU.mult).then_inc(setup,1)
            dve.wait_ge(setup,TAPS+1)
            with dve.Fori(0,BATCH) as b:
                wait(dve,x_in,b,1)
                for k in range(CHUNKS): norm.inc(dve.bn_stats(stats[:,k,:],xn[:,k*CHUNK:(k+1)*CHUNK]))
                wait(dve,norm,b,CHUNKS)
                dve.sem_inc(apart,1)
                norm.link(dve,b,dve.bn_aggr(mv[:,:],stats[:,:,:]))
                wait(dve,dl_full,b,1)
                dl_taken.link(dve,b,dve.tensor_copy(gmv[:,:],dl[0][:,0:2]))
                norm.link(dve,b,dve.tensor_tensor(dev[:,:],mv[:,0:1],gmv[:,0:1],ALU.subtract))
                norm.link(dve,b,dve.tensor_tensor(dev[:,:],dev[:,:],dev[:,:],ALU.mult))
                wait(dve,dl_full,b,2)
                dl_taken.link(dve,b,dve.tensor_tensor(var[:,:],dl[1][:,0:1],gmv[:,1:2],ALU.add))
                norm.link(dve,b,dve.tensor_scalar(var[:,:],var[:,:],EPS,None,ALU.add))
                wait(dve,std_ready,b,1)
                norm.link(dve,b,dve.reciprocal(rstd[:,:],std[:,:]))
                for k in range(CHUNKS):
                    s=xn[:,k*CHUNK:(k+1)*CHUNK]
                    norm.inc(dve.tensor_scalar(s,s,gmv[:,0:1],rstd[:,0:1],ALU.subtract,ALU.mult))
                wait(dve,u_full,b-1,TILES)
                for t in range(TAPS):
                    for r in range(2):
                        if t==0: wait(dve,mm_taken,b,IN[0]+(CHUNKS//2+1,CHUNKS)[r])
                        else: wait(dve,conv,b,2*t+r-1)
                        out=xa[:,0,r*(TOK//2):(r+1)*(TOK//2)].rearrange("p (r c) -> p r c",c=IMG)
                        src=shifted(0,r*IMG//2,IMG//2,t)
                        if t==0: ins=dve.tensor_scalar(out,src,conv_w[:,0,0:1],conv_b[:,0:1],ALU.mult,ALU.add)
                        else: ins=dve.scalar_tensor_tensor(out=out,in0=src,scalar=conv_w[:,0,t:t+1],in1=out,op0=ALU.mult,op1=ALU.add)
                        conv.inc(ins)
                def take_tile(j):
                    n=j%R
                    u=up[j%2][:,:].rearrange("p (h k e) -> p h k e",h=2,k=DIRS)
                    wait(dve,u_full,b,j+1)
                    s=(j//2)%2
                    if j%2==0: wait(dve,skip_out[s],b,j//4)
                    skip_ready.inc(dve.tensor_tensor(skip[:,s,j%2,:].rearrange("p (h e) -> p h e",h=2),u[:,:,0,:],d4[:,:].rearrange("p (h e) -> p h e",h=2),ALU.mult))
                    wait(dve,dp_ready,b,j-R+1)
                    dl_=delta[:,(j//PART_TILES)%2,j%PART_TILES,:].rearrange("p (h e) -> p h e",h=2)
                    u_taken.inc(dve.tensor_tensor(du[:,n,:].rearrange("p (h k e) -> p h k e",h=2,k=DIRS),u,dl_.unsqueeze(2).broadcast_to((128,2,DIRS,DH)),ALU.mult))
                def last_part(j):
                    wait(dve,mid,b,j+1)
                    dp_ready.inc(dve.tensor_tensor(dp[:,j%R,2,:],du[:,j%R,:],dp[:,j%R,1,:],ALU.subtract))
                def tiles(js):
                    for j in js:
                        take_tile(j)
                        if j: last_part(j-1)
                for q in range(PARTS+1):
                    if q<PARTS:
                        dq=delta[:,q%2,:,:]; flat=dq.rearrange("p j f -> p (j f)")
                        wait(dve,delta_out[q%2],b,q//2*2)
                        wait(dve,u_taken,b,(q-1)*PART_TILES)
                        for k in range(2):
                            i=2+2*q+k
                            wait(dve,dl_full,b,i+1)
                            dl_taken.inc(dve.tensor_tensor(dq[:,2*k:2*k+2,:],dl[i%2][:,:].rearrange("p (j f) -> p j f",j=2),b_dt[:,:].unsqueeze(1).broadcast_to((128,2,INNER)),ALU.add))
                        wait(dve,dl_taken,b,2+2*q+2)
                        v_steps.inc(dve.scalar_tensor_tensor(out=ex[:,:],in0=flat,scalar=-1.0,in1=flat,op0=ALU.mult,op1=ALU.min))
                    if q: tiles(range((q-1)*PART_TILES,(q-1)*PART_TILES+2))
                    if q<PARTS:
                        wait(dve,e_ready,b,q+1)
                        v_steps.link(dve,b,dve.tensor_scalar(ln[:,:],ex[:,:],1.0,None,ALU.add))
                        v_steps.inc(dve.scalar_tensor_tensor(out=ex[:,:],in0=ln[:,:],scalar=-1.0,in1=ex[:,:],op0=ALU.add,op1=ALU.subtract))
                    if q: tiles(range((q-1)*PART_TILES+2,q*PART_TILES))
                    if q<PARTS:
                        wait(dve,l_ready,b,q+1)
                        v_steps.link(dve,b,dve.scalar_tensor_tensor(out=ln[:,:],in0=flat,scalar=0.0,in1=ln[:,:],op0=ALU.max,op1=ALU.add))
                        v_steps.link(dve,b,dve.tensor_tensor(flat,ln[:,:],ex[:,:],ALU.subtract))
                last_part(TILES-1)
                for c in (norm,dl_taken,conv,v_steps,u_taken,dp_ready,skip_ready): c.done()

        @block.tensor
        def _(pe):
            for c in (mm_full,dl_full,u_full): c.credit(pe)
            pe.wait_ge(w_ld,16*len(loads)); pe.wait_ge(setup,TAPS+1)
            with pe.Fori(0,BATCH) as b:
                def bank(n):
                    wait(pe,mm_taken,b,n-1)
                    return mm[n%2]
                wait(pe,norm,b,CHUNKS+1)
                wait(pe,dl_taken,b-1,DL)
                dl_full.inc(pe.matmul(dl[0][:,0:2],group[:,:],mv[:,:],start=True,stop=True))
                wait(pe,norm,b,CHUNKS+3)
                dl_full.inc(pe.matmul(dl[1][:,0:1],group[:,:],dev[:,:],start=True,stop=True))
                for h in range(2):
                    for k in range(CHUNKS):
                        m=bank(IN[h]+k)
                        if h==0: wait(pe,norm,b,CHUNKS+5+k+1)
                        mm_full.inc(pe.matmul(m[:,:],w_in[:,h*128:(h+1)*128],xn[:,k*CHUNK:(k+1)*CHUNK],start=True,stop=True))
                for k in range(TILES//2):
                    m=bank(GT+k)
                    for j in range(2):
                        t=2*k+j
                        ins=pe.matmul(m[:,j*INNER:(j+1)*INNER],xn[:,t*TILE:(t+1)*TILE],w_in[:,INNER:2*INNER],start=True,stop=True)
                    mm_full.inc(ins)
                for k in range(CHUNKS):
                    m=bank(CV+k)
                    wait(pe,mm_taken,b,IN[1]+min(k+2,CHUNKS))
                    for t in range(TAPS):
                        ins=pe.matmul(m[:,:].rearrange("p (r c) -> p r c",c=IMG),tapdiag[:,t,:],shifted(1,8*k,8,t),start=(t==0),stop=(t==TAPS-1))
                    mm_full.inc(ins)
                for k in range(CHUNKS):
                    m=bank(XD+k)
                    wait(pe,xa0,b,k//(CHUNKS//2)+1)
                    for h in range(2):
                        ins=pe.matmul(m[0:XD_ROWS,:],w_x[:,h,:],xa[:,h,k*CHUNK:(k+1)*CHUNK],start=(h==0),stop=(h==1))
                    mm_full.inc(ins)
                def turn_tile(j):
                    wait(pe,u_taken,b,j-1)
                    wait(pe,skip_ready,b,j-1)
                    if j==0: wait(pe,turned,b,2)
                    for h in range(2):
                        for k in range(DIRS):
                            src=(xa,xr)[k//2][:,h,:]
                            out=up[j%2][:,(h*DIRS+k)*DH:(h*DIRS+k+1)*DH]
                            if k%2==0: ins=pe.transpose(out,src[:,j*TILE:(j+1)*TILE],ident[:,:])
                            else:
                                for c in range(2):
                                    ins=pe.matmul(out[c*IMG:(c+1)*IMG,:],src.rearrange("p (r c) -> p c r",c=IMG)[:,2*j+c,:],ident[:,:],start=True,stop=True)
                    u_full.inc(ins)
                for q in range(PARTS+1):
                    if q<PARTS:
                        for k in range(2):
                            i=2+2*q+k
                            wait(pe,dl_taken,b,i-1)
                            t=q*PART_TILES+2*k
                            wait(pe,mm_taken,b,XD+t*TILE//CHUNK+1)
                            for j in range(2):
                                ins=pe.matmul(dl[i%2][:,j*INNER:(j+1)*INNER],xd[0:RANK,(t+j)*TILE:(t+j+1)*TILE],w_dt[:,:],start=True,stop=True)
                            dl_full.inc(ins)
                    if q:
                        for j in range((q-1)*PART_TILES,q*PART_TILES): turn_tile(j)
                for c in (mm_full,dl_full,u_full): c.done()

GTILES=4; GROUP_TOK=GTILES*TILE; NG=TILES//GTILES
HEADS=8; EXPERTS=8
YD_PER=2*GTILES+2*2*GTILES+1

class Phase:
    def __init__(self, nc, ctx, tag): self.nc,self.ctx,self.tag=nc,ctx,tag
    def sb(self,name,shape,dt=F32): return self.ctx.enter_context(self.nc.sbuf_tensor(self.tag+name,shape,dt))
    def ps(self,name,n=512): return self.ctx.enter_context(self.nc.psum_tensor(self.tag+name,[128,n],F32))
    def count(self,name,per,step=1): return Count(self.ctx.enter_context(self.nc.semaphore(self.tag+name)),per,step)
    def sem(self,name): return self.ctx.enter_context(self.nc.semaphore(self.tag+name))

def wait(eng,c,image,n): eng.wait_ge(c.sem,c.at(image,n))

def rsqrt(pool,c,r,b,i,n,mv,rstd,half,eps):
    wait(pool,c,b,3*n*i+2*n)
    r.link(pool,b,pool.tensor_tensor(rstd,mv[:,:,1:2],eps,ALU.add))
    r.inc(pool.tensor_tensor(rstd,rstd,half,ALU.pow))

def normalize(dve,apart,c,r,b,out,src,stats,mv,rstd):
    n=len(src)
    for j in range(n): c.inc(dve.bn_stats(stats[:,j,:],src[j]))
    wait(dve,c,b,c.n)
    dve.sem_inc(apart,1)
    for j in range(n): c.inc(dve.bn_aggr(mv[:,j,:],stats[:,j,:]))
    wait(dve,c,b,c.n)
    wait(dve,r,b,2*(c.n//(3*n)+1))
    for j in range(n):
        c.inc(dve.tensor_scalar(out[j],src[j],mv[:,j,0:1],rstd[:,j,:],ALU.subtract,ALU.mult))

def merge_directions(nc, d):
    with ExitStack() as ctx:
        p=Phase(nc,ctx,"md_"); sb,ps,count=p.sb,p.ps,p.count
        ident=sb("ident",[128,128]); flip=sb("flip",[128,128]); w_out=sb("w_out",[128,2,128]); ln_w=sb("ln_w",[128,INNER]); ln_b=sb("ln_b",[128,INNER])
        ys=sb("ys",[128,2,DIRS,GTILES,INNER]); skip=sb("skip",[128,2,GTILES,INNER]); gate=sb("gate",[128,2,GTILES,INNER]); xin=sb("xin",[128,2,GTILES,CH])
        yn=sb("yn",[128,2,GTILES,INNER]); yt=sb("yt",[128,2,GROUP_TOK]); x1=sb("x1",[128,2,GTILES,CH])
        stats=sb("stats",[128,2,6]); mv=sb("mv",[128,2,2]); rstd=sb("rstd",[128,2,1]); half=sb("half",[128,2,1]); eps=sb("eps",[128,2,1])
        ybank=[ps(f"y{i}") for i in range(4)]; tbank=ps("tb",1024); obank=[ps(f"o{i}") for i in range(2)]
        w_ld=p.sem("w_ld")
        y_in=[count(f"y_in{q}",NG//2*YD_PER,16) for q in range(2)]
        xg_in=[count(f"xg_in{q}",NG//2*2,16) for q in range(2)]
        y_sum=count("y_sum",NG*2); normed=count("normed",NG*2*6); consts=p.sem("consts"); apart=p.sem("apart"); rstd_ready=count("rstd_ready",NG*4); affine=count("affine",NG*3)
        t_full=count("t_full",NG); t_taken=count("t_taken",NG); o_full=count("o_full",NG); o_taken=count("o_taken",NG)
        x1_out=[count(f"x1_out{q}",NG//2,16) for q in range(2)]
        block=ctx.enter_context(nc.Block())
        loads=((ident[:,:],"ident"),(flip[:,:],"flip"),(w_out[:,:,:],"w_out"),(ln_w[:,:],"ln_w"),(ln_b[:,:],"ln_b"))

        @block.sync
        def _(sp):
            for dst,name in loads: sp.dma_start(dst,d[name]).then_inc(w_ld,16)
            for c in (*y_in,*xg_in,*x1_out): c.credit(sp)
            y_d=d["y"].rearrange("b (t h) (k e) -> b k t h e",h=2,k=DIRS)
            def store(b,g):
                wait(sp,o_taken,b,g+1)
                x1_out[g%2].inc(sp.dma_start(d["x1"][b,g*GROUP_TOK:(g+1)*GROUP_TOK].rearrange("(j t) c -> t j c",t=TILE), x1[:,g%2,:,:]))
            with sp.Fori(0,BATCH) as b:
                for g in range(NG):
                    q=g%2
                    wait(sp,y_sum,b,2*(g-1))
                    for j in range(GTILES):
                        t=g*GTILES+j; m=TILES-1-t
                        for k,tile in ((0,t),(2,m)):
                            y_in[q].inc(sp.dma_start(ys[:,q,k,j,:].rearrange("p (h e) -> p h e",h=2),y_d[b,k,tile*TILE:(tile+1)*TILE]))
                        for k,tile in ((1,t),(3,m)):
                            for r in range(2):
                                y_in[q].inc(sp.dma_start(ys[r*IMG:(r+1)*IMG,q,k,j,:].rearrange("p (h e) -> p h e",h=2),y_d[b,k,2*tile+r:2*tile+r+(IMG-1)*IMG+1:IMG]))
                    tok=slice(g*GROUP_TOK,(g+1)*GROUP_TOK)
                    y_in[q].inc(sp.dma_start(skip[:,q,:,:],d["skip"][b,tok].rearrange("(j t) f -> t j f",t=TILE)))
                    wait(sp,affine,b,3*(g-1))
                    xg_in[q].inc(sp.dma_start(gate[:,q,:,:],d["gate"][b,tok].rearrange("(j t) f -> t j f",t=TILE)))
                    wait(sp,o_full,b,g-1)
                    xg_in[q].inc(sp.dma_start(xin[:,q,:,:],d["x"][b,tok].rearrange("(j t) f -> t j f",t=TILE)))
                    if g>1: store(b,g-2)
                store(b,NG-2); store(b,NG-1)
            for c in x1_out: wait(sp,c,BATCH-1,c.per)

        @block.gpsimd
        def _(pool):
            for c in (affine,rstd_ready): c.credit(pool)
            pool.memset(half[:,:,:],-0.5).then_inc(consts,1)
            pool.memset(eps[:,:,:],EPS).then_inc(consts,1)
            pool.wait_ge(consts,2)
            pool.wait_ge(w_ld,16*len(loads))
            with pool.Fori(0,BATCH) as b:
                def rstds(g):
                    for i in (2*g,2*g+1): rsqrt(pool,normed,rstd_ready,b,i,2,mv,rstd[:,:,:],half[:,:,:],eps[:,:,:])
                rstds(0)
                for g in range(NG):
                    if g+1<NG: rstds(g+1)
                    y=yn[:,g%2,:,:]
                    wait(pool,normed,b,12*(g+1))
                    wait(pool,xg_in[g%2],b,(g//2+1)*2)
                    for m in (ln_w,ln_b):
                        affine.link(pool,b,pool.tensor_tensor(y,y,m[:,:].unsqueeze(1).broadcast_to((128,GTILES,INNER)),ALU.mult if m is ln_w else ALU.add))
                    affine.inc(pool.tensor_tensor(y,y,gate[:,g%2,:,:],ALU.mult))

        @block.scalar
        def _(act):
            for c in (t_taken,o_taken): c.credit(act)
            with act.Fori(0,BATCH) as b:
                for g in range(NG):
                    wait(act,t_full,b,g+1); wait(act,o_full,b,g)
                    t_taken.inc(act.activation(yt[:,:,:].rearrange("p h t -> p (h t)"),tbank[:,:],ACT.Copy))
                    wait(act,o_full,b,g+1); wait(act,x1_out[g%2],b,g//2)
                    o_taken.inc(act.activation(x1[:,g%2,:,:].rearrange("p j c -> p (j c)"),obank[g%2][:,:],ACT.Copy))

        @block.vector
        def _(dve):
            normed.credit(dve)
            with dve.Fori(0,BATCH) as b:
                for g in range(NG):
                    wait(dve,t_full,b,g-1)
                    for k in range(2):
                        i=2*g+k
                        wait(dve,y_sum,b,i+1)
                        src=[ybank[i%4][:,j*INNER:(j+1)*INNER] for j in range(2)]
                        out=[yn[:,g%2,2*k+j,:] for j in range(2)]
                        wait(dve,normed,b,normed.n)
                        normalize(dve,apart,normed,rstd_ready,b,out,src,stats,mv,rstd)
                normed.done()

        @block.tensor
        def _(pe):
            for c in (y_sum,t_full,o_full): c.credit(pe)
            pe.wait_ge(w_ld,16*len(loads))
            def sum_y(b,g):
                q=g%2
                wait(pe,y_in[q],b,(g//2+1)*YD_PER)
                for k in range(2):
                    i=2*g+k
                    wait(pe,normed,b,6*(i-3))
                    for j in range(2):
                        t=2*k+j
                        out=ybank[i%4][:,j*INNER:(j+1)*INNER]
                        terms=((ident,ys[:,q,0,t,:]),(ident,ys[:,q,1,t,:]),(flip,ys[:,q,2,t,:]),(flip,ys[:,q,3,t,:]),(ident,skip[:,q,t,:]))
                        for n,(m,y) in enumerate(terms):
                            ins=pe.matmul(out,m[:,:],y,start=(n==0),stop=(n==len(terms)-1))
                    y_sum.inc(ins)
            def project(b,g):
                q=g%2
                wait(pe,affine,b,3*(g+1)); wait(pe,t_taken,b,g)
                for h in range(2):
                    for j in range(GTILES):
                        ins=pe.transpose(tbank[:,h*512+j*TILE:h*512+(j+1)*TILE],yn[:,q,j,h*128:(h+1)*128],ident[:,:])
                t_full.inc(ins)
                wait(pe,t_taken,b,g+1); wait(pe,o_taken,b,g-1)
                wait(pe,xg_in[q],b,(g//2+1)*2)
                for j in range(GTILES):
                    out=obank[q][:,j*CH:(j+1)*CH]
                    for h in range(2):
                        pe.matmul(out,yt[:,h,j*TILE:(j+1)*TILE],w_out[:,h,:],start=(h==0),stop=False)
                    ins=pe.matmul(out,ident[:,:],xin[:,q,j,:],start=False,stop=True)
                o_full.inc(ins)
            with pe.Fori(0,BATCH) as b:
                sum_y(b,0)
                for g in range(NG):
                    if g+1<NG: sum_y(b,g+1)
                    project(b,g)
                for c in (y_sum,t_full,o_full): c.done()

def attend(nc, d):
    with ExitStack() as ctx:
        p=Phase(nc,ctx,"at_"); sb,ps,count=p.sb,p.ps,p.count
        HW=HEADS*CH
        ident=sb("ident",[128,128]); wk=sb("wk",[128,HW]); wv=sb("wv",[128,HW]); qs=sb("qs",[128,HEADS*(HEADS+1)]); qt=sb("qt",[128,HEADS])
        upto=sb("upto",[128,128]); beyond=sb("beyond",[128,128])
        x1=sb("x1",[128,2,GTILES,CH]); tn=sb("tn",[128,2,GTILES,CH]); tt=sb("tt",[128,2,GROUP_TOK])
        kh=sb("kh",[128,2,512]); s=sb("s",[HEADS,512]); m=sb("m",[HEADS,512]); e=sb("e",[HEADS,2,512]); u=sb("u",[HEADS,512]); r=sb("r",[HEADS,2,512]); last=sb("last",[HEADS,2])
        er=sb("er",[128,2,GTILES*2*HEADS]); v=sb("v",[128,2,HW]); ev=sb("ev",[128,2,HW]); wr=sb("wr",[128,2,HW]); x2=sb("x2",[128,2,GTILES,CH]); mean=sb("mean",[128,2,CH])
        stats=sb("stats",[128,GTILES,6]); mv=sb("mv",[128,GTILES,2]); rstd=sb("rstd",[128,GTILES,1]); half=sb("half",[128,GTILES,1]); eps=sb("eps",[128,GTILES,1])
        kb=[ps(f"kb{i}") for i in range(2)]; vb=ps("vb",1024); wb=ps("wb",1024); tb=ps("tb"); sbk=ps("sb")
        w_ld=p.sem("w_ld"); setup=p.sem("setup")
        x_in=[count(f"x_in{i}",NG//2,16) for i in range(2)]; x_out=[count(f"x_out{i}",NG//2,16) for i in range(2)]
        normed=count("normed",NG*3*GTILES); consts=p.sem("consts"); apart=p.sem("apart"); rstd_ready=count("rstd_ready",NG*2); t_full=count("t_full",NG*2); t_taken=count("t_taken",NG)
        k_full=count("k_full",NG*HEADS); k_taken=count("k_taken",NG*HEADS);
        scan=count("scan",2+NG*8); e_ready=count("e_ready",NG); er_taken=count("er_taken",NG); s_used=count("s_used",NG*HEADS)
        v_full=count("v_full",TILES); v_taken=count("v_taken",TILES); ev_ready=count("ev_ready",TILES)
        w_full=count("w_full",2*TILES); weighed=count("weighed",TILES); reduced=count("reduced",TILES); added=count("added",TILES)
        block=ctx.enter_context(nc.Block())
        loads=((ident[:,:],"ident"),(wk[:,:],"w_k"),(wv[:,:],"w_v"),(qt[:,:],"q_t"),(upto[:,:],"upto"),(beyond[:,:],"beyond"))

        @block.sync
        def _(sp):
            for dst,name in loads: sp.dma_start(dst,d[name]).then_inc(w_ld,16)
            for c in (*x_in,*x_out): c.credit(sp)
            with sp.Fori(0,BATCH) as b:
                def store(g):
                    wait(sp,added,b,(g+1)*GTILES)
                    x_out[g%2].inc(sp.dma_start(d["x2"][b,g*GROUP_TOK:(g+1)*GROUP_TOK].rearrange("(j t) c -> t j c",t=TILE), x2[:,g%2,:,:]))
                for g in range(NG):
                    wait(sp,added,b,(g-1)*GTILES)
                    x_in[g%2].inc(sp.dma_start(x1[:,g%2,:,:],d["x1"][b,g*GROUP_TOK:(g+1)*GROUP_TOK].rearrange("(j t) c -> t j c",t=TILE)))
                    if g>1: store(g-2)
                store(NG-2); store(NG-1)
            for c in x_out: wait(sp,c,BATCH-1,c.per)

        @block.gpsimd
        def _(pool):
            for c in (ev_ready,rstd_ready): c.credit(pool)
            pool.memset(half[:,:,:],-0.5).then_inc(consts,1)
            pool.memset(eps[:,:,:],EPS).then_inc(consts,1)
            pool.wait_ge(consts,2)
            pool.memset(qs[:,:],0.0).then_inc(setup,1)
            pool.wait_ge(w_ld,16*len(loads)); pool.wait_ge(setup,1)
            pool.tensor_copy(qs[:,:].rearrange("p (h x) -> p h x",h=HEADS)[:,:,0],qt[:,:]).then_inc(setup,1)
            with pool.Fori(0,BATCH) as b:
                def rstds(g): rsqrt(pool,normed,rstd_ready,b,g,GTILES,mv,rstd[:,:,:],half[:,:,:],eps[:,:,:])
                rstds(0); rstds(1)
                for j in range(TILES):
                    g=j//GTILES; i=j%GTILES
                    wait(pool,v_taken,b,j+1); wait(pool,er_taken,b,g+1); wait(pool,w_full,b,2*(j-1))
                    ej=er[:,g%2,i*16:i*16+8].unsqueeze(2).broadcast_to((128,HEADS,CH))
                    ev_ready.inc(pool.tensor_tensor(ev[:,j%2,:].rearrange("p (h c) -> p h c",h=HEADS),v[:,j%2,:].rearrange("p (h c) -> p h c",h=HEADS),ej,ALU.mult))
                    if i==GTILES-1 and g+2<NG: rstds(g+2)

        @block.scalar
        def _(act):
            for c in (t_taken,k_taken,e_ready,v_taken): c.credit(act)
            with act.Fori(0,BATCH) as b:
                def turn(g):
                    wait(act,t_full,b,2*g+1); wait(act,v_full,b,(g-1)*GTILES)
                    t_taken.inc(act.activation(tt[:,g%2,:],tb[:,:],ACT.Copy))
                def silu_k(g,h):
                    n=g*HEADS+h
                    wait(act,k_full,b,n+1); wait(act,s_used,b,n-1)
                    k_taken.inc(act.activation(kh[:,n%2,:],kb[n%2][:,:],ACT.Silu))
                def exps(g):
                    wait(act,scan,b,2+8*g+3)
                    e_ready.inc(act.activation(e[:,g%2,:],e[:,g%2,:],ACT.Exp))
                def silu_v(j):
                    wait(act,v_full,b,j+1); wait(act,ev_ready,b,j-1)
                    v_taken.inc(act.activation(v[:,j%2,:],vb[:,:],ACT.Silu))
                turn(0)
                for h in range(HEADS): silu_k(0,h)
                exps(0)
                for g in range(NG):
                    if g+1<NG: turn(g+1)
                    silu_v(g*GTILES)
                    for i in range(GTILES):
                        if i+1<GTILES: silu_v(g*GTILES+i+1)
                        if g+1<NG:
                            silu_k(g+1,2*i); silu_k(g+1,2*i+1)
                    if g+1<NG: exps(g+1)

        @block.vector
        def _(dve):
            for c in (normed,scan,er_taken,weighed,reduced,added): c.credit(dve)
            with dve.Fori(0,BATCH) as b:
                def norm(g):
                    wait(dve,x_in[g%2],b,g//2+1); wait(dve,t_full,b,2*(g-2)+1); wait(dve,normed,b,normed.n)
                    normalize(dve,apart,normed,rstd_ready,b,[tn[:,g%2,j,:] for j in range(GTILES)],[x1[:,g%2,j,:] for j in range(GTILES)],stats,mv,rstd)
                def scans(g):
                    wait(dve,s_used,b,HEADS*(g+1))
                    scan.link(dve,b,dve.tensor_copy(s[:,:],sbk[0:HEADS,:]))
                    scan.link(dve,b,dve.tensor_tensor_scan(m[:,:],s[:,:],s[:,:],last[:,0:1],ALU.max,ALU.max))
                    wait(dve,t_full,b,2*(g-1))
                    scan.link(dve,b,dve.tensor_tensor(e[:,g%2,:],s[:,:],m[:,:],ALU.subtract))
                    scan.inc(dve.tensor_copy(last[:,0:1],m[:,511:512]))
                    wait(dve,e_ready,b,g+1)
                    scan.link(dve,b,dve.tensor_tensor_scan(u[:,:],e[:,g%2,:],e[:,g%2,:],last[:,1:2],ALU.add,ALU.max))
                    scan.link(dve,b,dve.tensor_copy(last[:,1:2],u[:,511:512]))
                    scan.link(dve,b,dve.reciprocal(r[:,g%2,:],u[:,:]))
                    scan.link(dve,b,dve.tensor_scalar(r[:,g%2,:],r[:,g%2,:],1.0/HEADS,None,ALU.mult))
                def take_er(g):
                    wait(dve,t_full,b,2*g+2); wait(dve,weighed,b,(g-1)*GTILES); wait(dve,ev_ready,b,(g-1)*GTILES)
                    er_taken.inc(dve.tensor_copy(er[:,g%2,:],tb[:,0:GTILES*2*HEADS]))
                def weigh(j):
                    g=j//GTILES; i=j%GTILES
                    wait(dve,w_full,b,2*j+1); wait(dve,reduced,b,j-1)
                    if i==0: wait(dve,er_taken,b,g+1)
                    rj=er[:,g%2,i*16+8:i*16+16].unsqueeze(2).broadcast_to((128,HEADS,CH))
                    weighed.inc(dve.tensor_tensor(wr[:,j%2,:].rearrange("p (h c) -> p h c",h=HEADS),wb[:,:].rearrange("p (h c) -> p h c",h=HEADS),rj,ALU.mult))
                def finish(j):
                    g=j//GTILES; i=j%GTILES
                    wait(dve,weighed,b,j+1); wait(dve,added,b,j-1)
                    reduced.inc(dve.tensor_reduce(mean[:,j%2,:],wr[:,j%2,:].rearrange("p (h c) -> p c h",h=HEADS),AX.X,ALU.add))
                    if i==0: wait(dve,x_out[g%2],b,g//2)
                    wait(dve,reduced,b,j+1)
                    added.inc(dve.tensor_tensor(x2[:,g%2,i,:],x1[:,g%2,i,:],mean[:,j%2,:],ALU.add))
                wait(dve,scan,b-1,scan.per)
                scan.link(dve,b,dve.memset(last[:,0:1],-3.0e38))
                scan.link(dve,b,dve.memset(last[:,1:2],0.0))
                norm(0)
                scans(0)
                norm(1)
                for g in range(NG):
                    take_er(g)
                    for i in range(GTILES):
                        j=g*GTILES+i
                        weigh(j)
                        finish(j)
                    if g+1<NG: scans(g+1)
                    if g+2<NG: norm(g+2)
                for c in (normed,scan,er_taken,weighed,reduced,added): c.done()

        @block.tensor
        def _(pe):
            for c in (t_full,k_full,s_used,v_full,w_full): c.credit(pe)
            pe.wait_ge(w_ld,16*len(loads)); pe.wait_ge(setup,2)
            with pe.Fori(0,BATCH) as b:
                def turn(g):
                    wait(pe,normed,b,(g+1)*3*GTILES); wait(pe,er_taken,b,g)
                    for j in range(GTILES): ins=pe.transpose(tb[:,j*TILE:(j+1)*TILE],tn[:,g%2,j,:],ident[:,:])
                    t_full.inc(ins)
                def turn_er(g):
                    wait(pe,t_taken,b,g+1); wait(pe,scan,b,2+8*g+8)
                    for j in range(GTILES):
                        for n,x in enumerate((e,r)):
                            ins=pe.matmul(tb[:,j*16+n*8:j*16+n*8+8],x[:,g%2,j*TILE:(j+1)*TILE],ident[0:HEADS,0:HEADS],start=True,stop=True)
                    t_full.inc(ins)
                def keys(g,h):
                    n=g*HEADS+h
                    if h==0: wait(pe,t_taken,b,g+1)
                    wait(pe,k_taken,b,n-1)
                    k_full.inc(pe.matmul(kb[n%2][:,:],wk[:,h*CH:(h+1)*CH],tt[:,g%2,:],start=True,stop=True))
                def score(g,h):
                    n=g*HEADS+h
                    wait(pe,k_taken,b,n+1)
                    if h==0: wait(pe,scan,b,2+8*(g-1)+1)
                    ins=pe.matmul(sbk[0:HEADS,:],qs[:,h*HEADS:(h+1)*HEADS],kh[:,n%2,:],start=(h==0),stop=(h==HEADS-1))
                    s_used.inc(ins)
                def values(j):
                    g=j//GTILES; i=j%GTILES
                    wait(pe,v_taken,b,j)
                    for n in range(2):
                        ins=pe.matmul(vb[:,n*512:(n+1)*512],tt[:,g%2,i*TILE:(i+1)*TILE],wv[:,n*512:(n+1)*512],start=True,stop=True)
                    v_full.inc(ins)
                def run(j,part):
                    if part==0: wait(pe,ev_ready,b,j+1)
                    wait(pe,weighed,b,j+part)
                    for n in range(2):
                        ins=pe.matmul(wb[:,n*512:(n+1)*512],(upto,beyond)[part][:,:],ev[:,j%2,n*512:(n+1)*512],start=(j==0 and part==0),stop=True,skip_group_check=True)
                    w_full.inc(ins)
                turn(0)
                for h in range(HEADS):
                    keys(0,h)
                    if h: score(0,h-1)
                score(0,HEADS-1)
                for g in range(NG):
                    turn_er(g)
                    if g+1<NG: turn(g+1)
                    values(g*GTILES)
                    for i in range(GTILES):
                        j=g*GTILES+i
                        run(j,0)
                        if i+1<GTILES: values(j+1)
                        if g+1<NG:
                            for h in (2*i,2*i+1):
                                keys(g+1,h)
                                if h: score(g+1,h-1)
                            if i==GTILES-1: score(g+1,HEADS-1)
                        run(j,1)

def experts(nc, d):
    with ExitStack() as ctx:
        p=Phase(nc,ctx,"ex_"); sb,ps,count=p.sb,p.ps,p.count
        EW=EXPERTS*CH
        ident=sb("ident",[128,128]); rw=sb("rw",[128,EXPERTS]); rb=sb("rb",[128,EXPERTS]); ew=sb("ew",[128,EW]); eb=sb("eb",[EXPERTS,CH]); iota=sb("iota",[128,EXPERTS])
        x2=sb("x2",[128,3,GTILES,CH]); tn=sb("tn",[128,2,GTILES,CH]); tt=sb("tt",[128,2,GROUP_TOK])
        lg=sb("lg",[128,GTILES,EXPERTS]); mx=sb("mx",[128,GTILES]); top=sb("top",[128,GTILES,8]); idx=sb("idx",[128,GTILES,8],mybir.dt.uint32); idf=sb("idf",[128,GTILES,8])
        den=sb("den",[128,GTILES,1]); w2=sb("w2",[128,GTILES,2]); wa=sb("wa",[128,GTILES,EXPERTS]); wb2=sb("wb2",[128,GTILES,EXPERTS]); sel=sb("sel",[128,2,GTILES,EXPERTS]); st=sb("st",[EXPERTS,512])
        pr=sb("pr",[128,2,EW]); mo=sb("mo",[128,2,GTILES,CH]); res=sb("res",[128,2,GTILES*CH])
        stats=sb("stats",[128,GTILES,6]); mv=sb("mv",[128,GTILES,2]); rstd=sb("rstd",[128,GTILES,1]); half=sb("half",[128,GTILES,1]); eps=sb("eps",[128,GTILES,1])
        tb=ps("tb"); lb=ps("lb"); wtb=ps("wtb"); bb=ps("bb"); eb_=[ps(f"eb{i}",1024) for i in range(2)]
        w_ld=p.sem("w_ld")
        XS=[len(range(i,NG,3)) for i in range(3)]
        x_in=[count(f"x_in{i}",XS[i],16) for i in range(3)]; x_out=[count(f"x_out{i}",NG//2,16) for i in range(2)]
        normed=count("normed",NG*3*GTILES); consts=p.sem("consts"); apart=p.sem("apart"); rstd_ready=count("rstd_ready",NG*2); t_full=count("t_full",NG); t_taken=count("t_taken",NG); l_full=count("l_full",NG)
        RS=3+2*GTILES+4+2*GTILES+1
        route=count("route",NG*RS); e_ready=count("e_ready",NG)
        wt_full=count("wt_full",NG); wt_taken=count("wt_taken",NG); b_full=count("b_full",NG)
        e_full=count("e_full",TILES); weighed=count("weighed",TILES); reduced=count("reduced",TILES); added=count("added",NG)
        block=ctx.enter_context(nc.Block())
        loads=((ident[:,:],"ident"),(rw[:,:],"router_w"),(rb[:,:],"router_b"),(ew[:,:],"expert_w"),(eb[:,:],"expert_b"),(iota[:,:],"iota"))

        @block.sync
        def _(sp):
            for dst,name in loads: sp.dma_start(dst,d[name]).then_inc(w_ld,16)
            for c in (*x_in,*x_out): c.credit(sp)
            with sp.Fori(0,BATCH) as b:
                def store(g):
                    wait(sp,added,b,g+1)
                    x_out[g%2].inc(sp.dma_start(d["out"][b,g*GROUP_TOK:(g+1)*GROUP_TOK].rearrange("(j t) c -> t j c",t=TILE), res[:,g%2,:].rearrange("p (j c) -> p j c",j=GTILES)))
                for g in range(NG):
                    if g<3:
                        wait(sp,b_full,b,0)
                    else: wait(sp,b_full,b,g-2)
                    x_in[g%3].inc(sp.dma_start(x2[:,g%3,:,:],d["x2"][b,g*GROUP_TOK:(g+1)*GROUP_TOK].rearrange("(j t) c -> t j c",t=TILE)))
                    if g>1: store(g-2)
                store(NG-2); store(NG-1)
            for c in x_out: wait(sp,c,BATCH-1,c.per)

        @block.gpsimd
        def _(pool):
            rstd_ready.credit(pool)
            pool.memset(half[:,:,:],-0.5).then_inc(consts,1)
            pool.memset(eps[:,:,:],EPS).then_inc(consts,1)
            pool.wait_ge(consts,2)
            with pool.Fori(0,BATCH) as b:
                for g in range(NG): rsqrt(pool,normed,rstd_ready,b,g,GTILES,mv,rstd[:,:,:],half[:,:,:],eps[:,:,:])

        @block.scalar
        def _(act):
            for c in (t_taken,e_ready,wt_taken): c.credit(act)
            with act.Fori(0,BATCH) as b:
                def turn(g):
                    wait(act,t_full,b,g+1); wait(act,e_full,b,(g-1)*GTILES)
                    t_taken.inc(act.activation(tt[:,g%2,:],tb[:,:],ACT.Copy))
                def exps(g):
                    wait(act,route,b,RS*g+3)
                    e_ready.inc(act.activation(lg[:,:,:],lg[:,:,:],ACT.Exp))
                turn(0); exps(0)
                for g in range(NG):
                    if g+1<NG: turn(g+1)
                    wait(act,wt_full,b,g+1); wait(act,b_full,b,g)
                    wt_taken.inc(act.activation(st[:,:],wtb[0:EXPERTS,:],ACT.Copy))
                    if g+1<NG: exps(g+1)

        @block.vector
        def _(dve):
            for c in (normed,route,weighed,reduced,added): c.credit(dve)
            dve.wait_ge(w_ld,16*len(loads))
            with dve.Fori(0,BATCH) as b:
                def norm(g):
                    wait(dve,x_in[g%3],b,g//3+1); wait(dve,t_full,b,g-1); wait(dve,normed,b,normed.n)
                    normalize(dve,apart,normed,rstd_ready,b,[tn[:,g%2,j,:] for j in range(GTILES)],[x2[:,g%3,j,:] for j in range(GTILES)],stats,mv,rstd)
                def link(ins): route.link(dve,b,ins)
                def weights(g):
                    wait(dve,l_full,b,g+1)
                    link(dve.tensor_tensor(lg[:,:,:],lb[:,0:GTILES*EXPERTS].rearrange("p (j e) -> p j e",j=GTILES),rb[:,:].unsqueeze(1).broadcast_to((128,GTILES,EXPERTS)),ALU.add))
                    link(dve.tensor_reduce(mx[:,:],lg[:,:,:],AX.X,ALU.max))
                    link(dve.tensor_tensor(lg[:,:,:],lg[:,:,:],mx[:,:].unsqueeze(2).broadcast_to((128,GTILES,EXPERTS)),ALU.subtract))
                    wait(dve,e_ready,b,g+1)
                    dve.sem_inc(apart,1)
                    for j in range(GTILES): route.inc(dve.max(top[:,j,:],lg[:,j,:]))
                    wait(dve,route,b,route.n)
                    dve.sem_inc(apart,1)
                    for j in range(GTILES): route.inc(dve.max_index(idx[:,j,:],top[:,j,:],lg[:,j,:]))
                    link(dve.tensor_tensor(den[:,:,:],top[:,:,0:1],top[:,:,1:2],ALU.add))
                    link(dve.reciprocal(den[:,:,:],den[:,:,:]))
                    link(dve.tensor_tensor(w2[:,:,:],top[:,:,0:2],den[:,:,:].broadcast_to((128,GTILES,2)),ALU.mult))
                    link(dve.tensor_copy(idf[:,:,:],idx[:,:,:]))
                    for j in range(GTILES):
                        for n,w in enumerate((wa,wb2)):
                            route.inc(dve.tensor_scalar(w[:,j,:],iota[:,:],idf[:,j,n:n+1],w2[:,j,n:n+1],ALU.is_equal,ALU.mult))
                    wait(dve,route,b,route.n)
                    wait(dve,wt_full,b,g-1); wait(dve,weighed,b,(g-1)*GTILES)
                    link(dve.tensor_tensor(sel[:,g%2,:,:],wa[:,:,:],wb2[:,:,:],ALU.add))
                def mix(j):
                    g=j//GTILES; i=j%GTILES
                    wait(dve,e_full,b,j+1); wait(dve,reduced,b,j-1)
                    weighed.inc(dve.tensor_tensor(pr[:,j%2,:].rearrange("p (e c) -> p e c",e=EXPERTS),eb_[j%2][:,:].rearrange("p (e c) -> p e c",e=EXPERTS),sel[:,g%2,i,:].unsqueeze(2).broadcast_to((128,EXPERTS,CH)),ALU.mult))
                def fold(j):
                    g=j//GTILES; i=j%GTILES
                    wait(dve,weighed,b,j+1)
                    if i==0: wait(dve,added,b,g-1)
                    reduced.inc(dve.tensor_reduce(mo[:,g%2,i,:],pr[:,j%2,:].rearrange("p (e c) -> p c e",e=EXPERTS),AX.X,ALU.add))
                norm(0); norm(1); weights(0)
                for g in range(NG):
                    for i in range(GTILES):
                        mix(g*GTILES+i)
                        if i: fold(g*GTILES+i-1)
                    fold((g+1)*GTILES-1)
                    if g+2<NG: norm(g+2)
                    if g+1<NG: weights(g+1)
                    wait(dve,b_full,b,g+1); wait(dve,reduced,b,(g+1)*GTILES); wait(dve,x_out[g%2],b,g//2)
                    added.inc(dve.tensor_tensor(res[:,g%2,:],mo[:,g%2,:,:].rearrange("p j c -> p (j c)"),bb[:,:],ALU.add))
                for c in (normed,route,weighed,reduced,added): c.done()

        @block.tensor
        def _(pe):
            for c in (t_full,l_full,e_full,wt_full,b_full): c.credit(pe)
            pe.wait_ge(w_ld,16*len(loads))
            with pe.Fori(0,BATCH) as b:
                def turn(g):
                    wait(pe,normed,b,(g+1)*3*GTILES); wait(pe,t_taken,b,g)
                    for j in range(GTILES): ins=pe.transpose(tb[:,j*TILE:(j+1)*TILE],tn[:,g%2,j,:],ident[:,:])
                    t_full.inc(ins)
                def logits(g):
                    wait(pe,t_taken,b,g+1); wait(pe,route,b,RS*(g-1)+1)
                    for j in range(GTILES): ins=pe.matmul(lb[:,j*EXPERTS:(j+1)*EXPERTS],tt[:,g%2,j*TILE:(j+1)*TILE],rw[:,:],start=True,stop=True)
                    l_full.inc(ins)
                def project(j):
                    g=j//GTILES; i=j%GTILES
                    wait(pe,weighed,b,j-1)
                    for n in range(2):
                        ins=pe.matmul(eb_[j%2][:,n*512:(n+1)*512],tt[:,g%2,i*TILE:(i+1)*TILE],ew[:,n*512:(n+1)*512],start=True,stop=True)
                    e_full.inc(ins)
                def biases(g):
                    wait(pe,route,b,RS*(g+1)); wait(pe,wt_taken,b,g)
                    for j in range(GTILES): ins=pe.matmul(wtb[0:EXPERTS,j*TILE:(j+1)*TILE],sel[:,g%2,j,:],ident[:,:],start=True,stop=True)
                    wt_full.inc(ins)
                    wait(pe,wt_taken,b,g+1); wait(pe,added,b,g)
                    for j in range(GTILES):
                        pe.matmul(bb[:,j*CH:(j+1)*CH],st[:,j*TILE:(j+1)*TILE],eb[:,:],start=True,stop=False)
                        ins=pe.matmul(bb[:,j*CH:(j+1)*CH],ident[:,:],x2[:,g%3,j,:],start=False,stop=True)
                    b_full.inc(ins)
                turn(0); logits(0)
                for g in range(NG):
                    for i in range(GTILES):
                        project(g*GTILES+i)
                        if i==1 and g+1<NG: turn(g+1)
                    biases(g)
                    if g+1<NG: logits(g+1)
                for c in (t_full,l_full,e_full,wt_full,b_full): c.done()



def build(nc, d):
    L = TOK
    def scratch(name, shape, dt=F32):
        d[name] = nc.dram_tensor("scratch_" + name, shape, dt, kind="Internal").ap()
    scratch("delta", [GROUPS, L * DH + 1024])
    scratch("drive", [3 * GROUPS, L * DIRS * DH + 2048], BF16)
    scratch("bterm", [TROWS, N_STATE, L], BF16)
    scratch("cmat", [128, L])
    scratch("gate", [BATCH, L, INNER])
    scratch("skip", [BATCH, L, INNER])
    scratch("y", [BATCH, L * HALVES, DIRS * DH])
    scratch("x1", [BATCH, L, CH])
    scratch("x2", [BATCH, L, CH])
    project_and_convolve(nc, d)
    selective_scan(nc, L, d["delta"].unsqueeze(0).broadcast_to((N_STATE, GROUPS, L * DH + 1024)), d["drive"], d["bterm"],
                   d["cmat"], d["a_log"], lambda t: d["y"].rearrange("b x f -> x b f")[bass.ds(t * HALVES, BLK * HALVES)])
    merge_directions(nc, d)
    attend(nc, d)
    experts(nc, d)


def laid_out(a):
    import numpy as np
    f = {k: np.asarray(v) for k, v in a.items()}
    x = f["x"].reshape(BATCH, TOK, CH)
    rows = lambda v: np.broadcast_to(v, (128, v.shape[-1]))
    halves = lambda v: v.reshape(2, 128, *v.shape[1:]).swapaxes(0, 1)
    w_x = np.zeros((INNER, XD_ROWS), np.float32)
    xp = f["L0_conv_w_xproj"]
    for row, lo, n in ((DT_ROW, 0, RANK), (B_ROW, RANK, N_STATE), (C_ROW, RANK + N_STATE, N_STATE)):
        w_x[:, row:row + n] = xp[:, lo:lo + n]
    a_log = np.broadcast_to(f["L0_conv_A_log"].reshape(HALVES, DH, N_STATE).transpose(2, 0, 1)[:, :, None, :],
                            (N_STATE, HALVES, BATCH, DH)).reshape(128, DH)
    w_kv = f["L1_attn_W_kv"].reshape(HEADS, CH, 2, CH)
    out = dict(
        x=x, x_t=x.transpose(0, 2, 1), w_in=f["L0_conv_w_in"], w_x=halves(w_x), w_dt=f["L0_conv_w_dt"],
        b_dt=rows(f["L0_conv_b_dt"]), conv_w=f["L0_conv_conv_w"].reshape(TAPS, 2, 128).transpose(2, 1, 0),
        conv_b=f["L0_conv_conv_b"].reshape(2, 128).T, d_param=rows(f["L0_conv_D_param"]), a_log=a_log,
        w_out=halves(f["L0_conv_w_out"]), ln_w=rows(f["L0_conv_ln_w"]), ln_b=rows(f["L0_conv_ln_b"]),
        w_k=w_kv[:, :, 0].transpose(2, 0, 1).reshape(CH, HEADS * CH),
        w_v=w_kv[:, :, 1].transpose(2, 0, 1).reshape(CH, HEADS * CH), q_t=f["L1_attn_q_proj"].T,
        router_w=f["L1_ffn_router_w"], router_b=rows(f["L1_ffn_router_b"]),
        expert_w=f["L1_ffn_expert_w"].transpose(1, 0, 2).reshape(CH, EXPERTS * CH), expert_b=f["L1_ffn_expert_b"],
        ident=np.eye(128, dtype=np.float32), flip=np.eye(128, dtype=np.float32)[::-1],
        group=np.kron(np.eye(32, dtype=np.float32), np.full((4, 4), 0.25, np.float32)),
        upto=np.triu(np.ones((128, 128), np.float32)), beyond=np.tril(np.ones((128, 128), np.float32), -1),
        iota=np.broadcast_to(np.arange(EXPERTS, dtype=np.float32), (128, EXPERTS)))
    return {k: np.ascontiguousarray(v) for k, v in out.items()}


def kernel(**inputs):
    import concourse.bacc as bacc
    from concourse.bass_utils import run_bass_kernel_spmd

    nc = bacc.Bacc("TRN2", target_bir_lowering=False, num_devices=1)
    arrays, d = {}, {}
    for name, a in laid_out(inputs).items():
        arrays["in_" + name] = a
        d[name] = nc.dram_tensor("in_" + name, a.shape, mybir.dt.from_np(a.dtype), kind="ExternalInput").ap()
    d["out"] = nc.dram_tensor("out_x", [BATCH, TOK, CH], F32, kind="ExternalOutput").ap()
    build(nc, d)
    r = run_bass_kernel_spmd(nc, [arrays], core_ids=[0])
    return r.results[0]["out_x"].reshape(BATCH, IMG, IMG, CH)
```

```python
from contextlib import ExitStack

import concourse.bass as bass
from concourse import mybir

F32=mybir.dt.float32; BF16=mybir.dt.bfloat16
ACT=mybir.ActivationFunctionType; ALU=mybir.AluOpType

N_STATE=16; BATCH=4; HALVES=2; DIRS=4; DH=128
GROUPS=BATCH*HALVES
TERMS=((0,0),(0,1),(0,2),(1,0),(1,1),(2,0))
TROWS=len(TERMS)*GROUPS
BLK=16; RING=4; STEPS=BLK*RING
DECAY_SCALE=2.0**30; DECAY_FLOOR=-200.0
FLOOR_STEPS=(0,2,4,6,8,10,12,14)
EXP_STEPS=(1,3,5,7,9,11,13,15); EXP_PART=BLK//len(EXP_STEPS)
TILES_PE=2; COLS=128//TILES_PE; HRING=8
SUM_AT=(1,0,1); SUM_LAG=(2,3,4)
CHUNK_LO=(0,43,86,DH); NCH=len(CHUNK_LO)-1; CE=43

def selective_scan(nc, L, delta_d, input_d, bterm_d, cmat_d, alog, y_d):
    BODIES=L//STEPS
    HC=DIRS*CE
    with ExitStack() as ctx:
        def sb(name,shape,dt=F32): return ctx.enter_context(nc.sbuf_tensor("ss_"+name,shape,dt))
        def ps(name): return ctx.enter_context(nc.psum_tensor("ss_"+name,[128,512],F32))
        def sem(name): return ctx.enter_context(nc.semaphore("ss_"+name))
        decay=sb("decay",[128,RING,BLK*DH])
        drive=sb("drive",[128,RING,BLK*DIRS*DH],BF16)
        bstream=sb("bstream",[TROWS,N_STATE,STEPS],BF16)
        bdiag=sb("bdiag",[128,RING,BLK,N_STATE,GROUPS],BF16)
        call=sb("call",[128,L])
        DIAG=TILES_PE*COLS+GROUPS
        cdiag=sb("cdiag",[128,2,BLK//TILES_PE*DIAG])
        hcopy=sb("hcopy",[128,NCH,HRING,HC])
        neg_a=sb("neg_a",[128,DH])
        alog_s=sb("alog_s",[128,DH])
        ysb=sb("ysb",[128,2,512])
        bmask=sb("bmask",[TROWS,GROUPS],BF16)
        bm_i=sb("bm_i",[128,GROUPS]); cmask=sb("cmask",[128,GROUPS])
        zero_w=sb("zero_w",[128,128],BF16); zero_x=sb("zero_x",[128,HC],BF16)
        state=[[ps(f"state{c}{i}") for i in range(2)] for c in range(NCH)]
        ybank=[ps(f"y{i}") for i in range(2)]
        delta_in=[sem(f"delta_in{q}") for q in range(RING)]
        drive_in=[sem(f"drive_in{q}") for q in range(RING)]
        b_in=sem("b_in"); c_in=sem("c_in"); a_in=sem("a_in")
        scaled=sem("scaled"); floored=sem("floored"); decay_ready=sem("decay_ready")
        bd_ready=sem("bd_ready"); cd_ready=sem("cd_ready");
        masks=sem("masks"); a_exp=sem("a_exp"); a_clip=sem("a_clip")
        zeroed=sem("zeroed"); drive_zero=sem("drive_zero")
        added=[sem(f"added{c}") for c in range(NCH)]
        decayed=[sem(f"decayed{c}") for c in range(NCH)]
        copied=[sem(f"copied{c}") for c in range(NCH)]
        summed=[sem(f"summed{c}") for c in range(NCH)]
        y_ready=sem("y_ready"); y_out=[sem(f"y_out{i}") for i in range(2)]
        block=ctx.enter_context(nc.Block())

        def width(c): return CHUNK_LO[c+1]-CHUNK_LO[c]
        def of_chunk(x,c):
            return x.rearrange("p (k e) -> p k e",k=DIRS)[:,:,CHUNK_LO[c]:CHUNK_LO[c+1]]
        def flat(x,c): return x[:,0:DIRS*width(c)]
        def split(x,c): return flat(x,c).rearrange("p (k e) -> p k e",k=DIRS)
        def at(i, first, per, c):
            if first:
                return c if c>0 else None
            return i*per + c
        def wait(eng, s, v):
            if v is not None: eng.wait_ge(s, v)

        @block.sync
        def _(sp):
            sp.dma_start(alog_s[:,:],alog).then_inc(a_in,16)
            sp.dma_start(call[:,:],cmat_d).then_inc(c_in,16)
            def body(i, first):
                wait(sp, bd_ready, at(i,first,RING,0))
                sp.dma_start(bstream[:,:,:], bterm_d[:,:,bass.ds(i*STEPS,STEPS)]).then_inc(b_in,16)
                for q in range(RING):
                    if first and q==0: sp.wait_ge(drive_zero,1)
                    wait(sp, decayed[-1], at(i,first,STEPS,(q-RING+1)*BLK))
                    sp.dma_start(decay[:,q,:], delta_d[:, :, bass.ds((i*STEPS+q*BLK)*DH,BLK*DH)]).then_inc(delta_in[q],16)
                    if not first: sp.wait_ge(added[-1], i*STEPS+(q-RING+1)*BLK+2)
                    row=0
                    for parts in (3,2,1):
                        n=parts*GROUPS
                        sp.dma_start(drive[row:row+n,q,:], input_d[0:n, bass.ds((i*STEPS+q*BLK)*DIRS*DH,BLK*DIRS*DH)]).then_inc(drive_in[q],16)
                        row+=n
                    if not first: store_y(i,q-4)
            def store_y(i,q):
                n=q%2
                sp.wait_ge(y_ready, i*RING+q+1)
                y=y_d(i*STEPS+q*BLK).rearrange("(a r) g f -> r a g f",r=TILES_PE)
                for r in range(TILES_PE): sp.dma_start(y[r], ysb[r*COLS:(r+1)*COLS,n,:]).then_inc(y_out[n],16)
            body(0,True)
            with sp.Fori(1,BODIES) as i: body(i,False)
            for q in range(RING-4,RING): store_y(BODIES-1,q)
            for n in range(2): sp.wait_ge(y_out[n], BODIES*RING//2*16*TILES_PE)

        @block.gpsimd
        def _(pool):
            pool.memset(bm_i[:,:],0.0).then_inc(masks,1)
            pool.memset(zero_w[:,:],0.0).then_inc(zeroed,1)
            pool.memset(zero_x[:,:],0.0).then_inc(zeroed,1)
            pool.memset(bdiag[:,:,:,:,:],0.0).then_inc(zeroed,1)
            pool.memset(cdiag[:,:,:],0.0).then_inc(zeroed,1)
            pool.wait_ge(masks,1)
            for m in range(128//GROUPS):
                pool.affine_select(out=bm_i[:,:],in_=bm_i[:,:],compare_op=ALU.not_equal,fill=1.0,base=-GROUPS*m,pattern=[[-1,GROUPS]],channel_multiplier=1).then_inc(masks,1)
                pool.wait_ge(masks,2+m)
            pool.tensor_copy(cmask[:,:],bm_i[:,:]).then_inc(masks,1)
            pool.tensor_copy(bmask[:,:],bm_i[0:TROWS,:]).then_inc(masks,1)
            pool.wait_ge(masks,3+128//GROUPS)
            pool.wait_ge(a_exp,1)
            pool.tensor_scalar(neg_a[:,:],neg_a[:,:],-1.0/DECAY_SCALE,None,ALU.mult).then_inc(a_clip,1)
            pool.wait_ge(a_clip,2)
            pool.wait_ge(zeroed,4)
            pool.wait_ge(c_in,16)
            def body(i, first):
                for q in range(RING):
                    pool.wait_ge(delta_in[q], i*16+16)
                    d=decay[:,q,:].rearrange("p (t d) -> p t d",d=DH)
                    pool.tensor_tensor(d,d,neg_a[:,:].unsqueeze(1).broadcast_to((128,BLK,DH)),ALU.mult).then_inc(scaled,1)
                    if q==0: pool.wait_ge(b_in, i*16+16)
                    if not first: pool.wait_ge(added[-1], i*STEPS+(q-RING+1)*BLK+2)
                    src=bstream[:,:,q*BLK:(q+1)*BLK].rearrange("p n t -> p t n").unsqueeze(3).broadcast_to((TROWS,BLK,N_STATE,GROUPS))
                    m=bmask[:,:].unsqueeze(1).unsqueeze(1).broadcast_to((TROWS,BLK,N_STATE,GROUPS))
                    pool.tensor_tensor(bdiag[0:TROWS,q],src,m,ALU.mult).then_inc(bd_ready,1)
                    wait(pool, summed[-1], at(i,first,STEPS,(q-1)*BLK))
                    cd=cdiag[:,q%2,:].rearrange("p (a x) -> p a x",x=DIAG)[:,:,0:TILES_PE*COLS].rearrange("p a (r x) -> p a r x",r=TILES_PE)[:,:,:,0:GROUPS]
                    c4=call[:,bass.ds(i*STEPS+q*BLK,BLK)].rearrange("p (a r) -> p a r",r=TILES_PE)
                    shape=(128,BLK//TILES_PE,TILES_PE,GROUPS)
                    pool.tensor_tensor(cd, c4.unsqueeze(3).broadcast_to(shape), cmask[:,:].unsqueeze(1).unsqueeze(1).broadcast_to(shape),ALU.mult).then_inc(cd_ready,1)
            body(0,True)
            with pool.Fori(1,BODIES) as i: body(i,False)

        @block.scalar
        def _(act):
            act.wait_ge(a_clip,1)
            act.activation(neg_a[:,:],alog_s[:,:],ACT.Exp).then_inc(a_exp,1)
            def exps(i,q,part):
                n=BLK*DH//len(FLOOR_STEPS); d=decay[:,q%RING,part*n:(part+1)*n]
                act.wait_ge(floored,(i*RING+q)*len(FLOOR_STEPS)+part+1)
                act.activation(d,d,ACT.Exp).then_inc(decay_ready,1)
            def copy(i,first,s,c):
                act.wait_ge(decayed[c], i*STEPS+s+1)
                wait(act, summed[c], at(i,first,STEPS,s-HRING))
                act.activation(flat(hcopy[:,c,(s-1)%HRING,:],c),flat(state[c][(s-1)%2],c),ACT.Copy).then_inc(copied[c],1)
            def evac_y(i,first,q):
                wait(act, summed[-1], at(i,first,STEPS,q*BLK))
                n=(q+1)%2
                k=(i*RING+q-1)
                if not (first and q<=2):
                    act.wait_ge(y_out[n], (i*2+(q-1)//2)*16*TILES_PE)
                act.activation(ysb[:,n,:],ybank[n][:,:],ACT.Copy).then_inc(y_ready,1)
            def body(i,first):
                for s in range(STEPS):
                    q=s//BLK
                    if s%BLK==5 and not (first and q==0):
                        evac_y(i,first,q)
                    if s%BLK in EXP_STEPS and not (first is None and q==RING-1): exps(i,q+1,EXP_STEPS.index(s%BLK))
                    for c in range(NCH):
                        if first and s==0: continue
                        copy(i,first,s,c)
            for part in range(len(EXP_STEPS)): exps(0,0,part)
            body(0,True)
            with act.Fori(1,BODIES-1) as i: body(i,False)
            body(BODIES-1,None)
            for c in range(NCH):
                act.wait_ge(added[c],L+2)
                act.wait_ge(summed[c],L-HRING)
                act.activation(flat(hcopy[:,c,(L-1)%HRING,:],c),flat(state[c][(L-1)%2],c),ACT.Copy).then_inc(copied[c],1)
            evac_y(BODIES-1,None,RING)

        @block.vector
        def _(dve):
            dve.memset(drive[:,:,:],0.0).then_inc(drive_zero,1)
            dve.wait_ge(a_in,16)
            dve.tensor_scalar(alog_s[:,:],alog_s[:,:],88.7,None,ALU.min).then_inc(a_clip,1)
            def floor(i,q,part):
                n=BLK*DH//len(FLOOR_STEPS)
                d=decay[:,q%RING,part*n:(part+1)*n]
                dve.wait_ge(scaled, i*RING+q+1)
                dve.tensor_scalar(d,d,DECAY_FLOOR/DECAY_SCALE,DECAY_SCALE,ALU.max,ALU.mult).then_inc(floored,1)
            def body(i,first):
                for s in range(STEPS):
                    q=s//BLK
                    for c in range(NCH):
                        if s%EXP_PART==0 and c==0: dve.wait_ge(decay_ready, i*(STEPS//EXP_PART)+s//EXP_PART+1)
                        dve.wait_ge(added[c], i*STEPS+s+2)
                        wait(dve, copied[c], at(i,first,STEPS,s-1))
                        a=decay[:,q,(s%BLK)*DH+CHUNK_LO[c]:(s%BLK)*DH+CHUNK_LO[c+1]].unsqueeze(1).broadcast_to((128,DIRS,width(c)))
                        op=dve.tensor_tensor(split(state[c][s%2],c),a,split(state[c][(s-1)%2],c),ALU.mult)
                        op.then_inc(decayed[c],1)
                    if s%BLK in FLOOR_STEPS and not (first is None and q==RING-1):
                        floor(i,q+1,FLOOR_STEPS.index(s%BLK))
            for part in range(len(FLOOR_STEPS)): floor(0,0,part)
            body(0,True)
            with dve.Fori(1,BODIES-1) as i: body(i,False)
            body(BODIES-1,None)

        @block.tensor
        def _(pe):
            pe.wait_ge(zeroed,4)
            for c in range(NCH):
                for j in range(2):
                    pe.matmul(state[c][j][:,0:HC],zero_w[:,:],zero_x[:,:],start=True,stop=True,skip_group_check=True).then_inc(added[c],1)
            def sum_states(i,first,s,c):
                b=s//BLK; t=s%BLK
                wait(pe, copied[c], at(i,first,STEPS,s+1))
                if t==0 and c==0:
                    wait(pe, cd_ready, at(i,first,RING,b+1))
                    wait(pe, y_ready, at(i,first,RING,b-1))
                row=t%TILES_PE*COLS; at0=t//TILES_PE*DIAG+t%TILES_PE*COLS
                pe.matmul(of_chunk(ybank[b%2][row:row+COLS,:],c),cdiag[:,b%2,at0-t//TILES_PE*GROUPS:at0-t//TILES_PE*GROUPS+COLS],split(hcopy[:,c,s%HRING,:],c),start=(t<TILES_PE and c==0),stop=(t>=BLK-TILES_PE),skip_group_check=True).then_inc(summed[c],1)
            def body(i,first):
                for s in range(STEPS):
                    q=s//BLK; t=s%BLK
                    if t==0:
                        pe.wait_ge(drive_in[q], i*48+48)
                        pe.wait_ge(bd_ready, i*RING+q+1)
                    for c in range(NCH):
                        pe.wait_ge(decayed[c], i*STEPS+s+1)
                        mm=pe.matmul(split(state[c][s%2],c),bdiag[:,q,t].rearrange("p n g -> p (n g)"),of_chunk(drive[:,q,t*DIRS*DH:(t+1)*DIRS*DH],c),start=False,stop=True,skip_group_check=True)
                        mm.then_inc(added[c],1)
                        if s%TILES_PE==SUM_AT[c] and not (first and s<SUM_LAG[c]+TILES_PE-1):
                            for n in range(s-SUM_LAG[c]-TILES_PE+1,s-SUM_LAG[c]+1): sum_states(i,first,n,c)
            body(0,True)
            with pe.Fori(1,BODIES) as i: body(i,False)
            for c in range(NCH):
                for s in range((STEPS-SUM_LAG[c])//TILES_PE*TILES_PE,STEPS): sum_states(BODIES-1,None,s,c)
        return None

IMG=64; TOK=IMG*IMG; CH=128; INNER=256; RANK=8; TAPS=9
TILE=128; TILES=TOK//TILE; PART_TILES=4; PARTS=TILES//PART_TILES
CHUNK=512; CHUNKS=TOK//CHUNK
PADW=IMG+2
DT_ROW,B_ROW,C_ROW,XD_ROWS=0,32,64,80
EPS=1e-5
AX=mybir.AxisListType

class Count:
    def __init__(self, sem, per, step=1):
        self.sem, self.per, self.step, self.n = sem, per, step, 0
    def credit(self, eng):
        eng.sem_inc(self.sem, self.per*self.step)
    def at(self, image, n):
        return (image+1)*(self.per*self.step) + n*self.step
    def inc(self, ins):
        ins.then_inc(self.sem, self.step)
        self.n += 1
        return self.n
    def link(self, eng, image, ins):
        eng.wait_ge(self.sem, self.at(image, self.inc(ins)))
    def done(self):
        assert self.n % self.per == 0, (self.n, self.per)

def project_and_convolve(nc, d):
    with ExitStack() as ctx:
        def sb(name,shape,dt=F32): return ctx.enter_context(nc.sbuf_tensor("pc_"+name,shape,dt))
        def ps(name,n=512): return ctx.enter_context(nc.psum_tensor("pc_"+name,[128,n],F32))
        def sem(name): return ctx.enter_context(nc.semaphore("pc_"+name))
        def count(name,per,step=1): return Count(sem(name),per,step)
        w_in=sb("w_in",[CH,2*INNER]); w_x=sb("w_x",[128,2,XD_ROWS]); w_dt=sb("w_dt",[RANK,INNER]); b_dt=sb("b_dt",[128,INNER])
        conv_w=sb("conv_w",[128,2,TAPS]); conv_b=sb("conv_b",[128,2]); tapdiag=sb("tapdiag",[128,TAPS,128])
        d4=sb("d4",[128,INNER]); ident=sb("ident",[128,128]); group=sb("group",[128,128])
        xn=sb("xn",[CH,TOK]); padded=sb("padded",[128,2,PADW*PADW])
        xa=sb("xa",[128,2,TOK]); xr=sb("xr",[128,2,TOK]); xd=sb("xd",[XD_ROWS,TOK])
        bres=sb("bres",[48,2,CHUNK]); bpart=sb("bpart",[48,2,3,CHUNK],BF16)
        stats=sb("stats",[128,CHUNKS,6]); mv=sb("mv",[128,2]); gmv=sb("gmv",[128,2]); dev=sb("dev",[128,1]); var=sb("var",[128,1]); std=sb("std",[128,1]); rstd=sb("rstd",[128,1])
        delta=sb("delta",[128,2,PART_TILES,INNER]); ex=sb("ex",[128,PART_TILES*INNER]); ln=sb("ln",[128,PART_TILES*INNER])
        R=3; LAG=2
        du=sb("du",[128,R,1024]); dp=sb("dp",[128,R,3,1024],BF16)
        gate=sb("gate",[128,2,2,INNER]); skip=sb("skip",[128,2,2,INNER])
        mm=[ps(f"mm{i}") for i in range(2)]; dl=[ps(f"dl{i}") for i in range(2)]; up=[ps(f"up{i}",1024) for i in range(2)]
        IN=(0,CHUNKS); GT=2*CHUNKS; CV=GT+TILES//2; XD=CV+CHUNKS; MM=XD+CHUNKS
        DL=2+TILES//2
        w_ld=sem("w_ld"); setup=sem("setup"); borders=sem("borders"); apart=sem("apart")
        x_in=count("x_in",1,16)
        mm_full=count("mm_full",MM); mm_taken=count("mm_taken",MM)
        dl_full=count("dl_full",DL); dl_taken=count("dl_taken",DL)
        u_full=count("u_full",TILES); u_taken=count("u_taken",TILES)
        norm=count("norm",CHUNKS+5+CHUNKS); std_ready=count("std_ready",1)
        conv=count("conv",2*TAPS); xa0=count("xa0",2); turned=count("turned",2)
        b_lead=count("b_lead",CHUNKS); b_rest=count("b_rest",CHUNKS); b_mid=count("b_mid",CHUNKS); b_last=count("b_last",2*CHUNKS)
        b_out=[count(f"b_out{n}",CHUNKS//2*3,16) for n in range(2)]; c_out=count("c_out",2,16)
        v_steps=count("v_steps",PARTS*5); e_ready=count("e_ready",PARTS); l_ready=count("l_ready",PARTS)
        delta_out=[count(f"delta_out{n}",PARTS,16) for n in range(2)]
        hi=count("hi",TILES); res=count("res",TILES); mid=count("mid",TILES); dp_ready=count("dp_ready",TILES)
        slot_n=[len(range(n,TILES,R)) for n in range(R)]
        dp_out=[count(f"dp_out{n}",slot_n[n],16) for n in range(R)]
        gate_ready=count("gate_ready",TILES//2); gate_out=[count(f"gate_out{n}",TILES//4,16) for n in range(2)]
        skip_ready=count("skip_ready",TILES); skip_out=[count(f"skip_out{n}",TILES//4,16) for n in range(2)]
        block=ctx.enter_context(nc.Block())

        def wait(eng,c,image,n): eng.wait_ge(c.sem,c.at(image,n))
        loads=((w_in[:,:],"w_in"),(w_x[:,:,:],"w_x"),(w_dt[:,:],"w_dt"),(b_dt[:,:],"b_dt"),(conv_w[:,:,:],"conv_w"),(conv_b[:,:],"conv_b"),(d4[:,:],"d_param"),(ident[:,:],"ident"),(group[:,:],"group"))

        def interior(h,k): return padded[:,h,:].rearrange("p (r c) -> p r c",c=PADW)[:,1+8*k:9+8*k,1:1+IMG]
        def shifted(h,row,rows,tap):
            return padded[:,h,:].rearrange("p (r c) -> p r c",c=PADW)[:,row+tap//3:row+tap//3+rows,tap%3:tap%3+IMG]

        @block.sync
        def _(sp):
            for dst,name in loads: sp.dma_start(dst,d[name]).then_inc(w_ld,16)
            for c in (x_in,*b_out,c_out,*delta_out,*dp_out,*skip_out): c.credit(sp)
            bterm=d["bterm"].rearrange("(x b) n l -> b n x l",b=BATCH)
            cmat=d["cmat"].rearrange("(n h b) l -> h b n l",h=2,b=BATCH)
            delta_d=d["delta"].rearrange("(h b) x -> h b x",h=2)
            drive_d=d["drive"].rearrange("(g b) x -> g b x",b=BATCH)
            with sp.Fori(0,BATCH) as b:
                wait(sp,mm_full,b-1,CV)
                x_in.inc(sp.dma_start(xn[:,:], d["x_t"][b]))
                for k in range(CHUNKS):
                    wait(sp,b_last,b,2*(k+1))
                    row=0
                    for i,terms in enumerate((3,2,1)):
                        n=2*terms
                        b_out[k%2].inc(sp.dma_start(bterm[b,:,row:row+n,k*CHUNK:(k+1)*CHUNK], bpart[B_ROW:B_ROW+16,k%2,i,:].unsqueeze(1).broadcast_to((16,n,CHUNK))))
                        row+=n
                wait(sp,mm_taken,b,MM)
                for h in range(2):
                    c_out.inc(sp.dma_start(cmat[h,b], xd[C_ROW:C_ROW+16,:]))
                def store_tile(j):
                    wait(sp,dp_ready,b,j+1)
                    dp_out[j%R].inc(sp.dma_start(drive_d[:,b,j*TILE*512:(j+1)*TILE*512].rearrange("g (t f) -> t g f",t=TILE), dp[:,j%R,:,:].rearrange("p a (h f) -> p (a h) f",h=2)))
                    if j%2==1:
                        n=(j//2)%2
                        wait(sp,skip_ready,b,j+1)
                        skip_out[n].inc(sp.dma_start(d["skip"][b,(j-1)*TILE:(j+1)*TILE].rearrange("(j t) f -> t j f",t=TILE), skip[:,n,:,:]))
                for q in range(PARTS+1):
                    for j in range(max(0,(q-1)*PART_TILES-LAG),q*PART_TILES-LAG): store_tile(j)
                    if q<PARTS:
                        wait(sp,v_steps,b,5*q+5)
                        for h in range(2):
                            delta_out[q%2].inc(sp.dma_start(delta_d[h,b,q*PART_TILES*TILE*DH:(q+1)*PART_TILES*TILE*DH].rearrange("(j t e) -> t j e",t=TILE,e=DH), delta[:,q%2,:,h*DH:(h+1)*DH]))
                for j in range(TILES-LAG,TILES): store_tile(j)
            for c in (*b_out,c_out,*delta_out,*dp_out,*skip_out,*gate_out): wait(sp,c,BATCH-1,c.per)

        @block.gpsimd
        def _(pool):
            pool.memset(padded[:,:,:],0.0).then_inc(borders,1)
            res.credit(pool)
            with pool.Fori(0,BATCH) as b:
                for j in range(TILES):
                    wait(pool,hi,b,j+1)
                    res.inc(pool.tensor_tensor(du[:,j%R,:],du[:,j%R,:],dp[:,j%R,0,:],ALU.subtract))

        @block.scalar
        def _(act):
            for c in (mm_taken,std_ready,xa0,turned,e_ready,l_ready,hi,mid,b_lead,b_mid,gate_ready,*gate_out): c.credit(act)
            act.wait_ge(w_ld,16*len(loads)); act.wait_ge(borders,1)
            with act.Fori(0,BATCH) as b:
                wait(act,norm,b,CHUNKS+4)
                std_ready.inc(act.activation(std[:,:],var[:,:],ACT.Sqrt))
                for h in range(2):
                    if h==0: wait(act,conv,b-1,2*TAPS)
                    for k in range(CHUNKS):
                        wait(act,mm_full,b,IN[h]+k+1)
                        mm_taken.inc(act.activation(interior(h,k),mm[(IN[h]+k)%2][:,:].rearrange("p (r c) -> p r c",c=IMG),ACT.Copy))
                for k in range(TILES//2):
                    wait(act,mm_full,b,GT+k+1)
                    wait(act,gate_out[k%2],b,k//2)
                    mm_taken.inc(act.activation(gate[:,k%2,:,:],mm[(GT+k)%2][:,:].rearrange("p (j f) -> p j f",j=2),ACT.Silu))
                    wait(act,mm_taken,b,GT+k+1)
                    gate_out[k%2].inc(act.dma_start(d["gate"][b,2*k*TILE:(2*k+2)*TILE].rearrange("(j t) f -> t j f",t=TILE), gate[:,k%2,:,:]))
                wait(act,u_full,b-1,TILES)
                for k in range(CHUNKS):
                    wait(act,mm_full,b,CV+k+1)
                    mm_taken.inc(act.activation(xa[:,1,k*CHUNK:(k+1)*CHUNK],mm[(CV+k)%2][:,:],ACT.Silu,bias=conv_b[:,1:2]))
                for k in range(2):
                    wait(act,conv,b,2*TAPS-1+k)
                    s=slice(k*(TOK//2),(k+1)*(TOK//2))
                    xa0.inc(act.activation(xa[:,0,s],xa[:,0,s],ACT.Silu))
                for h in range(2):
                    if h==0: wait(act,xa0,b,2)
                    else: wait(act,mm_taken,b,CV+CHUNKS)
                    turned.inc(act.activation(xr[:,h,:],xa[:,h,::-1],ACT.Copy))
                def b_middle(k):
                    wait(act,b_rest,b,k+1)
                    b_mid.inc(act.activation(bpart[B_ROW:B_ROW+16,k%2,1,:],bres[B_ROW:B_ROW+16,k%2,:],ACT.Copy))
                wait(act,b_rest,b-1,CHUNKS); wait(act,c_out,b-1,2); wait(act,dl_full,b-1,DL)
                for k in range(CHUNKS):
                    wait(act,mm_full,b,XD+k+1)
                    mm_taken.inc(act.activation(xd[:,k*CHUNK:(k+1)*CHUNK],mm[(XD+k)%2][0:XD_ROWS,:],ACT.Copy))
                    wait(act,mm_taken,b,XD+k+1); wait(act,b_out[k%2],b,3*(k//2))
                    b_lead.inc(act.activation(bpart[B_ROW:B_ROW+16,k%2,0,:],xd[B_ROW:B_ROW+16,k*CHUNK:(k+1)*CHUNK],ACT.Copy))
                    if k: b_middle(k-1)
                b_middle(CHUNKS-1)
                def lead(j):
                    wait(act,u_taken,b,j+1)
                    wait(act,dp_out[j%R],b,j//R)
                    hi.inc(act.activation(dp[:,j%R,0,:],du[:,j%R,:],ACT.Copy))
                def middle(j):
                    wait(act,res,b,j+1)
                    mid.inc(act.activation(dp[:,j%R,1,:],du[:,j%R,:],ACT.Copy))
                def parts(j):
                    lead(j)
                    if j: middle(j-1)
                for q in range(PARTS+1):
                    if q<PARTS:
                        wait(act,v_steps,b,5*q+1)
                        e_ready.inc(act.activation(ex[:,:],ex[:,:],ACT.Exp))
                    if q:
                        for j in range((q-1)*PART_TILES,(q-1)*PART_TILES+2): parts(j)
                    if q<PARTS:
                        wait(act,v_steps,b,5*q+3)
                        l_ready.inc(act.activation(ln[:,:],ln[:,:],ACT.Ln))
                    if q:
                        for j in range((q-1)*PART_TILES+2,q*PART_TILES): parts(j)
                middle(TILES-1)

        @block.vector
        def _(dve):
            for c in (norm,dl_taken,conv,b_rest,b_last,v_steps,u_taken,dp_ready,skip_ready): c.credit(dve)
            dve.wait_ge(w_ld,16*len(loads))
            for t in range(TAPS):
                dve.tensor_scalar(tapdiag[:,t,:],ident[:,:],conv_w[:,1,t:t+1],None,ALU.mult).then_inc(setup,1)
            dve.tensor_scalar(d4[:,:],d4[:,:],float(DIRS),None,ALU.mult).then_inc(setup,1)
            dve.wait_ge(setup,TAPS+1)
            with dve.Fori(0,BATCH) as b:
                wait(dve,x_in,b,1)
                for k in range(CHUNKS): norm.inc(dve.bn_stats(stats[:,k,:],xn[:,k*CHUNK:(k+1)*CHUNK]))
                wait(dve,norm,b,CHUNKS)
                dve.sem_inc(apart,1)
                norm.link(dve,b,dve.bn_aggr(mv[:,:],stats[:,:,:]))
                wait(dve,dl_full,b,1)
                dl_taken.link(dve,b,dve.tensor_copy(gmv[:,:],dl[0][:,0:2]))
                norm.link(dve,b,dve.tensor_tensor(dev[:,:],mv[:,0:1],gmv[:,0:1],ALU.subtract))
                norm.link(dve,b,dve.tensor_tensor(dev[:,:],dev[:,:],dev[:,:],ALU.mult))
                wait(dve,dl_full,b,2)
                dl_taken.link(dve,b,dve.tensor_tensor(var[:,:],dl[1][:,0:1],gmv[:,1:2],ALU.add))
                norm.link(dve,b,dve.tensor_scalar(var[:,:],var[:,:],EPS,None,ALU.add))
                wait(dve,std_ready,b,1)
                norm.link(dve,b,dve.reciprocal(rstd[:,:],std[:,:]))
                for k in range(CHUNKS):
                    s=xn[:,k*CHUNK:(k+1)*CHUNK]
                    norm.inc(dve.tensor_scalar(s,s,gmv[:,0:1],rstd[:,0:1],ALU.subtract,ALU.mult))
                wait(dve,u_full,b-1,TILES)
                for t in range(TAPS):
                    for r in range(2):
                        if t==0: wait(dve,mm_taken,b,IN[0]+(CHUNKS//2+1,CHUNKS)[r])
                        else: wait(dve,conv,b,2*t+r-1)
                        out=xa[:,0,r*(TOK//2):(r+1)*(TOK//2)].rearrange("p (r c) -> p r c",c=IMG)
                        src=shifted(0,r*IMG//2,IMG//2,t)
                        if t==0: ins=dve.tensor_scalar(out,src,conv_w[:,0,0:1],conv_b[:,0:1],ALU.mult,ALU.add)
                        else: ins=dve.scalar_tensor_tensor(out=out,in0=src,scalar=conv_w[:,0,t:t+1],in1=out,op0=ALU.mult,op1=ALU.add)
                        conv.inc(ins)
                def b_finish(k):
                    rest=bres[B_ROW:B_ROW+16,k%2,:]
                    wait(dve,b_mid,b,k+1)
                    b_last.link(dve,b,dve.tensor_tensor(rest,rest,bpart[B_ROW:B_ROW+16,k%2,1,:],ALU.subtract))
                    b_last.inc(dve.tensor_copy(bpart[B_ROW:B_ROW+16,k%2,2,:],rest))
                for k in range(CHUNKS):
                    wait(dve,b_lead,b,k+1); wait(dve,b_last,b,2*(k-1))
                    b_rest.inc(dve.tensor_tensor(bres[B_ROW:B_ROW+16,k%2,:],xd[B_ROW:B_ROW+16,k*CHUNK:(k+1)*CHUNK],bpart[B_ROW:B_ROW+16,k%2,0,:],ALU.subtract))
                    if k: b_finish(k-1)
                b_finish(CHUNKS-1)
                def take_tile(j):
                    n=j%R
                    u=up[j%2][:,:].rearrange("p (h k e) -> p h k e",h=2,k=DIRS)
                    wait(dve,u_full,b,j+1)
                    s=(j//2)%2
                    if j%2==0: wait(dve,skip_out[s],b,j//4)
                    skip_ready.inc(dve.tensor_tensor(skip[:,s,j%2,:].rearrange("p (h e) -> p h e",h=2),u[:,:,0,:],d4[:,:].rearrange("p (h e) -> p h e",h=2),ALU.mult))
                    wait(dve,dp_ready,b,j-R+1)
                    dl_=delta[:,(j//PART_TILES)%2,j%PART_TILES,:].rearrange("p (h e) -> p h e",h=2)
                    u_taken.inc(dve.tensor_tensor(du[:,n,:].rearrange("p (h k e) -> p h k e",h=2,k=DIRS),u,dl_.unsqueeze(2).broadcast_to((128,2,DIRS,DH)),ALU.mult))
                def last_part(j):
                    wait(dve,mid,b,j+1)
                    dp_ready.inc(dve.tensor_tensor(dp[:,j%R,2,:],du[:,j%R,:],dp[:,j%R,1,:],ALU.subtract))
                def tiles(js):
                    for j in js:
                        take_tile(j)
                        if j>=LAG: last_part(j-LAG)
                for q in range(PARTS+1):
                    if q<PARTS:
                        dq=delta[:,q%2,:,:]; flat=dq.rearrange("p j f -> p (j f)")
                        wait(dve,delta_out[q%2],b,q//2*2)
                        wait(dve,u_taken,b,(q-1)*PART_TILES)
                        for k in range(2):
                            i=2+2*q+k
                            wait(dve,dl_full,b,i+1)
                            dl_taken.inc(dve.tensor_tensor(dq[:,2*k:2*k+2,:],dl[i%2][:,:].rearrange("p (j f) -> p j f",j=2),b_dt[:,:].unsqueeze(1).broadcast_to((128,2,INNER)),ALU.add))
                        wait(dve,dl_taken,b,2+2*q+2)
                        v_steps.inc(dve.scalar_tensor_tensor(out=ex[:,:],in0=flat,scalar=-1.0,in1=flat,op0=ALU.mult,op1=ALU.min))
                    if q: tiles(range((q-1)*PART_TILES,(q-1)*PART_TILES+2))
                    if q<PARTS:
                        wait(dve,e_ready,b,q+1)
                        v_steps.link(dve,b,dve.tensor_scalar(ln[:,:],ex[:,:],1.0,None,ALU.add))
                        v_steps.inc(dve.scalar_tensor_tensor(out=ex[:,:],in0=ln[:,:],scalar=-1.0,in1=ex[:,:],op0=ALU.add,op1=ALU.subtract))
                    if q: tiles(range((q-1)*PART_TILES+2,q*PART_TILES))
                    if q<PARTS:
                        wait(dve,l_ready,b,q+1)
                        v_steps.link(dve,b,dve.scalar_tensor_tensor(out=ln[:,:],in0=flat,scalar=0.0,in1=ln[:,:],op0=ALU.max,op1=ALU.add))
                        v_steps.link(dve,b,dve.tensor_tensor(flat,ln[:,:],ex[:,:],ALU.subtract))
                for j in range(TILES-LAG,TILES): last_part(j)
                for c in (norm,dl_taken,conv,b_rest,b_last,v_steps,u_taken,dp_ready,skip_ready): c.done()

        @block.tensor
        def _(pe):
            for c in (mm_full,dl_full,u_full): c.credit(pe)
            pe.wait_ge(w_ld,16*len(loads)); pe.wait_ge(setup,TAPS+1)
            with pe.Fori(0,BATCH) as b:
                def bank(n):
                    wait(pe,mm_taken,b,n-1)
                    return mm[n%2]
                wait(pe,norm,b,CHUNKS+1)
                wait(pe,dl_taken,b-1,DL)
                dl_full.inc(pe.matmul(dl[0][:,0:2],group[:,:],mv[:,:],start=True,stop=True))
                wait(pe,norm,b,CHUNKS+3)
                dl_full.inc(pe.matmul(dl[1][:,0:1],group[:,:],dev[:,:],start=True,stop=True))
                for h in range(2):
                    for k in range(CHUNKS):
                        m=bank(IN[h]+k)
                        if h==0: wait(pe,norm,b,CHUNKS+5+k+1)
                        mm_full.inc(pe.matmul(m[:,:],w_in[:,h*128:(h+1)*128],xn[:,k*CHUNK:(k+1)*CHUNK],start=True,stop=True))
                for k in range(TILES//2):
                    m=bank(GT+k)
                    for j in range(2):
                        t=2*k+j
                        ins=pe.matmul(m[:,j*INNER:(j+1)*INNER],xn[:,t*TILE:(t+1)*TILE],w_in[:,INNER:2*INNER],start=True,stop=True)
                    mm_full.inc(ins)
                for k in range(CHUNKS):
                    m=bank(CV+k)
                    wait(pe,mm_taken,b,IN[1]+min(k+2,CHUNKS))
                    for t in range(TAPS):
                        ins=pe.matmul(m[:,:].rearrange("p (r c) -> p r c",c=IMG),tapdiag[:,t,:],shifted(1,8*k,8,t),start=(t==0),stop=(t==TAPS-1))
                    mm_full.inc(ins)
                for k in range(CHUNKS):
                    m=bank(XD+k)
                    wait(pe,xa0,b,k//(CHUNKS//2)+1)
                    for h in range(2):
                        ins=pe.matmul(m[0:XD_ROWS,:],w_x[:,h,:],xa[:,h,k*CHUNK:(k+1)*CHUNK],start=(h==0),stop=(h==1))
                    mm_full.inc(ins)
                def turn_tile(j):
                    wait(pe,u_taken,b,j-1)
                    wait(pe,skip_ready,b,j-1)
                    if j==0: wait(pe,turned,b,2)
                    for h in range(2):
                        for k in range(DIRS):
                            src=(xa,xr)[k//2][:,h,:]
                            out=up[j%2][:,(h*DIRS+k)*DH:(h*DIRS+k+1)*DH]
                            if k%2==0: ins=pe.transpose(out,src[:,j*TILE:(j+1)*TILE],ident[:,:])
                            else:
                                for c in range(2):
                                    ins=pe.matmul(out[c*IMG:(c+1)*IMG,:],src.rearrange("p (r c) -> p c r",c=IMG)[:,2*j+c,:],ident[:,:],start=True,stop=True)
                    u_full.inc(ins)
                for q in range(PARTS+1):
                    if q<PARTS:
                        for k in range(2):
                            i=2+2*q+k
                            wait(pe,dl_taken,b,i-1)
                            t=q*PART_TILES+2*k
                            wait(pe,mm_taken,b,XD+t*TILE//CHUNK+1)
                            for j in range(2):
                                ins=pe.matmul(dl[i%2][:,j*INNER:(j+1)*INNER],xd[0:RANK,(t+j)*TILE:(t+j+1)*TILE],w_dt[:,:],start=True,stop=True)
                            dl_full.inc(ins)
                    if q:
                        for j in range((q-1)*PART_TILES,q*PART_TILES): turn_tile(j)
                for c in (mm_full,dl_full,u_full): c.done()

GTILES=4; GROUP_TOK=GTILES*TILE; NG=TILES//GTILES
HEADS=8; EXPERTS=8
YD_PER=2*HALVES+2*2*HALVES+1

class Phase:
    def __init__(self, nc, ctx, tag): self.nc,self.ctx,self.tag=nc,ctx,tag
    def sb(self,name,shape,dt=F32): return self.ctx.enter_context(self.nc.sbuf_tensor(self.tag+name,shape,dt))
    def ps(self,name,n=512): return self.ctx.enter_context(self.nc.psum_tensor(self.tag+name,[128,n],F32))
    def count(self,name,per,step=1): return Count(self.ctx.enter_context(self.nc.semaphore(self.tag+name)),per,step)
    def sem(self,name): return self.ctx.enter_context(self.nc.semaphore(self.tag+name))

def wait(eng,c,image,n): eng.wait_ge(c.sem,c.at(image,n))

def rsqrt(pool,c,r,b,i,n,mv,rstd,half,eps):
    wait(pool,c,b,3*n*i+2*n)
    r.link(pool,b,pool.tensor_tensor(rstd,mv[:,:,1:2],eps,ALU.add))
    r.inc(pool.tensor_tensor(rstd,rstd,half,ALU.pow))

def normalize(dve,apart,c,r,b,out,src,stats,mv,rstd):
    n=len(src)
    for j in range(n): c.inc(dve.bn_stats(stats[:,j,:],src[j]))
    wait(dve,c,b,c.n)
    dve.sem_inc(apart,1)
    for j in range(n): c.inc(dve.bn_aggr(mv[:,j,:],stats[:,j,:]))
    wait(dve,c,b,c.n)
    wait(dve,r,b,2*(c.n//(3*n)+1))
    for j in range(n):
        c.inc(dve.tensor_scalar(out[j],src[j],mv[:,j,0:1],rstd[:,j,:],ALU.subtract,ALU.mult))

def merge_directions(nc, d):
    with ExitStack() as ctx:
        p=Phase(nc,ctx,"md_"); sb,ps,count=p.sb,p.ps,p.count
        ident=sb("ident",[128,128]); flip=sb("flip",[128,128]); w_out=sb("w_out",[128,2,128]); ln_w=sb("ln_w",[128,INNER]); ln_b=sb("ln_b",[128,INNER])
        ys=sb("ys",[128,2,DIRS,GTILES,INNER]); skip=sb("skip",[128,2,GTILES,INNER]); gate=sb("gate",[128,2,GTILES,INNER]); xin=sb("xin",[128,2,GTILES,CH])
        yn=sb("yn",[128,2,GTILES,INNER]); yt=sb("yt",[128,2,GROUP_TOK]); x1=sb("x1",[128,2,GTILES,CH])
        stats=sb("stats",[128,GTILES,6]); mv=sb("mv",[128,GTILES,2]); std=sb("std",[128,GTILES,1]); rstd=sb("rstd",[128,GTILES,1]); eps=sb("eps",[128,1])
        ybank=[ps(f"y{i}") for i in range(4)]; tbank=ps("tb",1024); obank=[ps(f"o{i}") for i in range(2)]
        w_ld=p.sem("w_ld"); eps_ready=p.sem("eps_ready"); apart=p.sem("apart")
        y_in=[count(f"y_in{q}",NG//2*YD_PER,16) for q in range(2)]
        xg_in=[count(f"xg_in{q}",NG//2*2,16) for q in range(2)]
        paired=count("paired",NG*3); turned_back=count("turned_back",NG*2); summed=count("summed",NG*2)
        normed=count("normed",NG*3*GTILES); std_ready=count("std_ready",NG); rstd_ready=count("rstd_ready",NG); affine=count("affine",NG*3)
        t_full=count("t_full",NG); t_taken=count("t_taken",NG); o_full=count("o_full",NG); o_taken=count("o_taken",NG)
        x1_out=[count(f"x1_out{q}",NG//2,16) for q in range(2)]
        block=ctx.enter_context(nc.Block())
        loads=((ident[:,:],"ident"),(flip[:,:],"flip"),(w_out[:,:,:],"w_out"),(ln_w[:,:],"ln_w"),(ln_b[:,:],"ln_b"))

        @block.sync
        def _(sp):
            for dst,name in loads: sp.dma_start(dst,d[name]).then_inc(w_ld,16)
            for c in (*y_in,*xg_in,*x1_out): c.credit(sp)
            y_d=d["y"].rearrange("(h b) t (k e) -> b k h t e",h=HALVES,k=DIRS)
            def store(b,g):
                wait(sp,o_taken,b,g+1)
                x1_out[g%2].inc(sp.dma_start(d["x1"][b,g*GROUP_TOK:(g+1)*GROUP_TOK].rearrange("(j t) c -> t j c",t=TILE), x1[:,g%2,:,:]))
            def finish(b,g):
                q=g%2; tok=slice(g*GROUP_TOK,(g+1)*GROUP_TOK)
                wait(sp,affine,b,3*(g-1))
                xg_in[q].inc(sp.dma_start(gate[:,q,:,:],d["gate"][b,tok].rearrange("(j t) f -> t j f",t=TILE)))
                wait(sp,o_full,b,g-1)
                xg_in[q].inc(sp.dma_start(xin[:,q,:,:],d["x"][b,tok].rearrange("(j t) f -> t j f",t=TILE)))
                if g>1: store(b,g-2)
            with sp.Fori(0,BATCH) as b:
                for g in range(NG):
                    q=g%2
                    wait(sp,turned_back,b,2*(g-1)); wait(sp,summed,b,2*(g-1))
                    for h in range(HALVES):
                        c=slice(h*DH,(h+1)*DH)
                        for k,first in ((0,g*GTILES),(2,TILES-(g+1)*GTILES)):
                            y_in[q].inc(sp.dma_start(ys[:,q,k,:,c],y_d[b,k,h,first*TILE:(first+GTILES)*TILE].rearrange("(j t) e -> t j e",t=TILE)))
                        for k,first in ((1,g*GTILES),(3,TILES-(g+1)*GTILES)):
                            for r in range(2):
                                y_in[q].inc(sp.dma_start(ys[r*IMG:(r+1)*IMG,q,k,:,c],y_d[b,k,h].rearrange("(c t r) e -> r c t e",r=2,c=IMG)[r,:,first:first+GTILES]))
                    y_in[q].inc(sp.dma_start(skip[:,q,:,:],d["skip"][b,g*GROUP_TOK:(g+1)*GROUP_TOK].rearrange("(j t) f -> t j f",t=TILE)))
                    if g: finish(b,g-1)
                finish(b,NG-1); store(b,NG-2); store(b,NG-1)
            for c in x1_out: wait(sp,c,BATCH-1,c.per)

        @block.gpsimd
        def _(pool):
            affine.credit(pool)
            pool.wait_ge(w_ld,16*len(loads))
            with pool.Fori(0,BATCH) as b:
                for g in range(NG):
                    y=yn[:,g%2,:,:]
                    wait(pool,normed,b,3*GTILES*(g+1))
                    wait(pool,xg_in[g%2],b,(g//2+1)*2)
                    for m in (ln_w,ln_b):
                        affine.link(pool,b,pool.tensor_tensor(y,y,m[:,:].unsqueeze(1).broadcast_to((128,GTILES,INNER)),ALU.mult if m is ln_w else ALU.add))
                    affine.inc(pool.tensor_tensor(y,y,gate[:,g%2,:,:],ALU.mult))

        @block.scalar
        def _(act):
            for c in (std_ready,t_taken,o_taken): c.credit(act)
            act.wait_ge(eps_ready,1)
            with act.Fori(0,BATCH) as b:
                def stds(g):
                    wait(act,normed,b,3*GTILES*g+2*GTILES); wait(act,rstd_ready,b,g)
                    std_ready.inc(act.activation(std[:,:,:],mv[:,:,1:2],ACT.Sqrt,bias=eps[:,:]))
                stds(0)
                for g in range(NG):
                    if g+1<NG: stds(g+1)
                    wait(act,t_full,b,g+1); wait(act,o_full,b,g)
                    t_taken.inc(act.activation(yt[:,:,:].rearrange("p h t -> p (h t)"),tbank[:,:],ACT.Copy))
                    wait(act,o_full,b,g+1); wait(act,x1_out[g%2],b,g//2)
                    o_taken.inc(act.activation(x1[:,g%2,:,:].rearrange("p j c -> p (j c)"),obank[g%2][:,:],ACT.Copy))

        @block.vector
        def _(dve):
            for c in (paired,summed,normed,rstd_ready): c.credit(dve)
            dve.memset(eps[:,:],EPS).then_inc(eps_ready,1)
            with dve.Fori(0,BATCH) as b:
                def pair(g):
                    y=[ys[:,g%2,k,:,:] for k in range(DIRS)]
                    wait(dve,y_in[g%2],b,(g//2+1)*YD_PER)
                    paired.inc(dve.tensor_tensor(y[2],y[2],y[3],ALU.add))
                    paired.link(dve,b,dve.tensor_tensor(y[0],y[0],y[1],ALU.add))
                    paired.inc(dve.tensor_tensor(y[0],y[0],skip[:,g%2,:,:],ALU.add))
                wait(dve,turned_back,b,0)
                pair(0)
                for g in range(NG):
                    y=yn[:,g%2,:,:]
                    wait(dve,t_full,b,g-1); wait(dve,paired,b,3*(g+1))
                    for k in range(2):
                        i=2*g+k
                        wait(dve,turned_back,b,i+1)
                        summed.inc(dve.tensor_tensor(y[:,2*k:2*k+2,:],ybank[i%4][:,:].rearrange("p (j f) -> p j f",j=2),ys[:,g%2,0,2*k:2*k+2,:],ALU.add))
                    wait(dve,summed,b,2*(g+1)); wait(dve,normed,b,3*GTILES*g)
                    for j in range(GTILES): normed.inc(dve.bn_stats(stats[:,j,:],y[:,j,:]))
                    wait(dve,normed,b,normed.n)
                    dve.sem_inc(apart,1)
                    for j in range(GTILES): normed.inc(dve.bn_aggr(mv[:,j,:],stats[:,j,:]))
                    if g+1<NG: pair(g+1)
                    wait(dve,std_ready,b,g+1); wait(dve,normed,b,normed.n)
                    rstd_ready.link(dve,b,dve.reciprocal(rstd[:,:,:],std[:,:,:]))
                    for j in range(GTILES):
                        normed.inc(dve.tensor_scalar(y[:,j,:],y[:,j,:],mv[:,j,0:1],rstd[:,j,:],ALU.subtract,ALU.mult))
                for c in (paired,summed,normed,rstd_ready): c.done()

        @block.tensor
        def _(pe):
            for c in (turned_back,t_full,o_full): c.credit(pe)
            pe.wait_ge(w_ld,16*len(loads))
            with pe.Fori(0,BATCH) as b:
                def turn_back(g):
                    wait(pe,paired,b,3*g+1)
                    for k in range(2):
                        i=2*g+k
                        wait(pe,summed,b,i-3)
                        for j in range(2):
                            ins=pe.matmul(ybank[i%4][:,j*INNER:(j+1)*INNER],flip[:,:],ys[:,g%2,2,GTILES-1-(2*k+j),:],start=True,stop=True)
                        turned_back.inc(ins)
                def project(g):
                    q=g%2
                    wait(pe,affine,b,3*(g+1)); wait(pe,t_taken,b,g)
                    for h in range(2):
                        for j in range(GTILES):
                            ins=pe.transpose(tbank[:,h*512+j*TILE:h*512+(j+1)*TILE],yn[:,q,j,h*128:(h+1)*128],ident[:,:])
                    t_full.inc(ins)
                    wait(pe,t_taken,b,g+1); wait(pe,o_taken,b,g-1)
                    wait(pe,xg_in[q],b,(g//2+1)*2)
                    for j in range(GTILES):
                        out=obank[q][:,j*CH:(j+1)*CH]
                        for h in range(2):
                            pe.matmul(out,yt[:,h,j*TILE:(j+1)*TILE],w_out[:,h,:],start=(h==0),stop=False)
                        ins=pe.matmul(out,ident[:,:],xin[:,q,j,:],start=False,stop=True)
                    o_full.inc(ins)
                turn_back(0)
                for g in range(NG):
                    if g+1<NG: turn_back(g+1)
                    project(g)
                for c in (turned_back,t_full,o_full): c.done()


def attend(nc, d):
    with ExitStack() as ctx:
        p=Phase(nc,ctx,"at_"); sb,ps,count=p.sb,p.ps,p.count
        HW=HEADS*CH
        ident=sb("ident",[128,128]); wk=sb("wk",[128,HW]); wv=sb("wv",[128,HW]); qs=sb("qs",[128,HEADS*(HEADS+1)]); qt=sb("qt",[128,HEADS])
        upto=sb("upto",[128,128]); beyond=sb("beyond",[128,128])
        x1=sb("x1",[128,2,GTILES,CH]); tn=sb("tn",[128,2,GTILES,CH]); tt=sb("tt",[128,2,GROUP_TOK])
        kh=sb("kh",[128,2,512]); s=sb("s",[HEADS,512]); m=sb("m",[HEADS,512]); e=sb("e",[HEADS,2,512]); u=sb("u",[HEADS,512]); r=sb("r",[HEADS,2,512]); last=sb("last",[HEADS,2])
        er=sb("er",[128,2,GTILES*2*HEADS]); v=sb("v",[128,2,HW]); ev=sb("ev",[128,2,HW]); wr=sb("wr",[128,2,HW]); x2=sb("x2",[128,2,GTILES,CH]); mean=sb("mean",[128,2,CH])
        stats=sb("stats",[128,GTILES,6]); mv=sb("mv",[128,GTILES,2]); rstd=sb("rstd",[128,GTILES,1]); half=sb("half",[128,GTILES,1]); eps=sb("eps",[128,GTILES,1])
        kb=[ps(f"kb{i}") for i in range(2)]; vb=ps("vb",1024); wb=ps("wb",1024); tb=ps("tb"); sbk=ps("sb")
        w_ld=p.sem("w_ld"); setup=p.sem("setup")
        x_in=[count(f"x_in{i}",NG//2,16) for i in range(2)]; x_out=[count(f"x_out{i}",NG//2,16) for i in range(2)]
        normed=count("normed",NG*3*GTILES); consts=p.sem("consts"); apart=p.sem("apart"); rstd_ready=count("rstd_ready",NG*2); t_full=count("t_full",NG*2); t_taken=count("t_taken",NG)
        k_full=count("k_full",NG*HEADS); k_taken=count("k_taken",NG*HEADS);
        scan=count("scan",2+NG*8); e_ready=count("e_ready",NG); er_taken=count("er_taken",NG); s_used=count("s_used",NG*HEADS)
        v_full=count("v_full",TILES); v_taken=count("v_taken",TILES); ev_ready=count("ev_ready",TILES)
        w_full=count("w_full",2*TILES); weighed=count("weighed",TILES); reduced=count("reduced",TILES); added=count("added",TILES)
        block=ctx.enter_context(nc.Block())
        loads=((ident[:,:],"ident"),(wk[:,:],"w_k"),(wv[:,:],"w_v"),(qt[:,:],"q_t"),(upto[:,:],"upto"),(beyond[:,:],"beyond"))

        @block.sync
        def _(sp):
            for dst,name in loads: sp.dma_start(dst,d[name]).then_inc(w_ld,16)
            for c in (*x_in,*x_out): c.credit(sp)
            with sp.Fori(0,BATCH) as b:
                def store(g):
                    wait(sp,added,b,(g+1)*GTILES)
                    x_out[g%2].inc(sp.dma_start(d["x2"][b,g*GROUP_TOK:(g+1)*GROUP_TOK].rearrange("(j t) c -> t j c",t=TILE), x2[:,g%2,:,:]))
                for g in range(NG):
                    wait(sp,added,b,(g-1)*GTILES)
                    x_in[g%2].inc(sp.dma_start(x1[:,g%2,:,:],d["x1"][b,g*GROUP_TOK:(g+1)*GROUP_TOK].rearrange("(j t) c -> t j c",t=TILE)))
                    if g>1: store(g-2)
                store(NG-2); store(NG-1)
            for c in x_out: wait(sp,c,BATCH-1,c.per)

        @block.gpsimd
        def _(pool):
            for c in (ev_ready,rstd_ready): c.credit(pool)
            pool.memset(half[:,:,:],-0.5).then_inc(consts,1)
            pool.memset(eps[:,:,:],EPS).then_inc(consts,1)
            pool.wait_ge(consts,2)
            pool.memset(qs[:,:],0.0).then_inc(setup,1)
            pool.wait_ge(w_ld,16*len(loads)); pool.wait_ge(setup,1)
            pool.tensor_copy(qs[:,:].rearrange("p (h x) -> p h x",h=HEADS)[:,:,0],qt[:,:]).then_inc(setup,1)
            with pool.Fori(0,BATCH) as b:
                def rstds(g): rsqrt(pool,normed,rstd_ready,b,g,GTILES,mv,rstd[:,:,:],half[:,:,:],eps[:,:,:])
                rstds(0); rstds(1)
                for j in range(TILES):
                    g=j//GTILES; i=j%GTILES
                    wait(pool,v_taken,b,j+1); wait(pool,er_taken,b,g+1); wait(pool,w_full,b,2*(j-1))
                    ej=er[:,g%2,i*16:i*16+8].unsqueeze(2).broadcast_to((128,HEADS,CH))
                    ev_ready.inc(pool.tensor_tensor(ev[:,j%2,:].rearrange("p (h c) -> p h c",h=HEADS),v[:,j%2,:].rearrange("p (h c) -> p h c",h=HEADS),ej,ALU.mult))
                    if i==GTILES-1 and g+2<NG: rstds(g+2)

        @block.scalar
        def _(act):
            for c in (t_taken,k_taken,e_ready,v_taken): c.credit(act)
            with act.Fori(0,BATCH) as b:
                def turn(g):
                    wait(act,t_full,b,2*g+1); wait(act,v_full,b,(g-1)*GTILES)
                    t_taken.inc(act.activation(tt[:,g%2,:],tb[:,:],ACT.Copy))
                def silu_k(g,h):
                    n=g*HEADS+h
                    wait(act,k_full,b,n+1); wait(act,s_used,b,n-1)
                    k_taken.inc(act.activation(kh[:,n%2,:],kb[n%2][:,:],ACT.Silu))
                def exps(g):
                    wait(act,scan,b,2+8*g+3)
                    e_ready.inc(act.activation(e[:,g%2,:],e[:,g%2,:],ACT.Exp))
                def silu_v(j):
                    wait(act,v_full,b,j+1); wait(act,ev_ready,b,j-1)
                    v_taken.inc(act.activation(v[:,j%2,:],vb[:,:],ACT.Silu))
                turn(0)
                for h in range(HEADS): silu_k(0,h)
                exps(0)
                for g in range(NG):
                    if g+1<NG: turn(g+1)
                    silu_v(g*GTILES)
                    for i in range(GTILES):
                        if i+1<GTILES: silu_v(g*GTILES+i+1)
                        if g+1<NG:
                            silu_k(g+1,2*i); silu_k(g+1,2*i+1)
                    if g+1<NG: exps(g+1)

        @block.vector
        def _(dve):
            for c in (normed,scan,er_taken,weighed,reduced,added): c.credit(dve)
            with dve.Fori(0,BATCH) as b:
                def norm(g):
                    wait(dve,x_in[g%2],b,g//2+1); wait(dve,t_full,b,2*(g-2)+1); wait(dve,normed,b,normed.n)
                    normalize(dve,apart,normed,rstd_ready,b,[tn[:,g%2,j,:] for j in range(GTILES)],[x1[:,g%2,j,:] for j in range(GTILES)],stats,mv,rstd)
                def scans(g):
                    wait(dve,s_used,b,HEADS*(g+1))
                    scan.link(dve,b,dve.tensor_copy(s[:,:],sbk[0:HEADS,:]))
                    scan.link(dve,b,dve.tensor_tensor_scan(m[:,:],s[:,:],s[:,:],last[:,0:1],ALU.max,ALU.max))
                    wait(dve,t_full,b,2*(g-1))
                    scan.link(dve,b,dve.tensor_tensor(e[:,g%2,:],s[:,:],m[:,:],ALU.subtract))
                    scan.inc(dve.tensor_copy(last[:,0:1],m[:,511:512]))
                    wait(dve,e_ready,b,g+1)
                    scan.link(dve,b,dve.tensor_tensor_scan(u[:,:],e[:,g%2,:],e[:,g%2,:],last[:,1:2],ALU.add,ALU.max))
                    scan.link(dve,b,dve.tensor_copy(last[:,1:2],u[:,511:512]))
                    scan.link(dve,b,dve.reciprocal(r[:,g%2,:],u[:,:]))
                    scan.link(dve,b,dve.tensor_scalar(r[:,g%2,:],r[:,g%2,:],1.0/HEADS,None,ALU.mult))
                def take_er(g):
                    wait(dve,t_full,b,2*g+2); wait(dve,weighed,b,(g-1)*GTILES); wait(dve,ev_ready,b,(g-1)*GTILES)
                    er_taken.inc(dve.tensor_copy(er[:,g%2,:],tb[:,0:GTILES*2*HEADS]))
                def weigh(j):
                    g=j//GTILES; i=j%GTILES
                    wait(dve,w_full,b,2*j+1); wait(dve,reduced,b,j-1)
                    if i==0: wait(dve,er_taken,b,g+1)
                    rj=er[:,g%2,i*16+8:i*16+16].unsqueeze(2).broadcast_to((128,HEADS,CH))
                    weighed.inc(dve.tensor_tensor(wr[:,j%2,:].rearrange("p (h c) -> p h c",h=HEADS),wb[:,:].rearrange("p (h c) -> p h c",h=HEADS),rj,ALU.mult))
                def finish(j):
                    g=j//GTILES; i=j%GTILES
                    wait(dve,weighed,b,j+1); wait(dve,added,b,j-1)
                    reduced.inc(dve.tensor_reduce(mean[:,j%2,:],wr[:,j%2,:].rearrange("p (h c) -> p c h",h=HEADS),AX.X,ALU.add))
                    if i==0: wait(dve,x_out[g%2],b,g//2)
                    wait(dve,reduced,b,j+1)
                    added.inc(dve.tensor_tensor(x2[:,g%2,i,:],x1[:,g%2,i,:],mean[:,j%2,:],ALU.add))
                wait(dve,scan,b-1,scan.per)
                scan.link(dve,b,dve.memset(last[:,0:1],-3.0e38))
                scan.link(dve,b,dve.memset(last[:,1:2],0.0))
                norm(0)
                scans(0)
                norm(1)
                for g in range(NG):
                    take_er(g)
                    for i in range(GTILES):
                        j=g*GTILES+i
                        weigh(j)
                        finish(j)
                    if g+1<NG: scans(g+1)
                    if g+2<NG: norm(g+2)
                for c in (normed,scan,er_taken,weighed,reduced,added): c.done()

        @block.tensor
        def _(pe):
            for c in (t_full,k_full,s_used,v_full,w_full): c.credit(pe)
            pe.wait_ge(w_ld,16*len(loads)); pe.wait_ge(setup,2)
            with pe.Fori(0,BATCH) as b:
                def turn(g):
                    wait(pe,normed,b,(g+1)*3*GTILES); wait(pe,er_taken,b,g)
                    for j in range(GTILES): ins=pe.transpose(tb[:,j*TILE:(j+1)*TILE],tn[:,g%2,j,:],ident[:,:])
                    t_full.inc(ins)
                def turn_er(g):
                    wait(pe,t_taken,b,g+1); wait(pe,scan,b,2+8*g+8)
                    for j in range(GTILES):
                        for n,x in enumerate((e,r)):
                            ins=pe.matmul(tb[:,j*16+n*8:j*16+n*8+8],x[:,g%2,j*TILE:(j+1)*TILE],ident[0:HEADS,0:HEADS],start=True,stop=True)
                    t_full.inc(ins)
                def keys(g,h):
                    n=g*HEADS+h
                    if h==0: wait(pe,t_taken,b,g+1)
                    wait(pe,k_taken,b,n-1)
                    k_full.inc(pe.matmul(kb[n%2][:,:],wk[:,h*CH:(h+1)*CH],tt[:,g%2,:],start=True,stop=True))
                def score(g,h):
                    n=g*HEADS+h
                    wait(pe,k_taken,b,n+1)
                    if h==0: wait(pe,scan,b,2+8*(g-1)+1)
                    ins=pe.matmul(sbk[0:HEADS,:],qs[:,h*HEADS:(h+1)*HEADS],kh[:,n%2,:],start=(h==0),stop=(h==HEADS-1))
                    s_used.inc(ins)
                def values(j):
                    g=j//GTILES; i=j%GTILES
                    wait(pe,v_taken,b,j)
                    for n in range(2):
                        ins=pe.matmul(vb[:,n*512:(n+1)*512],tt[:,g%2,i*TILE:(i+1)*TILE],wv[:,n*512:(n+1)*512],start=True,stop=True)
                    v_full.inc(ins)
                def run(j,part):
                    if part==0: wait(pe,ev_ready,b,j+1)
                    wait(pe,weighed,b,j+part)
                    for n in range(2):
                        ins=pe.matmul(wb[:,n*512:(n+1)*512],(upto,beyond)[part][:,:],ev[:,j%2,n*512:(n+1)*512],start=(j==0 and part==0),stop=True,skip_group_check=True)
                    w_full.inc(ins)
                turn(0)
                for h in range(HEADS):
                    keys(0,h)
                    if h: score(0,h-1)
                score(0,HEADS-1)
                for g in range(NG):
                    turn_er(g)
                    if g+1<NG: turn(g+1)
                    values(g*GTILES)
                    for i in range(GTILES):
                        j=g*GTILES+i
                        run(j,0)
                        if i+1<GTILES: values(j+1)
                        if g+1<NG:
                            for h in (2*i,2*i+1):
                                keys(g+1,h)
                                if h: score(g+1,h-1)
                            if i==GTILES-1: score(g+1,HEADS-1)
                        run(j,1)

def experts(nc, d):
    with ExitStack() as ctx:
        p=Phase(nc,ctx,"ex_"); sb,ps,count=p.sb,p.ps,p.count
        EW=EXPERTS*CH
        ident=sb("ident",[128,128]); rw=sb("rw",[128,EXPERTS]); rb=sb("rb",[128,EXPERTS]); ew=sb("ew",[128,EW]); eb=sb("eb",[EXPERTS,CH]); iota=sb("iota",[128,EXPERTS])
        x2=sb("x2",[128,3,GTILES,CH]); tn=sb("tn",[128,2,GTILES,CH]); tt=sb("tt",[128,2,GROUP_TOK])
        lg=sb("lg",[128,GTILES,EXPERTS]); mx=sb("mx",[128,GTILES]); top=sb("top",[128,GTILES,8]); idx=sb("idx",[128,GTILES,8],mybir.dt.uint32); idf=sb("idf",[128,GTILES,8])
        den=sb("den",[128,GTILES,1]); w2=sb("w2",[128,GTILES,2]); wa=sb("wa",[128,GTILES,EXPERTS]); wb2=sb("wb2",[128,GTILES,EXPERTS]); sel=sb("sel",[128,2,GTILES,EXPERTS]); st=sb("st",[EXPERTS,512])
        pr=sb("pr",[128,2,EW]); mo=sb("mo",[128,2,GTILES,CH]); res=sb("res",[128,2,GTILES*CH])
        stats=sb("stats",[128,GTILES,6]); mv=sb("mv",[128,GTILES,2]); rstd=sb("rstd",[128,GTILES,1]); half=sb("half",[128,GTILES,1]); eps=sb("eps",[128,GTILES,1])
        tb=ps("tb"); lb=ps("lb"); wtb=ps("wtb"); bb=ps("bb"); eb_=[ps(f"eb{i}",1024) for i in range(2)]
        w_ld=p.sem("w_ld")
        XS=[len(range(i,NG,3)) for i in range(3)]
        x_in=[count(f"x_in{i}",XS[i],16) for i in range(3)]; x_out=[count(f"x_out{i}",NG//2,16) for i in range(2)]
        normed=count("normed",NG*3*GTILES); consts=p.sem("consts"); apart=p.sem("apart"); rstd_ready=count("rstd_ready",NG*2); t_full=count("t_full",NG); t_taken=count("t_taken",NG); l_full=count("l_full",NG)
        RS=3+2*GTILES+4+2*GTILES+1
        route=count("route",NG*RS); e_ready=count("e_ready",NG)
        wt_full=count("wt_full",NG); wt_taken=count("wt_taken",NG); b_full=count("b_full",NG)
        e_full=count("e_full",TILES); weighed=count("weighed",TILES); reduced=count("reduced",TILES); added=count("added",NG)
        block=ctx.enter_context(nc.Block())
        loads=((ident[:,:],"ident"),(rw[:,:],"router_w"),(rb[:,:],"router_b"),(ew[:,:],"expert_w"),(eb[:,:],"expert_b"),(iota[:,:],"iota"))

        @block.sync
        def _(sp):
            for dst,name in loads: sp.dma_start(dst,d[name]).then_inc(w_ld,16)
            for c in (*x_in,*x_out): c.credit(sp)
            with sp.Fori(0,BATCH) as b:
                def store(g):
                    wait(sp,added,b,g+1)
                    x_out[g%2].inc(sp.dma_start(d["out"][b,g*GROUP_TOK:(g+1)*GROUP_TOK].rearrange("(j t) c -> t j c",t=TILE), res[:,g%2,:].rearrange("p (j c) -> p j c",j=GTILES)))
                for g in range(NG):
                    if g<3:
                        wait(sp,b_full,b,0)
                    else: wait(sp,b_full,b,g-2)
                    x_in[g%3].inc(sp.dma_start(x2[:,g%3,:,:],d["x2"][b,g*GROUP_TOK:(g+1)*GROUP_TOK].rearrange("(j t) c -> t j c",t=TILE)))
                    if g>1: store(g-2)
                store(NG-2); store(NG-1)
            for c in x_out: wait(sp,c,BATCH-1,c.per)

        @block.gpsimd
        def _(pool):
            rstd_ready.credit(pool)
            pool.memset(half[:,:,:],-0.5).then_inc(consts,1)
            pool.memset(eps[:,:,:],EPS).then_inc(consts,1)
            pool.wait_ge(consts,2)
            with pool.Fori(0,BATCH) as b:
                for g in range(NG): rsqrt(pool,normed,rstd_ready,b,g,GTILES,mv,rstd[:,:,:],half[:,:,:],eps[:,:,:])

        @block.scalar
        def _(act):
            for c in (t_taken,e_ready,wt_taken): c.credit(act)
            with act.Fori(0,BATCH) as b:
                def turn(g):
                    wait(act,t_full,b,g+1); wait(act,e_full,b,(g-1)*GTILES)
                    t_taken.inc(act.activation(tt[:,g%2,:],tb[:,:],ACT.Copy))
                def exps(g):
                    wait(act,route,b,RS*g+3)
                    e_ready.inc(act.activation(lg[:,:,:],lg[:,:,:],ACT.Exp))
                turn(0); exps(0)
                for g in range(NG):
                    if g+1<NG: turn(g+1)
                    wait(act,wt_full,b,g+1); wait(act,b_full,b,g)
                    wt_taken.inc(act.activation(st[:,:],wtb[0:EXPERTS,:],ACT.Copy))
                    if g+1<NG: exps(g+1)

        @block.vector
        def _(dve):
            for c in (normed,route,weighed,reduced,added): c.credit(dve)
            dve.wait_ge(w_ld,16*len(loads))
            with dve.Fori(0,BATCH) as b:
                def norm(g):
                    wait(dve,x_in[g%3],b,g//3+1); wait(dve,t_full,b,g-1); wait(dve,normed,b,normed.n)
                    normalize(dve,apart,normed,rstd_ready,b,[tn[:,g%2,j,:] for j in range(GTILES)],[x2[:,g%3,j,:] for j in range(GTILES)],stats,mv,rstd)
                def link(ins): route.link(dve,b,ins)
                def weights(g):
                    wait(dve,l_full,b,g+1)
                    link(dve.tensor_tensor(lg[:,:,:],lb[:,0:GTILES*EXPERTS].rearrange("p (j e) -> p j e",j=GTILES),rb[:,:].unsqueeze(1).broadcast_to((128,GTILES,EXPERTS)),ALU.add))
                    link(dve.tensor_reduce(mx[:,:],lg[:,:,:],AX.X,ALU.max))
                    link(dve.tensor_tensor(lg[:,:,:],lg[:,:,:],mx[:,:].unsqueeze(2).broadcast_to((128,GTILES,EXPERTS)),ALU.subtract))
                    wait(dve,e_ready,b,g+1)
                    dve.sem_inc(apart,1)
                    for j in range(GTILES): route.inc(dve.max(top[:,j,:],lg[:,j,:]))
                    wait(dve,route,b,route.n)
                    dve.sem_inc(apart,1)
                    for j in range(GTILES): route.inc(dve.max_index(idx[:,j,:],top[:,j,:],lg[:,j,:]))
                    link(dve.tensor_tensor(den[:,:,:],top[:,:,0:1],top[:,:,1:2],ALU.add))
                    link(dve.reciprocal(den[:,:,:],den[:,:,:]))
                    link(dve.tensor_tensor(w2[:,:,:],top[:,:,0:2],den[:,:,:].broadcast_to((128,GTILES,2)),ALU.mult))
                    link(dve.tensor_copy(idf[:,:,:],idx[:,:,:]))
                    for j in range(GTILES):
                        for n,w in enumerate((wa,wb2)):
                            route.inc(dve.tensor_scalar(w[:,j,:],iota[:,:],idf[:,j,n:n+1],w2[:,j,n:n+1],ALU.is_equal,ALU.mult))
                    wait(dve,route,b,route.n)
                    wait(dve,wt_full,b,g-1); wait(dve,weighed,b,(g-1)*GTILES)
                    link(dve.tensor_tensor(sel[:,g%2,:,:],wa[:,:,:],wb2[:,:,:],ALU.add))
                def mix(j):
                    g=j//GTILES; i=j%GTILES
                    wait(dve,e_full,b,j+1); wait(dve,reduced,b,j-1)
                    weighed.inc(dve.tensor_tensor(pr[:,j%2,:].rearrange("p (e c) -> p e c",e=EXPERTS),eb_[j%2][:,:].rearrange("p (e c) -> p e c",e=EXPERTS),sel[:,g%2,i,:].unsqueeze(2).broadcast_to((128,EXPERTS,CH)),ALU.mult))
                def fold(j):
                    g=j//GTILES; i=j%GTILES
                    wait(dve,weighed,b,j+1)
                    if i==0: wait(dve,added,b,g-1)
                    reduced.inc(dve.tensor_reduce(mo[:,g%2,i,:],pr[:,j%2,:].rearrange("p (e c) -> p c e",e=EXPERTS),AX.X,ALU.add))
                norm(0); norm(1); weights(0)
                for g in range(NG):
                    for i in range(GTILES):
                        mix(g*GTILES+i)
                        if i: fold(g*GTILES+i-1)
                    fold((g+1)*GTILES-1)
                    if g+2<NG: norm(g+2)
                    if g+1<NG: weights(g+1)
                    wait(dve,b_full,b,g+1); wait(dve,reduced,b,(g+1)*GTILES); wait(dve,x_out[g%2],b,g//2)
                    added.inc(dve.tensor_tensor(res[:,g%2,:],mo[:,g%2,:,:].rearrange("p j c -> p (j c)"),bb[:,:],ALU.add))
                for c in (normed,route,weighed,reduced,added): c.done()

        @block.tensor
        def _(pe):
            for c in (t_full,l_full,e_full,wt_full,b_full): c.credit(pe)
            pe.wait_ge(w_ld,16*len(loads))
            with pe.Fori(0,BATCH) as b:
                def turn(g):
                    wait(pe,normed,b,(g+1)*3*GTILES); wait(pe,t_taken,b,g)
                    for j in range(GTILES): ins=pe.transpose(tb[:,j*TILE:(j+1)*TILE],tn[:,g%2,j,:],ident[:,:])
                    t_full.inc(ins)
                def logits(g):
                    wait(pe,t_taken,b,g+1); wait(pe,route,b,RS*(g-1)+1)
                    for j in range(GTILES): ins=pe.matmul(lb[:,j*EXPERTS:(j+1)*EXPERTS],tt[:,g%2,j*TILE:(j+1)*TILE],rw[:,:],start=True,stop=True)
                    l_full.inc(ins)
                def project(j):
                    g=j//GTILES; i=j%GTILES
                    wait(pe,weighed,b,j-1)
                    for n in range(2):
                        ins=pe.matmul(eb_[j%2][:,n*512:(n+1)*512],tt[:,g%2,i*TILE:(i+1)*TILE],ew[:,n*512:(n+1)*512],start=True,stop=True)
                    e_full.inc(ins)
                def biases(g):
                    wait(pe,route,b,RS*(g+1)); wait(pe,wt_taken,b,g)
                    for j in range(GTILES): ins=pe.matmul(wtb[0:EXPERTS,j*TILE:(j+1)*TILE],sel[:,g%2,j,:],ident[:,:],start=True,stop=True)
                    wt_full.inc(ins)
                    wait(pe,wt_taken,b,g+1); wait(pe,added,b,g)
                    for j in range(GTILES):
                        pe.matmul(bb[:,j*CH:(j+1)*CH],st[:,j*TILE:(j+1)*TILE],eb[:,:],start=True,stop=False)
                        ins=pe.matmul(bb[:,j*CH:(j+1)*CH],ident[:,:],x2[:,g%3,j,:],start=False,stop=True)
                    b_full.inc(ins)
                turn(0); logits(0)
                for g in range(NG):
                    for i in range(GTILES):
                        project(g*GTILES+i)
                        if i==1 and g+1<NG: turn(g+1)
                    biases(g)
                    if g+1<NG: logits(g+1)
                for c in (t_full,l_full,e_full,wt_full,b_full): c.done()



def build(nc, d):
    L = TOK
    def scratch(name, shape, dt=F32):
        d[name] = nc.dram_tensor("scratch_" + name, shape, dt, kind="Internal").ap()
    scratch("delta", [GROUPS, L * DH + 1024])
    scratch("drive", [3 * GROUPS, L * DIRS * DH + 2048], BF16)
    scratch("bterm", [TROWS, N_STATE, L], BF16)
    scratch("cmat", [128, L])
    scratch("gate", [BATCH, L, INNER])
    scratch("skip", [BATCH, L, INNER])
    scratch("y", [GROUPS, L, DIRS * DH])
    scratch("x1", [BATCH, L, CH])
    scratch("x2", [BATCH, L, CH])
    project_and_convolve(nc, d)
    selective_scan(nc, L, d["delta"].unsqueeze(0).broadcast_to((N_STATE, GROUPS, L * DH + 1024)), d["drive"], d["bterm"],
                   d["cmat"], d["a_log"], lambda t: d["y"].rearrange("g l f -> l g f")[bass.ds(t, BLK)])
    merge_directions(nc, d)
    attend(nc, d)
    experts(nc, d)


def laid_out(a):
    import numpy as np
    f = {k: np.asarray(v) for k, v in a.items()}
    x = f["x"].reshape(BATCH, TOK, CH)
    rows = lambda v: np.broadcast_to(v, (128, v.shape[-1]))
    halves = lambda v: v.reshape(2, 128, *v.shape[1:]).swapaxes(0, 1)
    w_x = np.zeros((INNER, XD_ROWS), np.float32)
    xp = f["L0_conv_w_xproj"]
    for row, lo, n in ((DT_ROW, 0, RANK), (B_ROW, RANK, N_STATE), (C_ROW, RANK + N_STATE, N_STATE)):
        w_x[:, row:row + n] = xp[:, lo:lo + n]
    a_log = np.broadcast_to(f["L0_conv_A_log"].reshape(HALVES, DH, N_STATE).transpose(2, 0, 1)[:, :, None, :],
                            (N_STATE, HALVES, BATCH, DH)).reshape(128, DH)
    w_kv = f["L1_attn_W_kv"].reshape(HEADS, CH, 2, CH)
    out = dict(
        x=x, x_t=x.transpose(0, 2, 1), w_in=f["L0_conv_w_in"], w_x=halves(w_x), w_dt=f["L0_conv_w_dt"],
        b_dt=rows(f["L0_conv_b_dt"]), conv_w=f["L0_conv_conv_w"].reshape(TAPS, 2, 128).transpose(2, 1, 0),
        conv_b=f["L0_conv_conv_b"].reshape(2, 128).T, d_param=rows(f["L0_conv_D_param"]), a_log=a_log,
        w_out=halves(f["L0_conv_w_out"]), ln_w=rows(f["L0_conv_ln_w"]), ln_b=rows(f["L0_conv_ln_b"]),
        w_k=w_kv[:, :, 0].transpose(2, 0, 1).reshape(CH, HEADS * CH),
        w_v=w_kv[:, :, 1].transpose(2, 0, 1).reshape(CH, HEADS * CH), q_t=f["L1_attn_q_proj"].T,
        router_w=f["L1_ffn_router_w"], router_b=rows(f["L1_ffn_router_b"]),
        expert_w=f["L1_ffn_expert_w"].transpose(1, 0, 2).reshape(CH, EXPERTS * CH), expert_b=f["L1_ffn_expert_b"],
        ident=np.eye(128, dtype=np.float32), flip=np.eye(128, dtype=np.float32)[::-1],
        group=np.kron(np.eye(32, dtype=np.float32), np.full((4, 4), 0.25, np.float32)),
        upto=np.triu(np.ones((128, 128), np.float32)), beyond=np.tril(np.ones((128, 128), np.float32), -1),
        iota=np.broadcast_to(np.arange(EXPERTS, dtype=np.float32), (128, EXPERTS)))
    return {k: np.ascontiguousarray(v) for k, v in out.items()}


def kernel(**inputs):
    import concourse.bacc as bacc
    from concourse.bass_utils import run_bass_kernel_spmd

    nc = bacc.Bacc("TRN2", target_bir_lowering=False, num_devices=1)
    arrays, d = {}, {}
    for name, a in laid_out(inputs).items():
        arrays["in_" + name] = a
        d[name] = nc.dram_tensor("in_" + name, a.shape, mybir.dt.from_np(a.dtype), kind="ExternalInput").ap()
    d["out"] = nc.dram_tensor("out_x", [BATCH, TOK, CH], F32, kind="ExternalOutput").ap()
    build(nc, d)
    r = run_bass_kernel_spmd(nc, [arrays], core_ids=[0])
    return r.results[0]["out_x"].reshape(BATCH, IMG, IMG, CH)
```

```python
from contextlib import ExitStack

import concourse.bass as bass
from concourse import mybir

F32=mybir.dt.float32
BF16=mybir.dt.bfloat16
ACT=mybir.ActivationFunctionType
ALU=mybir.AluOpType

N_STATE=16
BATCH=4
HALVES=2
DIRS=4
DH=128
GROUPS=BATCH*HALVES
TERMS=((0, 0), (0, 1), (0, 2), (1, 0), (1, 1), (2, 0))
TROWS=len(TERMS)*GROUPS
BLK=16
RING=4
STEPS=BLK*RING
DECAY_SCALE=2.0**30
DECAY_FLOOR=-200.0
FLOOR_STEPS=(0, 2, 4, 6, 8, 10, 12, 14)
EXP_STEPS=(1, 3, 5, 7, 9, 11, 13, 15)
EXP_PART=BLK//len(EXP_STEPS)
TILES_PE=2
COLS=128//TILES_PE
HRING=8
SUM_AT=(1, 0, 1)
SUM_LAG=(2, 3, 4)
CHUNK_LO=(0, 43, 86, DH)
NCH=len(CHUNK_LO)-1
CE=43

def selective_scan(nc, L, delta_d, input_d, bterm_d, cmat_d, alog, mask_d, y_d):
    BODIES=L//STEPS
    HC=DIRS*CE
    with ExitStack() as ctx:
        def sb(name, shape, dt=F32): return ctx.enter_context(nc.sbuf_tensor("ss_"+name, shape, dt))
        def ps(name): return ctx.enter_context(nc.psum_tensor("ss_"+name, [128, 512], F32))
        def sem(name): return ctx.enter_context(nc.semaphore("ss_"+name))
        decay=sb("decay", [128, RING, BLK*DH])
        drive=sb("drive", [128, RING, BLK*DIRS*DH], BF16)
        bstream=sb("bstream", [TROWS, N_STATE, STEPS], BF16)
        bdiag=sb("bdiag", [128, RING, BLK, N_STATE, GROUPS], BF16)
        call=sb("call", [128, L])
        DIAG=TILES_PE*COLS+GROUPS
        cdiag=sb("cdiag", [128, 2, BLK//TILES_PE*DIAG])
        hcopy=sb("hcopy", [128, NCH, HRING, HC])
        neg_a=sb("neg_a", [128, DH])
        alog_s=sb("alog_s", [128, DH])
        ysb=sb("ysb", [128, 2, 512])
        bmask=sb("bmask", [TROWS, GROUPS], BF16)
        cmask=sb("cmask", [128, GROUPS])
        zero_w=sb("zero_w", [128, 128], BF16)
        zero_x=sb("zero_x", [128, HC], BF16)
        state=[[ps(f"state{c}{i}") for i in range(2)] for c in range(NCH)]
        ybank=[ps(f"y{i}") for i in range(2)]
        delta_in=[sem(f"delta_in{q}") for q in range(RING)]
        drive_in=[sem(f"drive_in{q}") for q in range(RING)]
        b_in=sem("b_in")
        c_in=sem("c_in")
        a_in=sem("a_in")
        scaled=sem("scaled")
        floored=sem("floored")
        decay_ready=sem("decay_ready")
        bd_ready=sem("bd_ready")
        cd_ready=sem("cd_ready")
        mask_in=sem("mask_in")
        bmask_ready=sem("bmask_ready")
        a_exp=sem("a_exp")
        a_clip=sem("a_clip")
        zeroed=sem("zeroed")
        drive_zero=sem("drive_zero")
        added=[sem(f"added{c}") for c in range(NCH)]
        decayed=[sem(f"decayed{c}") for c in range(NCH)]
        copied=[sem(f"copied{c}") for c in range(NCH)]
        summed=[sem(f"summed{c}") for c in range(NCH)]
        y_ready=sem("y_ready")
        y_out=[sem(f"y_out{i}") for i in range(2)]
        block=ctx.enter_context(nc.Block())

        def width(c): return CHUNK_LO[c+1]-CHUNK_LO[c]
        def of_chunk(x, c):
            return x.rearrange("p (k e) -> p k e", k=DIRS)[:, :, CHUNK_LO[c]:CHUNK_LO[c+1]]
        def flat(x, c): return x[:, 0:DIRS*width(c)]
        def split(x, c): return flat(x, c).rearrange("p (k e) -> p k e", k=DIRS)
        def at(i, first, per, c):
            if first:
                return c if c>0 else None
            return i*per + c
        def wait(eng, s, v):
            if v is not None: eng.wait_ge(s, v)

        @block.sync
        def _(sp):
            sp.dma_start(alog_s[:, :], alog).then_inc(a_in, 16)
            sp.dma_start(cmask[:, :], mask_d).then_inc(mask_in, 16)
            sp.dma_start(call[:, :], cmat_d).then_inc(c_in, 16)
            def body(i, first):
                wait(sp, bd_ready, at(i, first, RING, 0))
                sp.dma_start(bstream[:, :, :], bterm_d[:, :, bass.ds(i*STEPS, STEPS)]).then_inc(b_in, 16)
                for q in range(RING):
                    wait(sp, decayed[-1], at(i, first, STEPS, (q-RING+1)*BLK))
                    sp.dma_start(decay[:, q, :], delta_d[:, :, bass.ds((i*STEPS+q*BLK)*DH, BLK*DH)]).then_inc(delta_in[q], 16)
                    if first: sp.wait_ge(drive_zero, q+1)
                    if not first: sp.wait_ge(added[-1], i*STEPS+(q-RING+1)*BLK+2)
                    row=0
                    for parts in (3, 2, 1):
                        n=parts*GROUPS
                        sp.dma_start(drive[row:row+n, q, :], input_d[0:n, bass.ds((i*STEPS+q*BLK)*DIRS*DH, BLK*DIRS*DH)]).then_inc(drive_in[q], 16)
                        row+=n
                    if not first: store_y(i, q-4)
            def store_y(i, q):
                n=q%2
                sp.wait_ge(y_ready, i*RING+q+1)
                y=y_d(i*STEPS+q*BLK).rearrange("(a r) g f -> r a g f", r=TILES_PE)
                for r in range(TILES_PE): sp.dma_start(y[r], ysb[r*COLS:(r+1)*COLS, n, :]).then_inc(y_out[n], 16)
            body(0, True)
            with sp.Fori(1, BODIES) as i: body(i, False)
            for q in range(RING-4, RING): store_y(BODIES-1, q)
            for n in range(2): sp.wait_ge(y_out[n], BODIES*RING//2*16*TILES_PE)

        @block.gpsimd
        def _(pool):
            pool.memset(zero_w[:, :], 0.0).then_inc(zeroed, 1)
            pool.memset(zero_x[:, :], 0.0).then_inc(zeroed, 1)
            pool.memset(bdiag[:, :, :, :, :], 0.0).then_inc(zeroed, 1)
            pool.memset(cdiag[:, :, :], 0.0).then_inc(zeroed, 1)
            pool.wait_ge(mask_in, 16)
            pool.tensor_copy(bmask[:, :], cmask[0:TROWS, :]).then_inc(bmask_ready, 1)
            pool.wait_ge(bmask_ready, 1)
            pool.wait_ge(a_exp, 1)
            pool.tensor_scalar(neg_a[:, :], neg_a[:, :], -1.0/DECAY_SCALE, None, ALU.mult).then_inc(a_clip, 1)
            pool.wait_ge(a_clip, 2)
            pool.wait_ge(zeroed, 4)
            pool.wait_ge(c_in, 16)
            def body(i, first):
                for q in range(RING):
                    pool.wait_ge(delta_in[q], i*16+16)
                    d=decay[:, q, :].rearrange("p (t d) -> p t d", d=DH)
                    pool.tensor_tensor(d, d, neg_a[:, :].unsqueeze(1).broadcast_to((128, BLK, DH)), ALU.mult).then_inc(scaled, 1)
                    if q==0: pool.wait_ge(b_in, i*16+16)
                    if not first: pool.wait_ge(added[-1], i*STEPS+(q-RING+1)*BLK+2)
                    src=bstream[:, :, q*BLK:(q+1)*BLK].rearrange("p n t -> p t n").unsqueeze(3).broadcast_to((TROWS, BLK, N_STATE, GROUPS))
                    m=bmask[:, :].unsqueeze(1).unsqueeze(1).broadcast_to((TROWS, BLK, N_STATE, GROUPS))
                    pool.tensor_tensor(bdiag[0:TROWS, q], src, m, ALU.mult).then_inc(bd_ready, 1)
                    wait(pool, summed[-1], at(i, first, STEPS, (q-1)*BLK))
                    cd=cdiag[:, q%2, :].rearrange("p (a x) -> p a x", x=DIAG)[:, :, 0:TILES_PE*COLS].rearrange("p a (r x) -> p a r x", r=TILES_PE)[:, :, :, 0:GROUPS]
                    c4=call[:, bass.ds(i*STEPS+q*BLK, BLK)].rearrange("p (a r) -> p a r", r=TILES_PE)
                    shape=(128, BLK//TILES_PE, TILES_PE, GROUPS)
                    pool.tensor_tensor(cd, c4.unsqueeze(3).broadcast_to(shape), cmask[:, :].unsqueeze(1).unsqueeze(1).broadcast_to(shape), ALU.mult).then_inc(cd_ready, 1)
            body(0, True)
            with pool.Fori(1, BODIES) as i: body(i, False)

        @block.scalar
        def _(act):
            act.wait_ge(a_clip, 1)
            act.activation(neg_a[:, :], alog_s[:, :], ACT.Exp).then_inc(a_exp, 1)
            def exps(i, q, part):
                n=BLK*DH//len(FLOOR_STEPS)
                d=decay[:, q%RING, part*n:(part+1)*n]
                act.wait_ge(floored, (i*RING+q)*len(FLOOR_STEPS)+part+1)
                act.activation(d, d, ACT.Exp).then_inc(decay_ready, 1)
            def copy(i, first, s, c):
                act.wait_ge(decayed[c], i*STEPS+s+1)
                wait(act, summed[c], at(i, first, STEPS, s-HRING))
                act.activation(flat(hcopy[:, c, (s-1)%HRING, :], c), flat(state[c][(s-1)%2], c), ACT.Copy).then_inc(copied[c], 1)
            def evac_y(i, first, q):
                wait(act, summed[-1], at(i, first, STEPS, q*BLK))
                n=(q+1)%2
                k=(i*RING+q-1)
                if not (first and q<=2):
                    act.wait_ge(y_out[n], (i*2+(q-1)//2)*16*TILES_PE)
                act.activation(ysb[:, n, :], ybank[n][:, :], ACT.Copy).then_inc(y_ready, 1)
            def body(i, first):
                for s in range(STEPS):
                    q=s//BLK
                    if s%BLK==6 and not (first and q==0):
                        evac_y(i, first, q)
                    if s%BLK in EXP_STEPS and not (first is None and q==RING-1): exps(i, q+1, EXP_STEPS.index(s%BLK))
                    for c in range(NCH):
                        if first and s==0: continue
                        copy(i, first, s, c)
            for part in range(len(EXP_STEPS)): exps(0, 0, part)
            body(0, True)
            with act.Fori(1, BODIES-1) as i: body(i, False)
            body(BODIES-1, None)
            for c in range(NCH):
                act.wait_ge(added[c], L+2)
                act.wait_ge(summed[c], L-HRING)
                act.activation(flat(hcopy[:, c, (L-1)%HRING, :], c), flat(state[c][(L-1)%2], c), ACT.Copy).then_inc(copied[c], 1)
            evac_y(BODIES-1, None, RING)

        @block.vector
        def _(dve):
            dve.wait_ge(a_in, 16)
            dve.tensor_scalar(alog_s[:, :], alog_s[:, :], 88.7, None, ALU.min).then_inc(a_clip, 1)
            for q in range(RING): dve.memset(drive[:, q, :], 0.0).then_inc(drive_zero, 1)
            def floor(i, q, part):
                n=BLK*DH//len(FLOOR_STEPS)
                d=decay[:, q%RING, part*n:(part+1)*n]
                dve.wait_ge(scaled, i*RING+q+1)
                dve.tensor_scalar(d, d, DECAY_FLOOR/DECAY_SCALE, DECAY_SCALE, ALU.max, ALU.mult).then_inc(floored, 1)
            def body(i, first):
                for s in range(STEPS):
                    q=s//BLK
                    for c in range(NCH):
                        if s%EXP_PART==0 and c==0: dve.wait_ge(decay_ready, i*(STEPS//EXP_PART)+s//EXP_PART+1)
                        dve.wait_ge(added[c], i*STEPS+s+2)
                        wait(dve, copied[c], at(i, first, STEPS, s-1))
                        a=decay[:, q, (s%BLK)*DH+CHUNK_LO[c]:(s%BLK)*DH+CHUNK_LO[c+1]].unsqueeze(1).broadcast_to((128, DIRS, width(c)))
                        op=dve.tensor_tensor(split(state[c][s%2], c), a, split(state[c][(s-1)%2], c), ALU.mult)
                        op.then_inc(decayed[c], 1)
                    if s%BLK in FLOOR_STEPS and not (first is None and q==RING-1):
                        floor(i, q+1, FLOOR_STEPS.index(s%BLK))
            for part in range(len(FLOOR_STEPS)): floor(0, 0, part)
            body(0, True)
            with dve.Fori(1, BODIES-1) as i: body(i, False)
            body(BODIES-1, None)

        @block.tensor
        def _(pe):
            pe.wait_ge(zeroed, 4)
            for c in range(NCH):
                for j in range(2):
                    pe.matmul(state[c][j][:, 0:HC], zero_w[:, :], zero_x[:, :], start=True, stop=True, skip_group_check=True).then_inc(added[c], 1)
            def sum_states(i, first, s, c):
                b=s//BLK
                t=s%BLK
                wait(pe, copied[c], at(i, first, STEPS, s+1))
                if t==0 and c==0:
                    wait(pe, cd_ready, at(i, first, RING, b+1))
                    wait(pe, y_ready, at(i, first, RING, b-1))
                row=t%TILES_PE*COLS
                pe.matmul(of_chunk(ybank[b%2][row:row+COLS, :], c), cdiag[:, b%2, t*COLS:(t+1)*COLS], split(hcopy[:, c, s%HRING, :], c), start=(t<TILES_PE and c==0), stop=(t>=BLK-TILES_PE), skip_group_check=True).then_inc(summed[c], 1)
            def body(i, first):
                for s in range(STEPS):
                    q=s//BLK
                    t=s%BLK
                    if t==0:
                        pe.wait_ge(drive_in[q], i*48+48)
                        pe.wait_ge(bd_ready, i*RING+q+1)
                    for c in range(NCH):
                        pe.wait_ge(decayed[c], i*STEPS+s+1)
                        mm=pe.matmul(split(state[c][s%2], c), bdiag[:, q, t].rearrange("p n g -> p (n g)"), of_chunk(drive[:, q, t*DIRS*DH:(t+1)*DIRS*DH], c), start=False, stop=True, skip_group_check=True)
                        mm.then_inc(added[c], 1)
                        if s%TILES_PE==SUM_AT[c] and not (first and s<SUM_LAG[c]+TILES_PE-1):
                            for n in range(s-SUM_LAG[c]-TILES_PE+1, s-SUM_LAG[c]+1): sum_states(i, first, n, c)
            body(0, True)
            with pe.Fori(1, BODIES) as i: body(i, False)
            for c in range(NCH):
                for s in range((STEPS-SUM_LAG[c])//TILES_PE*TILES_PE, STEPS): sum_states(BODIES-1, None, s, c)

IMG=64
TOK=IMG*IMG
CH=128
INNER=256
RANK=8
TAPS=9
TILE=128
TILES=TOK//TILE
PART_TILES=4
PARTS=TILES//PART_TILES
CHUNK=512
CHUNKS=TOK//CHUNK
PADW=IMG+2
DT_ROW, B_ROW, C_ROW, XD_ROWS=0, 32, 64, 80
EPS=1e-5
AX=mybir.AxisListType

class Count:
    def __init__(self, sem, per, step=1):
        self.sem, self.per, self.step, self.n = sem, per, step, 0
    def credit(self, eng):
        eng.sem_inc(self.sem, self.per*self.step)
    def at(self, image, n):
        return (image+1)*(self.per*self.step) + n*self.step
    def inc(self, ins):
        ins.then_inc(self.sem, self.step)
        self.n += 1
        return self.n
    def link(self, eng, image, ins):
        eng.wait_ge(self.sem, self.at(image, self.inc(ins)))
    def done(self):
        assert self.n % self.per == 0, (self.n, self.per)

def project_and_convolve(nc, d):
    with ExitStack() as ctx:
        def sb(name, shape, dt=F32): return ctx.enter_context(nc.sbuf_tensor("pc_"+name, shape, dt))
        def ps(name, n=512): return ctx.enter_context(nc.psum_tensor("pc_"+name, [128, n], F32))
        def sem(name): return ctx.enter_context(nc.semaphore("pc_"+name))
        def count(name, per, step=1): return Count(sem(name), per, step)
        w_in=sb("w_in", [CH, 2*INNER])
        w_x=sb("w_x", [128, 2, XD_ROWS])
        w_dt=sb("w_dt", [RANK, INNER])
        b_dt=sb("b_dt", [128, INNER])
        conv_w=sb("conv_w", [128, 2, TAPS])
        conv_b=sb("conv_b", [128, 2])
        tapdiag=sb("tapdiag", [128, TAPS, 128])
        d4=sb("d4", [128, INNER])
        ident=sb("ident", [128, 128])
        group=sb("group", [128, 128])
        xn=sb("xn", [CH, TOK])
        padded=sb("padded", [128, 2, PADW*PADW])
        xa=sb("xa", [128, 2, TOK])
        xr=sb("xr", [128, 2, TOK])
        xd=sb("xd", [XD_ROWS, TOK])
        bres=sb("bres", [48, 2, CHUNK])
        bpart=sb("bpart", [48, 2, 3, CHUNK], BF16)
        stats=sb("stats", [128, CHUNKS, 6])
        mv=sb("mv", [128, 2])
        gmv=sb("gmv", [128, 2])
        dev=sb("dev", [128, 1])
        var=sb("var", [128, 1])
        std=sb("std", [128, 1])
        rstd=sb("rstd", [128, 1])
        delta=sb("delta", [128, 2, PART_TILES, INNER])
        ex=sb("ex", [128, PART_TILES*INNER])
        ln=sb("ln", [128, PART_TILES*INNER])
        R=3
        LAG=2
        du=sb("du", [128, R, 1024])
        dp=sb("dp", [128, R, 3, 1024], BF16)
        gate=sb("gate", [128, 2, 2, INNER])
        skip=sb("skip", [128, 2, 2, INNER])
        mm=[ps(f"mm{i}") for i in range(2)]
        dl=[ps(f"dl{i}") for i in range(2)]
        up=[ps(f"up{i}", 1024) for i in range(2)]
        PE_CHUNKS=CHUNKS//2
        IN=(0, CHUNKS)
        GT=2*CHUNKS
        CV=GT+TILES//2
        XD=CV+PE_CHUNKS
        MM=XD+CHUNKS
        DL=2+TILES//2
        w_ld=sem("w_ld")
        setup=sem("setup")
        borders=sem("borders")
        apart=sem("apart")
        x_in=count("x_in", 1, 16)
        mm_full=count("mm_full", MM)
        mm_taken=count("mm_taken", MM)
        dl_full=count("dl_full", DL)
        dl_taken=count("dl_taken", DL)
        u_full=count("u_full", TILES)
        u_taken=count("u_taken", TILES)
        norm=count("norm", CHUNKS+5+CHUNKS)
        std_ready=count("std_ready", 1)
        conv=count("conv", 3*TAPS)
        silus=count("silus", 3)
        turned=count("turned", 2)
        b_lead=count("b_lead", CHUNKS)
        b_rest=count("b_rest", CHUNKS)
        b_mid=count("b_mid", CHUNKS)
        b_last=count("b_last", 2*CHUNKS)
        b_out=[count(f"b_out{n}", CHUNKS//2*3, 16) for n in range(2)]
        c_out=count("c_out", 2, 16)
        v_steps=count("v_steps", PARTS*5)
        e_ready=count("e_ready", PARTS)
        l_ready=count("l_ready", PARTS)
        delta_out=[count(f"delta_out{n}", PARTS, 16) for n in range(2)]
        hi=count("hi", TILES)
        res=count("res", TILES)
        mid=count("mid", TILES)
        dp_ready=count("dp_ready", TILES)
        slot_n=[len(range(n, TILES, R)) for n in range(R)]
        dp_out=[count(f"dp_out{n}", slot_n[n], 16) for n in range(R)]
        gate_out=[count(f"gate_out{n}", TILES//4, 16) for n in range(2)]
        skip_ready=count("skip_ready", TILES)
        skip_out=[count(f"skip_out{n}", TILES//4, 16) for n in range(2)]
        block=ctx.enter_context(nc.Block())

        def wait(eng, c, image, n): eng.wait_ge(c.sem, c.at(image, n))
        loads=((w_in[:, :], "w_in"), (w_x[:, :, :], "w_x"), (w_dt[:, :], "w_dt"), (b_dt[:, :], "b_dt"), (conv_w[:, :, :], "conv_w"), (conv_b[:, :], "conv_b"), (d4[:, :], "d_param"), (ident[:, :], "ident"), (group[:, :], "group"))

        def interior(h, k): return padded[:, h, :].rearrange("p (r c) -> p r c", c=PADW)[:, 1+8*k:9+8*k, 1:1+IMG]
        def shifted(h, row, rows, tap):
            return padded[:, h, :].rearrange("p (r c) -> p r c", c=PADW)[:, row+tap//3:row+tap//3+rows, tap%3:tap%3+IMG]

        @block.sync
        def _(sp):
            for dst, name in loads: sp.dma_start(dst, d[name]).then_inc(w_ld, 16)
            for c in (x_in, *b_out, c_out, *delta_out, *dp_out, *skip_out): c.credit(sp)
            bterm=d["bterm"].rearrange("(x b) n l -> b n x l", b=BATCH)
            cmat=d["cmat"].rearrange("(n h b) l -> h b n l", h=2, b=BATCH)
            delta_d=d["delta"].rearrange("(h b) x -> h b x", h=2)
            drive_d=d["drive"].rearrange("(g b) x -> g b x", b=BATCH)
            x_in.inc(sp.dma_start(xn[:, :], d["x_t"][0]))
            def store_image(b, last):
                for k in range(CHUNKS):
                    wait(sp, b_last, b, 2*(k+1))
                    row=0
                    for i, terms in enumerate((3, 2, 1)):
                        n=2*terms
                        b_out[k%2].inc(sp.dma_start(bterm[b, :, row:row+n, k*CHUNK:(k+1)*CHUNK], bpart[B_ROW:B_ROW+16, k%2, i, :].unsqueeze(1).broadcast_to((16, n, CHUNK))))
                        row+=n
                wait(sp, mm_taken, b, MM)
                for h in range(2):
                    c_out.inc(sp.dma_start(cmat[h, b], xd[C_ROW:C_ROW+16, :]))
                if not last:
                    wait(sp, mm_full, b, CV)
                    x_in.inc(sp.dma_start(xn[:, :], d["x_t"][b+1]))
                def store_tile(j):
                    wait(sp, dp_ready, b, j+1)
                    dp_out[j%R].inc(sp.dma_start(drive_d[:, b, j*TILE*512:(j+1)*TILE*512].rearrange("g (t f) -> t g f", t=TILE), dp[:, j%R, :, :].rearrange("p a (h f) -> p (a h) f", h=2)))
                    if j%2==1:
                        n=(j//2)%2
                        wait(sp, skip_ready, b, j+1)
                        skip_out[n].inc(sp.dma_start(d["skip"][b, (j-1)*TILE:(j+1)*TILE].rearrange("(j t) f -> t j f", t=TILE), skip[:, n, :, :]))
                for q in range(PARTS+1):
                    for j in range(max(0, (q-1)*PART_TILES-LAG), q*PART_TILES-LAG): store_tile(j)
                    if q<PARTS:
                        wait(sp, v_steps, b, 5*q+5)
                        for h in range(2):
                            delta_out[q%2].inc(sp.dma_start(delta_d[h, b, q*PART_TILES*TILE*DH:(q+1)*PART_TILES*TILE*DH].rearrange("(j t e) -> t j e", t=TILE, e=DH), delta[:, q%2, :, h*DH:(h+1)*DH]))
                for j in range(TILES-LAG, TILES): store_tile(j)
            with sp.Fori(0, BATCH-1) as b: store_image(b, False)
            store_image(BATCH-1, True)
            for c in (*b_out, c_out, *delta_out, *dp_out, *skip_out, *gate_out): wait(sp, c, BATCH-1, c.per)

        @block.gpsimd
        def _(pool):
            pool.memset(padded[:, :, :], 0.0).then_inc(borders, 1)
            res.credit(pool)
            with pool.Fori(0, BATCH) as b:
                for j in range(TILES):
                    wait(pool, hi, b, j+1)
                    res.inc(pool.tensor_tensor(du[:, j%R, :], du[:, j%R, :], dp[:, j%R, 0, :], ALU.subtract))

        @block.scalar
        def _(act):
            for c in (mm_taken, std_ready, silus, turned, e_ready, l_ready, hi, mid, b_lead, b_mid, *gate_out): c.credit(act)
            act.wait_ge(w_ld, 16*len(loads))
            act.wait_ge(borders, 1)
            with act.Fori(0, BATCH) as b:
                wait(act, norm, b, CHUNKS+4)
                std_ready.inc(act.activation(std[:, :], var[:, :], ACT.Sqrt))
                for h in range(2):
                    if h==0: wait(act, conv, b-1, 3*TAPS)
                    for k in range(CHUNKS):
                        wait(act, mm_full, b, IN[h]+k+1)
                        mm_taken.inc(act.activation(interior(h, k), mm[(IN[h]+k)%2][:, :].rearrange("p (r c) -> p r c", c=IMG), ACT.Copy))
                for k in range(TILES//2):
                    wait(act, mm_full, b, GT+k+1)
                    wait(act, gate_out[k%2], b, k//2)
                    mm_taken.inc(act.activation(gate[:, k%2, :, :], mm[(GT+k)%2][:, :].rearrange("p (j f) -> p j f", j=2), ACT.Silu))
                    wait(act, mm_taken, b, GT+k+1)
                    gate_out[k%2].inc(act.dma_start(d["gate"][b, 2*k*TILE:(2*k+2)*TILE].rearrange("(j t) f -> t j f", t=TILE), gate[:, k%2, :, :]))
                wait(act, u_full, b-1, TILES)
                for k in range(PE_CHUNKS):
                    wait(act, mm_full, b, CV+k+1)
                    mm_taken.inc(act.activation(xa[:, 1, k*CHUNK:(k+1)*CHUNK], mm[(CV+k)%2][:, :], ACT.Silu, bias=conv_b[:, 1:2]))
                def silu_rows(h, r, n):
                    wait(act, conv, b, n)
                    x=xa[:, h, r*(TOK//2):(r+1)*(TOK//2)]
                    silus.inc(act.activation(x, x, ACT.Silu))
                silu_rows(0, 0, 2*TAPS-1)
                silu_rows(0, 1, 2*TAPS)
                wait(act, silus, b, 2)
                turned.inc(act.activation(xr[:, 0, :], xa[:, 0, ::-1], ACT.Copy))
                silu_rows(1, 1, 3*TAPS)
                wait(act, silus, b, 3)
                wait(act, mm_taken, b, CV+PE_CHUNKS)
                turned.inc(act.activation(xr[:, 1, :], xa[:, 1, ::-1], ACT.Copy))
                def b_middle(k):
                    wait(act, b_rest, b, k+1)
                    b_mid.inc(act.activation(bpart[B_ROW:B_ROW+16, k%2, 1, :], bres[B_ROW:B_ROW+16, k%2, :], ACT.Copy))
                wait(act, b_rest, b-1, CHUNKS)
                wait(act, c_out, b-1, 2)
                wait(act, dl_full, b-1, DL)
                for k in range(CHUNKS):
                    wait(act, mm_full, b, XD+k+1)
                    mm_taken.inc(act.activation(xd[:, k*CHUNK:(k+1)*CHUNK], mm[(XD+k)%2][0:XD_ROWS, :], ACT.Copy))
                    wait(act, mm_taken, b, XD+k+1)
                    wait(act, b_out[k%2], b, 3*(k//2))
                    b_lead.inc(act.activation(bpart[B_ROW:B_ROW+16, k%2, 0, :], xd[B_ROW:B_ROW+16, k*CHUNK:(k+1)*CHUNK], ACT.Copy))
                    if k: b_middle(k-1)
                b_middle(CHUNKS-1)
                def lead(j):
                    wait(act, u_taken, b, j+1)
                    wait(act, dp_out[j%R], b, j//R)
                    hi.inc(act.activation(dp[:, j%R, 0, :], du[:, j%R, :], ACT.Copy))
                def middle(j):
                    wait(act, res, b, j+1)
                    mid.inc(act.activation(dp[:, j%R, 1, :], du[:, j%R, :], ACT.Copy))
                def parts(j):
                    lead(j)
                    if j: middle(j-1)
                for q in range(PARTS+1):
                    if q<PARTS:
                        wait(act, v_steps, b, 5*q+1)
                        e_ready.inc(act.activation(ex[:, :], ex[:, :], ACT.Exp))
                    if q:
                        for j in range((q-1)*PART_TILES, (q-1)*PART_TILES+2): parts(j)
                    if q<PARTS:
                        wait(act, v_steps, b, 5*q+3)
                        l_ready.inc(act.activation(ln[:, :], ln[:, :], ACT.Ln))
                    if q:
                        for j in range((q-1)*PART_TILES+2, q*PART_TILES): parts(j)
                middle(TILES-1)

        @block.vector
        def _(dve):
            for c in (norm, dl_taken, conv, b_rest, b_last, v_steps, u_taken, dp_ready, skip_ready): c.credit(dve)
            dve.wait_ge(w_ld, 16*len(loads))
            for t in range(TAPS):
                dve.tensor_scalar(tapdiag[:, t, :], ident[:, :], conv_w[:, 1, t:t+1], None, ALU.mult).then_inc(setup, 1)
            dve.tensor_scalar(d4[:, :], d4[:, :], float(DIRS), None, ALU.mult).then_inc(setup, 1)
            dve.wait_ge(setup, TAPS+1)
            with dve.Fori(0, BATCH) as b:
                wait(dve, x_in, b, 1)
                for k in range(CHUNKS): norm.inc(dve.bn_stats(stats[:, k, :], xn[:, k*CHUNK:(k+1)*CHUNK]))
                wait(dve, norm, b, CHUNKS)
                dve.sem_inc(apart, 1)
                norm.link(dve, b, dve.bn_aggr(mv[:, :], stats[:, :, :]))
                wait(dve, dl_full, b, 1)
                dl_taken.link(dve, b, dve.tensor_copy(gmv[:, :], dl[0][:, 0:2]))
                norm.link(dve, b, dve.tensor_tensor(dev[:, :], mv[:, 0:1], gmv[:, 0:1], ALU.subtract))
                norm.link(dve, b, dve.tensor_tensor(dev[:, :], dev[:, :], dev[:, :], ALU.mult))
                wait(dve, dl_full, b, 2)
                dl_taken.link(dve, b, dve.tensor_tensor(var[:, :], dl[1][:, 0:1], gmv[:, 1:2], ALU.add))
                norm.link(dve, b, dve.tensor_scalar(var[:, :], var[:, :], EPS, None, ALU.add))
                wait(dve, std_ready, b, 1)
                norm.link(dve, b, dve.reciprocal(rstd[:, :], std[:, :]))
                for k in range(CHUNKS):
                    s=xn[:, k*CHUNK:(k+1)*CHUNK]
                    norm.inc(dve.tensor_scalar(s, s, gmv[:, 0:1], rstd[:, 0:1], ALU.subtract, ALU.mult))
                wait(dve, u_full, b-1, TILES)
                def tap(h, r, t, before):
                    if t==0: wait(dve, mm_taken, b, IN[h]+(CHUNKS//2+1, CHUNKS)[r])
                    else: wait(dve, conv, b, before)
                    out=xa[:, h, r*(TOK//2):(r+1)*(TOK//2)].rearrange("p (r c) -> p r c", c=IMG)
                    src=shifted(h, r*IMG//2, IMG//2, t)
                    if t==0: ins=dve.tensor_scalar(out, src, conv_w[:, h, 0:1], conv_b[:, h:h+1], ALU.mult, ALU.add)
                    else: ins=dve.scalar_tensor_tensor(out=out, in0=src, scalar=conv_w[:, h, t:t+1], in1=out, op0=ALU.mult, op1=ALU.add)
                    conv.inc(ins)
                for t in range(TAPS):
                    for r in range(2): tap(0, r, t, 2*t+r-1)
                for t in range(TAPS): tap(1, 1, t, 2*TAPS+t)
                def b_finish(k):
                    rest=bres[B_ROW:B_ROW+16, k%2, :]
                    wait(dve, b_mid, b, k+1)
                    b_last.link(dve, b, dve.tensor_tensor(rest, rest, bpart[B_ROW:B_ROW+16, k%2, 1, :], ALU.subtract))
                    b_last.inc(dve.tensor_copy(bpart[B_ROW:B_ROW+16, k%2, 2, :], rest))
                for k in range(CHUNKS):
                    wait(dve, b_lead, b, k+1)
                    wait(dve, b_last, b, 2*(k-1))
                    b_rest.inc(dve.tensor_tensor(bres[B_ROW:B_ROW+16, k%2, :], xd[B_ROW:B_ROW+16, k*CHUNK:(k+1)*CHUNK], bpart[B_ROW:B_ROW+16, k%2, 0, :], ALU.subtract))
                    if k: b_finish(k-1)
                b_finish(CHUNKS-1)
                def take_tile(j):
                    n=j%R
                    u=up[j%2][:, :].rearrange("p (h k e) -> p h k e", h=2, k=DIRS)
                    wait(dve, u_full, b, j+1)
                    s=(j//2)%2
                    if j%2==0: wait(dve, skip_out[s], b, j//4)
                    skip_ready.inc(dve.tensor_tensor(skip[:, s, j%2, :].rearrange("p (h e) -> p h e", h=2), u[:, :, 0, :], d4[:, :].rearrange("p (h e) -> p h e", h=2), ALU.mult))
                    wait(dve, dp_ready, b, j-R+1)
                    dl_=delta[:, (j//PART_TILES)%2, j%PART_TILES, :].rearrange("p (h e) -> p h e", h=2)
                    u_taken.inc(dve.tensor_tensor(du[:, n, :].rearrange("p (h k e) -> p h k e", h=2, k=DIRS), u, dl_.unsqueeze(2).broadcast_to((128, 2, DIRS, DH)), ALU.mult))
                def last_part(j):
                    wait(dve, mid, b, j+1)
                    dp_ready.inc(dve.tensor_tensor(dp[:, j%R, 2, :], du[:, j%R, :], dp[:, j%R, 1, :], ALU.subtract))
                def tiles(js):
                    for j in js:
                        take_tile(j)
                        if j>=LAG: last_part(j-LAG)
                for q in range(PARTS+1):
                    if q<PARTS:
                        dq=delta[:, q%2, :, :]
                        flat=dq.rearrange("p j f -> p (j f)")
                        wait(dve, delta_out[q%2], b, q//2*2)
                        wait(dve, u_taken, b, (q-1)*PART_TILES)
                        for k in range(2):
                            i=2+2*q+k
                            wait(dve, dl_full, b, i+1)
                            dl_taken.inc(dve.tensor_tensor(dq[:, 2*k:2*k+2, :], dl[i%2][:, :].rearrange("p (j f) -> p j f", j=2), b_dt[:, :].unsqueeze(1).broadcast_to((128, 2, INNER)), ALU.add))
                        wait(dve, dl_taken, b, 2+2*q+2)
                        v_steps.inc(dve.scalar_tensor_tensor(out=ex[:, :], in0=flat, scalar=-1.0, in1=flat, op0=ALU.mult, op1=ALU.min))
                    if q: tiles(range((q-1)*PART_TILES, (q-1)*PART_TILES+2))
                    if q<PARTS:
                        wait(dve, e_ready, b, q+1)
                        v_steps.link(dve, b, dve.tensor_scalar(ln[:, :], ex[:, :], 1.0, None, ALU.add))
                        v_steps.inc(dve.scalar_tensor_tensor(out=ex[:, :], in0=ln[:, :], scalar=-1.0, in1=ex[:, :], op0=ALU.add, op1=ALU.subtract))
                    if q: tiles(range((q-1)*PART_TILES+2, q*PART_TILES))
                    if q<PARTS:
                        wait(dve, l_ready, b, q+1)
                        v_steps.link(dve, b, dve.scalar_tensor_tensor(out=ln[:, :], in0=flat, scalar=0.0, in1=ln[:, :], op0=ALU.max, op1=ALU.add))
                        v_steps.link(dve, b, dve.tensor_tensor(flat, ln[:, :], ex[:, :], ALU.subtract))
                for j in range(TILES-LAG, TILES): last_part(j)
                for c in (norm, dl_taken, conv, b_rest, b_last, v_steps, u_taken, dp_ready, skip_ready): c.done()

        @block.tensor
        def _(pe):
            for c in (mm_full, dl_full, u_full): c.credit(pe)
            pe.wait_ge(w_ld, 16*len(loads))
            pe.wait_ge(setup, TAPS+1)
            with pe.Fori(0, BATCH) as b:
                def bank(n):
                    wait(pe, mm_taken, b, n-1)
                    return mm[n%2]
                wait(pe, norm, b, CHUNKS+1)
                wait(pe, dl_taken, b-1, DL)
                dl_full.inc(pe.matmul(dl[0][:, 0:2], group[:, :], mv[:, :], start=True, stop=True))
                wait(pe, norm, b, CHUNKS+3)
                dl_full.inc(pe.matmul(dl[1][:, 0:1], group[:, :], dev[:, :], start=True, stop=True))
                for h in range(2):
                    for k in range(CHUNKS):
                        m=bank(IN[h]+k)
                        if h==0: wait(pe, norm, b, CHUNKS+5+k+1)
                        mm_full.inc(pe.matmul(m[:, :], w_in[:, h*128:(h+1)*128], xn[:, k*CHUNK:(k+1)*CHUNK], start=True, stop=True))
                for k in range(TILES//2):
                    m=bank(GT+k)
                    for j in range(2):
                        t=2*k+j
                        ins=pe.matmul(m[:, j*INNER:(j+1)*INNER], xn[:, t*TILE:(t+1)*TILE], w_in[:, INNER:2*INNER], start=True, stop=True)
                    mm_full.inc(ins)
                for k in range(PE_CHUNKS):
                    m=bank(CV+k)
                    wait(pe, mm_taken, b, IN[1]+min(k+2, CHUNKS))
                    for t in range(TAPS):
                        ins=pe.matmul(m[:, :].rearrange("p (r c) -> p r c", c=IMG), tapdiag[:, t, :], shifted(1, 8*k, 8, t), start=(t==0), stop=(t==TAPS-1))
                    mm_full.inc(ins)
                for k in range(CHUNKS):
                    m=bank(XD+k)
                    wait(pe, silus, b, (1, 3)[k//(CHUNKS//2)])
                    wait(pe, mm_taken, b, CV+PE_CHUNKS)
                    for h in range(2):
                        ins=pe.matmul(m[0:XD_ROWS, :], w_x[:, h, :], xa[:, h, k*CHUNK:(k+1)*CHUNK], start=(h==0), stop=(h==1))
                    mm_full.inc(ins)
                def turn_tile(j):
                    wait(pe, u_taken, b, j-1)
                    wait(pe, skip_ready, b, j-1)
                    if j==0: wait(pe, turned, b, 2)
                    for h in range(2):
                        for k in range(DIRS):
                            src=(xa, xr)[k//2][:, h, :]
                            out=up[j%2][:, (h*DIRS+k)*DH:(h*DIRS+k+1)*DH]
                            if k%2==0: ins=pe.transpose(out, src[:, j*TILE:(j+1)*TILE], ident[:, :])
                            else:
                                for c in range(2):
                                    ins=pe.matmul(out[c*IMG:(c+1)*IMG, :], src.rearrange("p (r c) -> p c r", c=IMG)[:, 2*j+c, :], ident[:, :], start=True, stop=True)
                    u_full.inc(ins)
                for q in range(PARTS+1):
                    if q<PARTS:
                        for k in range(2):
                            i=2+2*q+k
                            wait(pe, dl_taken, b, i-1)
                            t=q*PART_TILES+2*k
                            wait(pe, mm_taken, b, XD+t*TILE//CHUNK+1)
                            for j in range(2):
                                ins=pe.matmul(dl[i%2][:, j*INNER:(j+1)*INNER], xd[0:RANK, (t+j)*TILE:(t+j+1)*TILE], w_dt[:, :], start=True, stop=True)
                            dl_full.inc(ins)
                    if q:
                        for j in range((q-1)*PART_TILES, q*PART_TILES): turn_tile(j)
                for c in (mm_full, dl_full, u_full): c.done()

GTILES=4
GROUP_TOK=GTILES*TILE
NG=TILES//GTILES
HEADS=8
EXPERTS=8
YD_PER=2*HALVES+2*2*HALVES+1

class Phase:
    def __init__(self, nc, ctx, tag): self.nc, self.ctx, self.tag=nc, ctx, tag
    def sb(self, name, shape, dt=F32): return self.ctx.enter_context(self.nc.sbuf_tensor(self.tag+name, shape, dt))
    def ps(self, name, n=512): return self.ctx.enter_context(self.nc.psum_tensor(self.tag+name, [128, n], F32))
    def count(self, name, per, step=1): return Count(self.ctx.enter_context(self.nc.semaphore(self.tag+name)), per, step)
    def sem(self, name): return self.ctx.enter_context(self.nc.semaphore(self.tag+name))

def wait(eng, c, image, n): eng.wait_ge(c.sem, c.at(image, n))

def rsqrt(pool, c, r, b, i, n, mv, rstd, half, eps):
    wait(pool, c, b, 3*n*i+2*n)
    r.link(pool, b, pool.tensor_tensor(rstd, mv[:, :, 1:2], eps, ALU.add))
    r.inc(pool.tensor_tensor(rstd, rstd, half, ALU.pow))

def normalize(dve, apart, c, r, b, out, src, stats, mv, rstd):
    n=len(src)
    for j in range(n): c.inc(dve.bn_stats(stats[:, j, :], src[j]))
    wait(dve, c, b, c.n)
    dve.sem_inc(apart, 1)
    for j in range(n): c.inc(dve.bn_aggr(mv[:, j, :], stats[:, j, :]))
    wait(dve, c, b, c.n)
    wait(dve, r, b, 2*(c.n//(3*n)+1))
    for j in range(n):
        c.inc(dve.tensor_scalar(out[j], src[j], mv[:, j, 0:1], rstd[:, j, :], ALU.subtract, ALU.mult))

def back(b, g, n):
    return (b, g-n) if g>=n else (b-1, g-n+NG)

def merge_directions(nc, d):
    with ExitStack() as ctx:
        p=Phase(nc, ctx, "md_")
        sb, ps, count=p.sb, p.ps, p.count
        ident=sb("ident", [128, 128])
        flip=sb("flip", [128, 128])
        w_out=sb("w_out", [128, 2, 128])
        ln_w=sb("ln_w", [128, INNER])
        ln_b=sb("ln_b", [128, INNER])
        ys=sb("ys", [128, 2, DIRS, GTILES, INNER])
        skip=sb("skip", [128, 2, GTILES, INNER])
        gate=sb("gate", [128, 2, GTILES, INNER])
        xin=sb("xin", [128, 2, GTILES, CH])
        yn=sb("yn", [128, 2, GTILES, INNER])
        yt=sb("yt", [128, 2, GROUP_TOK])
        x1=sb("x1", [128, 2, GTILES, CH])
        stats=sb("stats", [128, GTILES, 6])
        mv=sb("mv", [128, GTILES, 2])
        std=sb("std", [128, GTILES, 1])
        rstd=sb("rstd", [128, GTILES, 1])
        eps=sb("eps", [128, 1])
        ybank=[ps(f"y{i}") for i in range(4)]
        tbank=ps("tb", 1024)
        obank=[ps(f"o{i}") for i in range(2)]
        w_ld=p.sem("w_ld")
        eps_ready=p.sem("eps_ready")
        apart=p.sem("apart")
        y_in=[count(f"y_in{q}", NG//2*YD_PER, 16) for q in range(2)]
        xg_in=[count(f"xg_in{q}", NG//2*2, 16) for q in range(2)]
        paired=count("paired", NG*3)
        turned_back=count("turned_back", NG*2)
        summed=count("summed", NG*2)
        normed=count("normed", NG*3*GTILES)
        std_ready=count("std_ready", NG)
        rstd_ready=count("rstd_ready", NG)
        affine=count("affine", NG*3)
        t_full=count("t_full", NG)
        t_taken=count("t_taken", NG)
        o_full=count("o_full", NG)
        o_taken=count("o_taken", NG)
        x1_out=[count(f"x1_out{q}", NG//2, 16) for q in range(2)]
        block=ctx.enter_context(nc.Block())
        loads=((ident[:, :], "ident"), (flip[:, :], "flip"), (w_out[:, :, :], "w_out"), (ln_w[:, :], "ln_w"), (ln_b[:, :], "ln_b"))

        @block.sync
        def _(sp):
            for dst, name in loads: sp.dma_start(dst, d[name]).then_inc(w_ld, 16)
            for c in (*y_in, *xg_in, *x1_out): c.credit(sp)
            y_d=d["y"].rearrange("(h b) t (k e) -> b k h t e", h=HALVES, k=DIRS)
            def store(b, g):
                wait(sp, o_taken, b, g+1)
                x1_out[g%2].inc(sp.dma_start(d["x1"][b, g*GROUP_TOK:(g+1)*GROUP_TOK].rearrange("(j t) c -> t j c", t=TILE), x1[:, g%2, :, :]))
            def finish(b, g):
                q=g%2
                tok=slice(g*GROUP_TOK, (g+1)*GROUP_TOK)
                wait(sp, affine, b, 3*(g-1))
                xg_in[q].inc(sp.dma_start(gate[:, q, :, :], d["gate"][b, tok].rearrange("(j t) f -> t j f", t=TILE)))
                wait(sp, o_full, b, g-1)
                xg_in[q].inc(sp.dma_start(xin[:, q, :, :], d["x"][b, tok].rearrange("(j t) f -> t j f", t=TILE)))
            def image(b, first):
                for g in range(NG):
                    q=g%2
                    wait(sp, turned_back, b, 2*(g-1))
                    wait(sp, summed, b, 2*(g-1))
                    for h in range(HALVES):
                        c=slice(h*DH, (h+1)*DH)
                        for k, lo in ((0, g*GTILES), (2, TILES-(g+1)*GTILES)):
                            y_in[q].inc(sp.dma_start(ys[:, q, k, :, c], y_d[b, k, h, lo*TILE:(lo+GTILES)*TILE].rearrange("(j t) e -> t j e", t=TILE)))
                        for k, lo in ((1, g*GTILES), (3, TILES-(g+1)*GTILES)):
                            for r in range(2):
                                y_in[q].inc(sp.dma_start(ys[r*IMG:(r+1)*IMG, q, k, :, c], y_d[b, k, h].rearrange("(c t r) e -> r c t e", r=2, c=IMG)[r, :, lo:lo+GTILES]))
                    y_in[q].inc(sp.dma_start(skip[:, q, :, :], d["skip"][b, g*GROUP_TOK:(g+1)*GROUP_TOK].rearrange("(j t) f -> t j f", t=TILE)))
                    if not (first and g<1): finish(*back(b, g, 1))
                    if not (first and g<3): store(*back(b, g, 3))
            image(0, True)
            with sp.Fori(1, BATCH) as b: image(b, False)
            finish(BATCH-1, NG-1)
            for g in range(NG-3, NG): store(BATCH-1, g)
            for c in x1_out: wait(sp, c, BATCH-1, c.per)

        @block.gpsimd
        def _(pool):
            affine.credit(pool)
            pool.wait_ge(w_ld, 16*len(loads))
            with pool.Fori(0, BATCH) as b:
                for g in range(NG):
                    y=yn[:, g%2, :, :]
                    wait(pool, normed, b, 3*GTILES*(g+1))
                    wait(pool, xg_in[g%2], b, (g//2+1)*2)
                    for m in (ln_w, ln_b):
                        affine.link(pool, b, pool.tensor_tensor(y, y, m[:, :].unsqueeze(1).broadcast_to((128, GTILES, INNER)), ALU.mult if m is ln_w else ALU.add))
                    affine.inc(pool.tensor_tensor(y, y, gate[:, g%2, :, :], ALU.mult))

        @block.scalar
        def _(act):
            for c in (std_ready, t_taken, o_taken): c.credit(act)
            act.wait_ge(eps_ready, 1)
            with act.Fori(0, BATCH) as b:
                def stds(g):
                    wait(act, normed, b, 3*GTILES*g+2*GTILES)
                    wait(act, rstd_ready, b, g)
                    std_ready.inc(act.activation(std[:, :, :], mv[:, :, 1:2], ACT.Sqrt, bias=eps[:, :]))
                stds(0)
                for g in range(NG):
                    if g+1<NG: stds(g+1)
                    wait(act, t_full, b, g+1)
                    wait(act, o_full, b, g)
                    t_taken.inc(act.activation(yt[:, :, :].rearrange("p h t -> p (h t)"), tbank[:, :], ACT.Copy))
                    wait(act, o_full, b, g+1)
                    wait(act, x1_out[g%2], b, g//2)
                    o_taken.inc(act.activation(x1[:, g%2, :, :].rearrange("p j c -> p (j c)"), obank[g%2][:, :], ACT.Copy))

        @block.vector
        def _(dve):
            for c in (paired, summed, normed, rstd_ready): c.credit(dve)
            dve.memset(eps[:, :], EPS).then_inc(eps_ready, 1)
            with dve.Fori(0, BATCH) as b:
                def pair(g):
                    y=[ys[:, g%2, k, :, :] for k in range(DIRS)]
                    wait(dve, y_in[g%2], b, (g//2+1)*YD_PER)
                    paired.inc(dve.tensor_tensor(y[2], y[2], y[3], ALU.add))
                    paired.link(dve, b, dve.tensor_tensor(y[0], y[0], y[1], ALU.add))
                    paired.inc(dve.tensor_tensor(y[0], y[0], skip[:, g%2, :, :], ALU.add))
                wait(dve, turned_back, b, 0)
                pair(0)
                for g in range(NG):
                    y=yn[:, g%2, :, :]
                    wait(dve, t_full, b, g-1)
                    wait(dve, paired, b, 3*(g+1))
                    for k in range(2):
                        i=2*g+k
                        wait(dve, turned_back, b, i+1)
                        summed.inc(dve.tensor_tensor(y[:, 2*k:2*k+2, :], ybank[i%4][:, :].rearrange("p (j f) -> p j f", j=2), ys[:, g%2, 0, 2*k:2*k+2, :], ALU.add))
                    wait(dve, summed, b, 2*(g+1))
                    wait(dve, normed, b, 3*GTILES*g)
                    for j in range(GTILES): normed.inc(dve.bn_stats(stats[:, j, :], y[:, j, :]))
                    wait(dve, normed, b, normed.n)
                    dve.sem_inc(apart, 1)
                    for j in range(GTILES): normed.inc(dve.bn_aggr(mv[:, j, :], stats[:, j, :]))
                    if g+1<NG: pair(g+1)
                    wait(dve, std_ready, b, g+1)
                    wait(dve, normed, b, normed.n)
                    rstd_ready.link(dve, b, dve.reciprocal(rstd[:, :, :], std[:, :, :]))
                    for j in range(GTILES):
                        normed.inc(dve.tensor_scalar(y[:, j, :], y[:, j, :], mv[:, j, 0:1], rstd[:, j, :], ALU.subtract, ALU.mult))
                for c in (paired, summed, normed, rstd_ready): c.done()

        @block.tensor
        def _(pe):
            for c in (turned_back, t_full, o_full): c.credit(pe)
            pe.wait_ge(w_ld, 16*len(loads))
            with pe.Fori(0, BATCH) as b:
                def turn_back(g):
                    wait(pe, paired, b, 3*g+1)
                    for k in range(2):
                        i=2*g+k
                        wait(pe, summed, b, i-3)
                        for j in range(2):
                            ins=pe.matmul(ybank[i%4][:, j*INNER:(j+1)*INNER], flip[:, :], ys[:, g%2, 2, GTILES-1-(2*k+j), :], start=True, stop=True)
                        turned_back.inc(ins)
                def project(g):
                    q=g%2
                    wait(pe, affine, b, 3*(g+1))
                    wait(pe, t_taken, b, g)
                    for h in range(2):
                        for j in range(GTILES):
                            ins=pe.transpose(tbank[:, h*512+j*TILE:h*512+(j+1)*TILE], yn[:, q, j, h*128:(h+1)*128], ident[:, :])
                    t_full.inc(ins)
                    wait(pe, t_taken, b, g+1)
                    wait(pe, o_taken, b, g-1)
                    wait(pe, xg_in[q], b, (g//2+1)*2)
                    for j in range(GTILES):
                        out=obank[q][:, j*CH:(j+1)*CH]
                        for h in range(2):
                            pe.matmul(out, yt[:, h, j*TILE:(j+1)*TILE], w_out[:, h, :], start=(h==0), stop=False)
                        ins=pe.matmul(out, ident[:, :], xin[:, q, j, :], start=False, stop=True)
                    o_full.inc(ins)
                turn_back(0)
                for g in range(NG):
                    if g+1<NG: turn_back(g+1)
                    project(g)
                for c in (turned_back, t_full, o_full): c.done()


def attend(nc, d):
    with ExitStack() as ctx:
        p=Phase(nc, ctx, "at_")
        sb, ps, count=p.sb, p.ps, p.count
        HW=HEADS*CH
        QCOLS=32
        QTILES=128//QCOLS
        QPITCH=QTILES*QCOLS+1
        HEADS_AT=((0, 1, 2, 3), (4, 5, 6, 7), (), ())
        ident=sb("ident", [128, 128])
        wk=sb("wk", [128, HW])
        wv=sb("wv", [128, HW])
        qs=sb("qs", [128, 2*QPITCH])
        head_rows=sb("head_rows", [128, HEADS])
        qt=sb("qt", [128, HEADS])
        upto=sb("upto", [128, 128])
        beyond=sb("beyond", [128, 128])
        x1=sb("x1", [128, 3, GTILES, CH])
        tn=sb("tn", [128, 2, GTILES, CH])
        tt=sb("tt", [128, 2, GROUP_TOK])
        kh=sb("kh", [128, HEADS, 512])
        s=sb("s", [128, 512])
        m=sb("m", [128, 512])
        e=sb("e", [128, 2, 512])
        u=sb("u", [128, 2, 512])
        last=sb("last", [128, 2])
        er=sb("er", [128, 2, GTILES*2*HEADS])
        v=sb("v", [128, 3, HW])
        ev=sb("ev", [128, 2, HW])
        wr=sb("wr", [128, 2, HW])
        x2=sb("x2", [128, 2, GTILES, CH])
        mean=sb("mean", [128, 2, CH])
        stats=sb("stats", [128, GTILES, 6])
        mv=sb("mv", [128, GTILES, 2])
        rstd=sb("rstd", [128, GTILES, 1])
        half=sb("half", [128, GTILES, 1])
        eps=sb("eps", [128, GTILES, 1])
        kb=[ps(f"kb{i}") for i in range(2)]
        vb=ps("vb", 1024)
        wb=ps("wb", 1024)
        tb=ps("tb")
        sbk=ps("sb")
        w_ld=p.sem("w_ld")
        setup=p.sem("setup")
        x_in=[count(f"x_in{i}", len(range(i, NG, 3)), 16) for i in range(3)]
        x_out=[count(f"x_out{i}", NG//2, 16) for i in range(2)]
        normed=count("normed", NG*3*GTILES)
        consts=p.sem("consts")
        apart=p.sem("apart")
        rstd_ready=count("rstd_ready", NG*2)
        t_full=count("t_full", NG*2)
        t_taken=count("t_taken", NG)
        k_full=count("k_full", NG*HEADS)
        k_taken=count("k_taken", NG*HEADS)
        scan=count("scan", 2+NG*6)
        e_ready=count("e_ready", NG)
        er_taken=count("er_taken", 2*NG)
        s_used=count("s_used", NG*HEADS)
        v_full=count("v_full", TILES)
        v_taken=count("v_taken", TILES)
        ev_ready=count("ev_ready", TILES)
        w_full=count("w_full", 2*TILES)
        weighed=count("weighed", TILES)
        reduced=count("reduced", TILES)
        added=count("added", TILES)
        block=ctx.enter_context(nc.Block())
        loads=((ident[:, :], "ident"), (wk[:, :], "w_k"), (wv[:, :], "w_v"), (qt[:, :], "q_t"), (head_rows[:, :], "head_rows"), (upto[:, :], "upto"), (beyond[:, :], "beyond"))

        @block.sync
        def _(sp):
            for dst, name in loads: sp.dma_start(dst, d[name]).then_inc(w_ld, 16)
            for c in (*x_in, *x_out): c.credit(sp)
            def store(b, g):
                wait(sp, added, b, (g+1)*GTILES)
                x_out[g%2].inc(sp.dma_start(d["x2"][b, g*GROUP_TOK:(g+1)*GROUP_TOK].rearrange("(j t) c -> t j c", t=TILE), x2[:, g%2, :, :]))
            def image(b, first):
                for g in range(NG):
                    wait(sp, added, b, (g-2 if g>2 else min(g-1, 0))*GTILES)
                    x_in[g%3].inc(sp.dma_start(x1[:, g%3, :, :], d["x1"][b, g*GROUP_TOK:(g+1)*GROUP_TOK].rearrange("(j t) c -> t j c", t=TILE)))
                    if not (first and g<2): store(*back(b, g, 2))
            image(0, True)
            with sp.Fori(1, BATCH) as b: image(b, False)
            for g in range(NG-2, NG): store(BATCH-1, g)
            for c in x_out: wait(sp, c, BATCH-1, c.per)

        @block.gpsimd
        def _(pool):
            for c in (ev_ready, rstd_ready): c.credit(pool)
            pool.memset(half[:, :, :], -0.5).then_inc(consts, 1)
            pool.memset(eps[:, :, :], EPS).then_inc(consts, 1)
            pool.wait_ge(consts, 2)
            pool.memset(qs[:, :], 0.0).then_inc(setup, 1)
            pool.wait_ge(w_ld, 16*len(loads))
            pool.wait_ge(setup, 1)
            queries=qs[:, :].rearrange("p (a x) -> p a x", x=QPITCH)[:, :, 0:QTILES*QCOLS].rearrange("p a (r y) -> p a r y", r=QTILES)[:, :, :, 0]
            pool.tensor_copy(queries, qt[:, :].rearrange("p (a r) -> p a r", r=QTILES)).then_inc(setup, 1)
            with pool.Fori(0, BATCH) as b:
                def rstds(g): rsqrt(pool, normed, rstd_ready, b, g, GTILES, mv, rstd[:, :, :], half[:, :, :], eps[:, :, :])
                rstds(0)
                rstds(1)
                for j in range(TILES):
                    g=j//GTILES
                    i=j%GTILES
                    wait(pool, v_taken, b, j+1)
                    wait(pool, er_taken, b, 2*g+1)
                    wait(pool, w_full, b, 2*(j-1))
                    ej=er[:, g%2, i*16:i*16+8].unsqueeze(2).broadcast_to((128, HEADS, CH))
                    ev_ready.inc(pool.tensor_tensor(ev[:, j%2, :].rearrange("p (h c) -> p h c", h=HEADS), v[:, j%3, :].rearrange("p (h c) -> p h c", h=HEADS), ej, ALU.mult))
                    if i==0 and g+2<NG: rstds(g+2)

        @block.scalar
        def _(act):
            for c in (t_taken, k_taken, e_ready, v_taken): c.credit(act)
            with act.Fori(0, BATCH) as b:
                def turn(g):
                    wait(act, t_full, b, 2*g+1)
                    wait(act, v_full, b, (g-1)*GTILES)
                    t_taken.inc(act.activation(tt[:, g%2, :], tb[:, :], ACT.Copy))
                def silu_k(g, h):
                    n=g*HEADS+h
                    wait(act, k_full, b, n+1)
                    wait(act, s_used, b, n-HEADS+1)
                    k_taken.inc(act.activation(kh[:, h, :], kb[n%2][:, :], ACT.Silu))
                def exps(g):
                    wait(act, scan, b, 2+6*g+3)
                    e_ready.inc(act.activation(e[:, g%2, :], e[:, g%2, :], ACT.Exp))
                def silu_v(j):
                    wait(act, v_full, b, j+1)
                    wait(act, ev_ready, b, j-2)
                    v_taken.inc(act.activation(v[:, j%3, :], vb[:, :], ACT.Silu))
                turn(0)
                for h in range(HEADS): silu_k(0, h)
                exps(0)
                silu_v(0)
                silu_v(1)
                for g in range(NG):
                    if g+1<NG: turn(g+1)
                    for i in range(GTILES):
                        j=g*GTILES+i
                        if i==2 and g+1<NG: exps(g+1)
                        if j+2<TILES: silu_v(j+2)
                        if g+1<NG:
                            for h in HEADS_AT[i]: silu_k(g+1, h)

        @block.vector
        def _(dve):
            for c in (normed, scan, er_taken, weighed, reduced, added): c.credit(dve)
            with dve.Fori(0, BATCH) as b:
                def norm(g):
                    wait(dve, x_in[g%3], b, g//3+1)
                    wait(dve, t_full, b, 2*(g-2)+1)
                    wait(dve, normed, b, normed.n)
                    normalize(dve, apart, normed, rstd_ready, b, [tn[:, g%2, j, :] for j in range(GTILES)], [x1[:, g%3, j, :] for j in range(GTILES)], stats, mv, rstd)
                def maxima(g):
                    wait(dve, s_used, b, HEADS*(g+1))
                    wait(dve, scan, b, scan.n)
                    scan.link(dve, b, dve.tensor_copy(s[:, :], sbk[:, :]))
                    scan.link(dve, b, dve.tensor_tensor_scan(m[:, :], s[:, :], s[:, :], last[:, 0:1], ALU.max, ALU.max))
                    wait(dve, t_full, b, 2*(g-1))
                    scan.link(dve, b, dve.tensor_tensor(e[:, g%2, :], s[:, :], m[:, :], ALU.subtract))
                    scan.inc(dve.tensor_copy(last[:, 0:1], m[:, 511:512]))
                def sums(g):
                    wait(dve, e_ready, b, g+1)
                    scan.link(dve, b, dve.tensor_tensor_scan(u[:, g%2, :], e[:, g%2, :], e[:, g%2, :], last[:, 1:2], ALU.add, ALU.max))
                    scan.inc(dve.tensor_copy(last[:, 1:2], u[:, g%2, 511:512]))
                def take_er(g):
                    wait(dve, t_full, b, 2*g+2)
                    wait(dve, weighed, b, (g-1)*GTILES)
                    wait(dve, ev_ready, b, (g-1)*GTILES)
                    er_taken.link(dve, b, dve.tensor_copy(er[:, g%2, :], tb[:, 0:GTILES*2*HEADS]))
                    sums_=er[:, g%2, :].rearrange("p (j x) -> p j x", j=GTILES)[:, :, HEADS:2*HEADS]
                    er_taken.inc(dve.reciprocal(sums_, sums_))
                def weigh(j):
                    g=j//GTILES
                    i=j%GTILES
                    wait(dve, w_full, b, 2*j+1)
                    wait(dve, reduced, b, j-1)
                    if i==0: wait(dve, er_taken, b, 2*(g+1))
                    rj=er[:, g%2, i*16+8:i*16+16].unsqueeze(2).broadcast_to((128, HEADS, CH))
                    weighed.inc(dve.tensor_tensor(wr[:, j%2, :].rearrange("p (h c) -> p h c", h=HEADS), wb[:, :].rearrange("p (h c) -> p h c", h=HEADS), rj, ALU.mult))
                def finish(j):
                    g=j//GTILES
                    i=j%GTILES
                    wait(dve, weighed, b, j+1)
                    wait(dve, added, b, j-1)
                    reduced.inc(dve.tensor_reduce(mean[:, j%2, :], wr[:, j%2, :].rearrange("p (h c) -> p c h", h=HEADS), AX.X, ALU.add))
                    if i==0: wait(dve, x_out[g%2], b, g//2)
                    wait(dve, reduced, b, j+1)
                    added.inc(dve.scalar_tensor_tensor(out=x2[:, g%2, i, :], in0=mean[:, j%2, :], scalar=1.0/HEADS, in1=x1[:, g%3, i, :], op0=ALU.mult, op1=ALU.add))
                wait(dve, scan, b-1, scan.per)
                scan.link(dve, b, dve.memset(last[:, 0:1], -3.0e38))
                scan.link(dve, b, dve.memset(last[:, 1:2], 0.0))
                norm(0)
                maxima(0)
                sums(0)
                norm(1)
                take_er(0)
                for g in range(NG):
                    for i in range(GTILES):
                        j=g*GTILES+i
                        weigh(j)
                        if i==2 and g+1<NG: sums(g+1)
                        if i==3 and g+1<NG: take_er(g+1)
                        finish(j)
                        if i==0 and g+2<NG: norm(g+2)
                        if i==1 and g+1<NG: maxima(g+1)
                for c in (normed, scan, er_taken, weighed, reduced, added): c.done()

        @block.tensor
        def _(pe):
            for c in (t_full, k_full, s_used, v_full, w_full): c.credit(pe)
            pe.wait_ge(w_ld, 16*len(loads))
            pe.wait_ge(setup, 2)
            with pe.Fori(0, BATCH) as b:
                def turn(g):
                    wait(pe, normed, b, (g+1)*3*GTILES)
                    wait(pe, er_taken, b, 2*(g-1)+1)
                    for j in range(GTILES): ins=pe.transpose(tb[:, j*TILE:(j+1)*TILE], tn[:, g%2, j, :], ident[:, :])
                    t_full.inc(ins)
                def turn_er(g):
                    wait(pe, t_taken, b, g+1)
                    wait(pe, scan, b, 2+6*g+5)
                    for j in range(GTILES):
                        for n, x in enumerate((e, u)):
                            ins=pe.matmul(tb[:, j*16+n*8:j*16+n*8+8], x[:, g%2, j*TILE:(j+1)*TILE], head_rows[:, :], start=True, stop=True)
                    t_full.inc(ins)
                def keys(g, h):
                    n=g*HEADS+h
                    if h==0: wait(pe, t_taken, b, g+1)
                    wait(pe, k_taken, b, n-1)
                    k_full.inc(pe.matmul(kb[n%2][:, :], wk[:, h*CH:(h+1)*CH], tt[:, g%2, :], start=True, stop=True))
                def score(g, h):
                    n=g*HEADS+h
                    wait(pe, k_taken, b, n+1)
                    if h==0: wait(pe, scan, b, 2+6*(g-1)+1)
                    row=h%QTILES*QCOLS
                    ins=pe.matmul(sbk[row:row+QCOLS, :], qs[:, h*QCOLS:(h+1)*QCOLS], kh[:, h, :], start=(h<QTILES), stop=(h>=HEADS-QTILES), skip_group_check=True)
                    s_used.inc(ins)
                def scores(g, a):
                    for h in range(a*QTILES, (a+1)*QTILES): score(g, h)
                def values(j):
                    g=j//GTILES
                    i=j%GTILES
                    wait(pe, v_taken, b, j)
                    for n in range(2):
                        ins=pe.matmul(vb[:, n*512:(n+1)*512], tt[:, g%2, i*TILE:(i+1)*TILE], wv[:, n*512:(n+1)*512], start=True, stop=True)
                    v_full.inc(ins)
                def run(j, part):
                    if part==0: wait(pe, ev_ready, b, j+1)
                    wait(pe, weighed, b, j+part)
                    for n in range(2):
                        ins=pe.matmul(wb[:, n*512:(n+1)*512], (upto, beyond)[part][:, :], ev[:, j%2, n*512:(n+1)*512], start=(j==0 and part==0), stop=True, skip_group_check=True)
                    w_full.inc(ins)
                turn(0)
                for h in range(HEADS):
                    keys(0, h)
                    if h==QTILES: scores(0, 0)
                scores(0, 1)
                turn_er(0)
                values(0)
                values(1)
                for g in range(NG):
                    if g+1<NG: turn(g+1)
                    for i in range(GTILES):
                        j=g*GTILES+i
                        run(j, 0)
                        if j+2<TILES: values(j+2)
                        if g+1<NG:
                            if i==1: scores(g+1, 0)
                            for h in HEADS_AT[i]: keys(g+1, h)
                            if i==3: turn_er(g+1)
                        run(j, 1)
                        if i==1 and g+1<NG: scores(g+1, 1)

def experts(nc, d):
    with ExitStack() as ctx:
        p=Phase(nc, ctx, "ex_")
        sb, ps, count=p.sb, p.ps, p.count
        EW=EXPERTS*CH
        ident=sb("ident", [128, 128])
        rw=sb("rw", [128, EXPERTS])
        rb=sb("rb", [128, EXPERTS])
        ew=sb("ew", [128, EW])
        eb=sb("eb", [EXPERTS, CH])
        iota=sb("iota", [128, EXPERTS])
        x2=sb("x2", [128, 3, GTILES, CH])
        tn=sb("tn", [128, 2, GTILES, CH])
        tt=sb("tt", [128, 2, GROUP_TOK])
        lg=sb("lg", [128, GTILES, EXPERTS])
        mx=sb("mx", [128, GTILES])
        top=sb("top", [128, GTILES, 8])
        idx=sb("idx", [128, GTILES, 8], mybir.dt.uint32)
        idf=sb("idf", [128, GTILES, 8])
        den=sb("den", [128, GTILES, 1])
        w2=sb("w2", [128, GTILES, 2])
        wa=sb("wa", [128, GTILES, EXPERTS])
        wb2=sb("wb2", [128, GTILES, EXPERTS])
        sel=sb("sel", [128, 2, GTILES, EXPERTS])
        st=sb("st", [EXPERTS, 512])
        pr=sb("pr", [128, 2, EW])
        mo=sb("mo", [128, 2, GTILES, CH])
        res=sb("res", [128, 2, GTILES*CH])
        stats=sb("stats", [128, GTILES, 6])
        mv=sb("mv", [128, GTILES, 2])
        rstd=sb("rstd", [128, GTILES, 1])
        half=sb("half", [128, GTILES, 1])
        eps=sb("eps", [128, GTILES, 1])
        tb=ps("tb")
        lb=ps("lb")
        wtb=ps("wtb")
        bb=ps("bb")
        eb_=[ps(f"eb{i}", 1024) for i in range(2)]
        w_ld=p.sem("w_ld")
        XS=[len(range(i, NG, 3)) for i in range(3)]
        x_in=[count(f"x_in{i}", XS[i], 16) for i in range(3)]
        x_out=[count(f"x_out{i}", NG//2, 16) for i in range(2)]
        normed=count("normed", NG*3*GTILES)
        consts=p.sem("consts")
        apart=p.sem("apart")
        rstd_ready=count("rstd_ready", NG*2)
        t_full=count("t_full", NG)
        t_taken=count("t_taken", NG)
        l_full=count("l_full", NG)
        RS=3+2*GTILES+4+2*GTILES+1
        route=count("route", NG*RS)
        e_ready=count("e_ready", NG)
        wt_full=count("wt_full", NG)
        wt_taken=count("wt_taken", NG)
        b_full=count("b_full", NG)
        e_full=count("e_full", TILES)
        weighed=count("weighed", TILES)
        reduced=count("reduced", TILES*3)
        added=count("added", NG)
        block=ctx.enter_context(nc.Block())
        loads=((ident[:, :], "ident"), (rw[:, :], "router_w"), (rb[:, :], "router_b"), (ew[:, :], "expert_w"), (eb[:, :], "expert_b"), (iota[:, :], "iota"))

        @block.sync
        def _(sp):
            for dst, name in loads: sp.dma_start(dst, d[name]).then_inc(w_ld, 16)
            for c in (*x_in, *x_out): c.credit(sp)
            def store(b, g):
                wait(sp, added, b, g+1)
                x_out[g%2].inc(sp.dma_start(d["out"][b, g*GROUP_TOK:(g+1)*GROUP_TOK].rearrange("(j t) c -> t j c", t=TILE), res[:, g%2, :].rearrange("p (j c) -> p j c", j=GTILES)))
            def image(b, first):
                for g in range(NG):
                    wait(sp, b_full, b, g-2 if g>2 else min(g-1, 0))
                    x_in[g%3].inc(sp.dma_start(x2[:, g%3, :, :], d["x2"][b, g*GROUP_TOK:(g+1)*GROUP_TOK].rearrange("(j t) c -> t j c", t=TILE)))
                    if not (first and g<2): store(*back(b, g, 2))
            image(0, True)
            with sp.Fori(1, BATCH) as b: image(b, False)
            for g in range(NG-2, NG): store(BATCH-1, g)
            for c in x_out: wait(sp, c, BATCH-1, c.per)

        @block.gpsimd
        def _(pool):
            for c in (rstd_ready, reduced): c.credit(pool)
            pool.memset(half[:, :, :], -0.5).then_inc(consts, 1)
            pool.memset(eps[:, :, :], EPS).then_inc(consts, 1)
            pool.wait_ge(consts, 2)
            with pool.Fori(0, BATCH) as b:
                def rstds(g): rsqrt(pool, normed, rstd_ready, b, g, GTILES, mv, rstd[:, :, :], half[:, :, :], eps[:, :, :])
                def fold(j):
                    g=j//GTILES
                    i=j%GTILES
                    x=pr[:, j%2, :]
                    wait(pool, weighed, b, j+1)
                    reduced.link(pool, b, pool.tensor_tensor(x[:, 0:4*CH], x[:, 0:4*CH], x[:, 4*CH:8*CH], ALU.add))
                    reduced.link(pool, b, pool.tensor_tensor(x[:, 0:2*CH], x[:, 0:2*CH], x[:, 2*CH:4*CH], ALU.add))
                    wait(pool, added, b, g-1)
                    reduced.inc(pool.tensor_tensor(mo[:, g%2, i, :], x[:, 0:CH], x[:, CH:2*CH], ALU.add))
                rstds(0)
                rstds(1)
                for g in range(NG):
                    for i in range(GTILES):
                        fold(g*GTILES+i)
                        if i==0 and g+2<NG: rstds(g+2)

        @block.scalar
        def _(act):
            for c in (t_taken, e_ready, wt_taken): c.credit(act)
            with act.Fori(0, BATCH) as b:
                def turn(g):
                    wait(act, t_full, b, g+1)
                    wait(act, e_full, b, (g-1)*GTILES)
                    t_taken.inc(act.activation(tt[:, g%2, :], tb[:, :], ACT.Copy))
                def exps(g):
                    wait(act, route, b, RS*g+3)
                    e_ready.inc(act.activation(lg[:, :, :], lg[:, :, :], ACT.Exp))
                turn(0)
                exps(0)
                for g in range(NG):
                    if g+1<NG: turn(g+1)
                    wait(act, wt_full, b, g+1)
                    wait(act, b_full, b, g)
                    wt_taken.inc(act.activation(st[:, :], wtb[0:EXPERTS, :], ACT.Copy))
                    if g+1<NG: exps(g+1)

        @block.vector
        def _(dve):
            for c in (normed, route, weighed, added): c.credit(dve)
            dve.wait_ge(w_ld, 16*len(loads))
            with dve.Fori(0, BATCH) as b:
                def norm(g):
                    wait(dve, x_in[g%3], b, g//3+1)
                    wait(dve, t_full, b, g-1)
                    wait(dve, normed, b, normed.n)
                    normalize(dve, apart, normed, rstd_ready, b, [tn[:, g%2, j, :] for j in range(GTILES)], [x2[:, g%3, j, :] for j in range(GTILES)], stats, mv, rstd)
                def link(ins): route.link(dve, b, ins)
                def weights(g):
                    wait(dve, l_full, b, g+1)
                    link(dve.tensor_tensor(lg[:, :, :], lb[:, 0:GTILES*EXPERTS].rearrange("p (j e) -> p j e", j=GTILES), rb[:, :].unsqueeze(1).broadcast_to((128, GTILES, EXPERTS)), ALU.add))
                    link(dve.tensor_reduce(mx[:, :], lg[:, :, :], AX.X, ALU.max))
                    link(dve.tensor_tensor(lg[:, :, :], lg[:, :, :], mx[:, :].unsqueeze(2).broadcast_to((128, GTILES, EXPERTS)), ALU.subtract))
                    wait(dve, e_ready, b, g+1)
                    dve.sem_inc(apart, 1)
                    for j in range(GTILES): route.inc(dve.max(top[:, j, :], lg[:, j, :]))
                    wait(dve, route, b, route.n)
                    dve.sem_inc(apart, 1)
                    for j in range(GTILES): route.inc(dve.max_index(idx[:, j, :], top[:, j, :], lg[:, j, :]))
                    link(dve.tensor_tensor(den[:, :, :], top[:, :, 0:1], top[:, :, 1:2], ALU.add))
                    link(dve.reciprocal(den[:, :, :], den[:, :, :]))
                    link(dve.tensor_tensor(w2[:, :, :], top[:, :, 0:2], den[:, :, :].broadcast_to((128, GTILES, 2)), ALU.mult))
                    link(dve.tensor_copy(idf[:, :, :], idx[:, :, :]))
                    for j in range(GTILES):
                        for n, w in enumerate((wa, wb2)):
                            route.inc(dve.tensor_scalar(w[:, j, :], iota[:, :], idf[:, j, n:n+1], w2[:, j, n:n+1], ALU.is_equal, ALU.mult))
                    wait(dve, route, b, route.n)
                    wait(dve, wt_full, b, g-1)
                    wait(dve, weighed, b, (g-1)*GTILES)
                    link(dve.tensor_tensor(sel[:, g%2, :, :], wa[:, :, :], wb2[:, :, :], ALU.add))
                def mix(j):
                    g=j//GTILES
                    i=j%GTILES
                    wait(dve, e_full, b, j+1)
                    wait(dve, reduced, b, 3*(j-1))
                    weighed.inc(dve.tensor_tensor(pr[:, j%2, :].rearrange("p (e c) -> p e c", e=EXPERTS), eb_[j%2][:, :].rearrange("p (e c) -> p e c", e=EXPERTS), sel[:, g%2, i, :].unsqueeze(2).broadcast_to((128, EXPERTS, CH)), ALU.mult))
                norm(0)
                norm(1)
                weights(0)
                for g in range(NG):
                    for i in range(GTILES):
                        mix(g*GTILES+i)
                        if i==1 and g+2<NG: norm(g+2)
                    if g+1<NG: weights(g+1)
                    wait(dve, b_full, b, g+1)
                    wait(dve, reduced, b, 3*(g+1)*GTILES)
                    wait(dve, x_out[g%2], b, g//2)
                    added.inc(dve.tensor_tensor(res[:, g%2, :], mo[:, g%2, :, :].rearrange("p j c -> p (j c)"), bb[:, :], ALU.add))
                for c in (normed, route, weighed, added): c.done()

        @block.tensor
        def _(pe):
            for c in (t_full, l_full, e_full, wt_full, b_full): c.credit(pe)
            pe.wait_ge(w_ld, 16*len(loads))
            with pe.Fori(0, BATCH) as b:
                def turn(g):
                    wait(pe, normed, b, (g+1)*3*GTILES)
                    wait(pe, t_taken, b, g)
                    for j in range(GTILES): ins=pe.transpose(tb[:, j*TILE:(j+1)*TILE], tn[:, g%2, j, :], ident[:, :])
                    t_full.inc(ins)
                def logits(g):
                    wait(pe, t_taken, b, g+1)
                    wait(pe, route, b, RS*(g-1)+1)
                    for j in range(GTILES): ins=pe.matmul(lb[:, j*EXPERTS:(j+1)*EXPERTS], tt[:, g%2, j*TILE:(j+1)*TILE], rw[:, :], start=True, stop=True)
                    l_full.inc(ins)
                def project(j):
                    g=j//GTILES
                    i=j%GTILES
                    wait(pe, weighed, b, j-1)
                    for n in range(2):
                        ins=pe.matmul(eb_[j%2][:, n*512:(n+1)*512], tt[:, g%2, i*TILE:(i+1)*TILE], ew[:, n*512:(n+1)*512], start=True, stop=True)
                    e_full.inc(ins)
                def biases(g):
                    wait(pe, route, b, RS*(g+1))
                    wait(pe, wt_taken, b, g)
                    for j in range(GTILES): ins=pe.matmul(wtb[0:EXPERTS, j*TILE:(j+1)*TILE], sel[:, g%2, j, :], ident[:, :], start=True, stop=True)
                    wt_full.inc(ins)
                    wait(pe, wt_taken, b, g+1)
                    wait(pe, added, b, g)
                    for j in range(GTILES):
                        pe.matmul(bb[:, j*CH:(j+1)*CH], st[:, j*TILE:(j+1)*TILE], eb[:, :], start=True, stop=False)
                        ins=pe.matmul(bb[:, j*CH:(j+1)*CH], ident[:, :], x2[:, g%3, j, :], start=False, stop=True)
                    b_full.inc(ins)
                turn(0)
                logits(0)
                for g in range(NG):
                    for i in range(GTILES):
                        project(g*GTILES+i)
                        if i==1 and g+1<NG: turn(g+1)
                    biases(g)
                    if g+1<NG: logits(g+1)
                for c in (t_full, l_full, e_full, wt_full, b_full): c.done()



def build(nc, d):
    L = TOK
    def scratch(name, shape, dt=F32):
        d[name] = nc.dram_tensor("scratch_" + name, shape, dt, kind="Internal").ap()
    scratch("delta", [GROUPS, L * DH + 1024])
    scratch("drive", [3 * GROUPS, L * DIRS * DH + 2048], BF16)
    scratch("bterm", [TROWS, N_STATE, L], BF16)
    scratch("cmat", [128, L])
    scratch("gate", [BATCH, L, INNER])
    scratch("skip", [BATCH, L, INNER])
    scratch("y", [GROUPS, L, DIRS * DH])
    scratch("x1", [BATCH, L, CH])
    scratch("x2", [BATCH, L, CH])
    project_and_convolve(nc, d)
    selective_scan(nc, L, d["delta"].unsqueeze(0).broadcast_to((N_STATE, GROUPS, L * DH + 1024)), d["drive"], d["bterm"],
                   d["cmat"], d["a_log"], d["group_mask"], lambda t: d["y"].rearrange("g l f -> l g f")[bass.ds(t, BLK)])
    merge_directions(nc, d)
    attend(nc, d)
    experts(nc, d)


def laid_out(a):
    import numpy as np
    f = {k: np.asarray(v) for k, v in a.items()}
    x = f["x"].reshape(BATCH, TOK, CH)
    rows = lambda v: np.broadcast_to(v, (128, v.shape[-1]))
    halves = lambda v: v.reshape(2, 128, *v.shape[1:]).swapaxes(0, 1)
    w_x = np.zeros((INNER, XD_ROWS), np.float32)
    xp = f["L0_conv_w_xproj"]
    for row, lo, n in ((DT_ROW, 0, RANK), (B_ROW, RANK, N_STATE), (C_ROW, RANK + N_STATE, N_STATE)):
        w_x[:, row:row + n] = xp[:, lo:lo + n]
    a_log = np.broadcast_to(f["L0_conv_A_log"].reshape(HALVES, DH, N_STATE).transpose(2, 0, 1)[:, :, None, :],
                            (N_STATE, HALVES, BATCH, DH)).reshape(128, DH)
    w_kv = f["L1_attn_W_kv"].reshape(HEADS, CH, 2, CH)
    out = dict(
        x=x, x_t=x.transpose(0, 2, 1), w_in=f["L0_conv_w_in"], w_x=halves(w_x), w_dt=f["L0_conv_w_dt"],
        b_dt=rows(f["L0_conv_b_dt"]), conv_w=f["L0_conv_conv_w"].reshape(TAPS, 2, 128).transpose(2, 1, 0),
        conv_b=f["L0_conv_conv_b"].reshape(2, 128).T, d_param=rows(f["L0_conv_D_param"]), a_log=a_log,
        w_out=halves(f["L0_conv_w_out"]), ln_w=rows(f["L0_conv_ln_w"]), ln_b=rows(f["L0_conv_ln_b"]),
        w_k=w_kv[:, :, 0].transpose(2, 0, 1).reshape(CH, HEADS * CH),
        w_v=w_kv[:, :, 1].transpose(2, 0, 1).reshape(CH, HEADS * CH), q_t=f["L1_attn_q_proj"].T,
        router_w=f["L1_ffn_router_w"], router_b=rows(f["L1_ffn_router_b"]),
        expert_w=f["L1_ffn_expert_w"].transpose(1, 0, 2).reshape(CH, EXPERTS * CH), expert_b=f["L1_ffn_expert_b"],
        ident=np.eye(128, dtype=np.float32), flip=np.eye(128, dtype=np.float32)[::-1],
        group=np.kron(np.eye(32, dtype=np.float32), np.full((4, 4), 0.25, np.float32)),
        head_rows=np.eye(128, dtype=np.float32)[[h % 4 * 32 + h // 4 for h in range(HEADS)]].T,
        group_mask=np.tile(np.eye(GROUPS, dtype=np.float32), (128 // GROUPS, 1)),
        upto=np.triu(np.ones((128, 128), np.float32)), beyond=np.tril(np.ones((128, 128), np.float32), -1),
        iota=np.broadcast_to(np.arange(EXPERTS, dtype=np.float32), (128, EXPERTS)))
    return {k: np.ascontiguousarray(v) for k, v in out.items()}


def kernel(**inputs):
    import concourse.bacc as bacc
    from concourse.bass_utils import run_bass_kernel_spmd

    nc = bacc.Bacc("TRN2", target_bir_lowering=False, num_devices=1)
    arrays, d = {}, {}
    for name, a in laid_out(inputs).items():
        arrays["in_" + name] = a
        d[name] = nc.dram_tensor("in_" + name, a.shape, mybir.dt.from_np(a.dtype), kind="ExternalInput").ap()
    d["out"] = nc.dram_tensor("out_x", [BATCH, TOK, CH], F32, kind="ExternalOutput").ap()
    build(nc, d)
    r = run_bass_kernel_spmd(nc, [arrays], core_ids=[0])
    return r.results[0]["out_x"].reshape(BATCH, IMG, IMG, CH)
```
